# Optimizing a Trainium2 kernel written in Bass

```python
import numpy as np
import jax
import jax.numpy as jnp

def _softmax(x, axis=-1):
    return jax.nn.softmax(x, axis=axis)

def _gelu(x):
    return jax.nn.gelu(x, approximate=True)

def _silu(x):
    return jax.nn.silu(x)

def _sigmoid(x):
    return jax.nn.sigmoid(x)

def _layernorm(x, axis=-1, eps=1e-05):
    m = jnp.mean(x, axis=axis, keepdims=True)
    v = jnp.var(x, axis=axis, keepdims=True)
    return (x - m) / jnp.sqrt(v + eps)

def _scatter_add(tgt, idx, src, axis=0):
    return tgt.at[idx].add(src)

def _segment_sum(src, seg, n):
    return jax.ops.segment_sum(src, seg, n)
kernel_name = 'mk_decoder_preln_d4_seqx_r8_2e40ed'

def setup_inputs(seed: int=0):
    np.random.seed(seed)
    _w = jnp.asarray

    def _rec_inputs():
        import jax
        import jax.numpy as jnp
        _rk = jax.random.key(seed)
        x = -1.394e-06 + 0.9999 * jax.random.normal(jax.random.fold_in(_rk, 1), (16, 64, 128), jnp.float32)
        _lenS = 64 - jax.random.randint(jax.random.fold_in(_rk, 7), (16,), 0, max(1, 64 // 4) + 1, jnp.int32)
        _lenS2 = 64 - jax.random.randint(jax.random.fold_in(_rk, 8), (16,), 0, max(1, 64 // 4) + 1, jnp.int32)
        _ctx_1024P = jax.random.normal(jax.random.fold_in(_rk, 11), (16, 16, 128), jnp.float32)
        _ctx_1024c = jax.random.dirichlet(jax.random.fold_in(_rk, 511), 0.3 * jnp.ones((16,), jnp.float32), (16, 64))
        _ctx_1024t = jnp.einsum('bsk,bkd->bsd', _ctx_1024c, _ctx_1024P)
        _ctx_1024t = _ctx_1024t * jax.lax.rsqrt(jnp.mean(jnp.square(_ctx_1024t)) + 1e-12) * 0.953939
        ctx_1024 = -0.000292821 + 1.00034 * (_ctx_1024t + 0.3 * jax.random.normal(jax.random.fold_in(_rk, 611), (16, 64, 128), jnp.float32))
        _validS = jnp.arange(64)[None, :] < _lenS[:, None]
        _validS2 = jnp.arange(64)[None, :] < _lenS2[:, None]
        _causal = jnp.tril(jnp.ones((64, 64), dtype=bool))
        mask_BxS2_bf1 = jnp.ones((16, 64), dtype=bool)
        return (x, ctx_1024, mask_BxS2_bf1)
    x, ctx_1024, mask_BxS2_bf1 = _rec_inputs()

    def _L0_attn_setup():
        import math
        import jax, jax.numpy as jnp
        import numpy as np
        D_MODEL = 128
        N_HEADS = 16
        D_K = D_MODEL // N_HEADS
        D_C = 32
        B, S = (2, 256)
        key = jax.random.key(seed)
        ks = jax.random.split(key, 7)
        sd = lambda fan_in: 1.0 / math.sqrt(fan_in)
        return {'x': jax.random.normal(ks[0], (B, S, D_MODEL), dtype=jnp.float32), 'W_dq': jax.random.uniform(ks[1], (D_MODEL, D_C), minval=-sd(D_MODEL), maxval=sd(D_MODEL), dtype=jnp.float32), 'W_uq': jax.random.uniform(ks[2], (D_C, N_HEADS * D_K), minval=-sd(D_C), maxval=sd(D_C), dtype=jnp.float32), 'W_dkv': jax.random.uniform(ks[3], (D_MODEL, D_C), minval=-sd(D_MODEL), maxval=sd(D_MODEL), dtype=jnp.float32), 'W_uk': jax.random.uniform(ks[4], (D_C, N_HEADS * D_K), minval=-sd(D_C), maxval=sd(D_C), dtype=jnp.float32), 'W_uv': jax.random.uniform(ks[5], (D_C, N_HEADS * D_K), minval=-sd(D_C), maxval=sd(D_C), dtype=jnp.float32), 'W_o': jax.random.uniform(ks[6], (N_HEADS * D_K, D_MODEL), minval=-sd(N_HEADS * D_K), maxval=sd(N_HEADS * D_K), dtype=jnp.float32)}
    _L0_attn_all = _L0_attn_setup()
    _L0_attn_in = {k: v for k, v in _L0_attn_all.items() if k in ('W_dq', 'W_uq', 'W_dkv', 'W_uk', 'W_uv', 'W_o')}
    del _L0_attn_all

    def _L0_xattn_setup():
        import jax, jax.numpy as jnp
        import numpy as np
        import math
        B, S, E = (2, 256, 128)
        H = 16
        DK = E // H
        MAX_DIST = 256

        def _split_heads(x):
            b, s, _ = x.shape
            return x.reshape(b, s, H, DK).transpose(0, 2, 1, 3)
        key = jax.random.key(seed)
        ks = jax.random.split(key, 9)
        sc = 1.0 / math.sqrt(E)
        return {'key': jax.random.normal(ks[0], (B, S, E), jnp.float32), 'query': jax.random.normal(ks[1], (B, S, E), jnp.float32), 'value': jax.random.normal(ks[2], (B, S, E), jnp.float32), 'wq': jax.random.normal(ks[3], (E, E), jnp.float32) * sc, 'wk': jax.random.normal(ks[4], (E, E), jnp.float32) * sc, 'wv': jax.random.normal(ks[5], (E, E), jnp.float32) * sc, 'fc_w': jax.random.normal(ks[6], (E, E), jnp.float32) * sc, 'fc_b': jax.random.normal(ks[7], (E,), jnp.float32) * sc, 'rel_table': jax.random.normal(ks[8], (2 * MAX_DIST - 1, H), jnp.float32) * 0.02}
    _L0_xattn_all = _L0_xattn_setup()
    _L0_xattn_in = {k: v for k, v in _L0_xattn_all.items() if k in ('wq', 'wk', 'wv', 'fc_w', 'fc_b', 'rel_table')}
    del _L0_xattn_all

    def _L0_ffn_setup():
        import jax, jax.numpy as jnp
        import numpy as np
        ALPHA = 1.0
        key = jax.random.key(seed)
        ks = jax.random.split(key, 7)
        B, S, IN, OUT = (8, 1024, 128, 128)
        RANK, DDIM, UDIM = (4, 100, 50)
        return {'hidden_states': jax.random.normal(ks[0], (B, S, IN), dtype=jnp.float32), 'W': jax.random.normal(ks[1], (OUT, IN), dtype=jnp.float32) * 0.02, 'b': jax.random.normal(ks[2], (OUT,), dtype=jnp.float32) * 0.02, 'lora_down': jax.random.normal(ks[3], (RANK, DDIM), dtype=jnp.float32) * 0.1, 'lora_up': jax.random.normal(ks[4], (UDIM, RANK), dtype=jnp.float32) * 0.1, 'down_aux': jax.random.normal(ks[5], (DDIM, IN), dtype=jnp.float32) * 0.03, 'up_aux': jax.random.normal(ks[6], (OUT, UDIM), dtype=jnp.float32) * 0.03}
    _L0_ffn_all = _L0_ffn_setup()
    _L0_ffn_in = {k: v for k, v in _L0_ffn_all.items() if k in ('W', 'b', 'lora_down', 'lora_up', 'down_aux', 'up_aux')}
    del _L0_ffn_all

    def _L1_attn_setup():
        import jax, jax.numpy as jnp
        import numpy as np
        L, B, D, N = (512, 4, 128, 16)
        key = jax.random.key(seed)
        ks = jax.random.split(key, 6)
        x = jax.random.normal(ks[0], (L, B, D), dtype=jnp.float32)
        delta = 0.2 * jax.random.normal(ks[1], (D, N, 1), dtype=jnp.float32)
        alpha = 0.2 * jax.random.normal(ks[2], (D, N, 1), dtype=jnp.float32)
        beta = 0.02 * jax.random.normal(ks[3], (D, N, 1), dtype=jnp.float32) + 1.0
        gamma = jax.random.normal(ks[4], (D, N), dtype=jnp.float32)
        omega = jax.random.normal(ks[5], (D,), dtype=jnp.float32)
        return {'x': x, 'delta': delta, 'alpha': alpha, 'beta': beta, 'gamma': gamma, 'omega': omega}
    _L1_attn_all = _L1_attn_setup()
    _L1_attn_in = {k: v for k, v in _L1_attn_all.items() if k in ('delta', 'alpha', 'beta', 'gamma', 'omega')}
    del _L1_attn_all

    def _L1_xattn_setup():
        import jax, jax.numpy as jnp
        import numpy as np
        D = 128
        B, S = (4, 256)
        key = jax.random.key(seed)
        ks = jax.random.split(key, 9)
        scale = 1.0 / np.sqrt(D)
        return {'queries': jax.random.normal(ks[0], (B, S, D), dtype=jnp.float32), 'keys': jax.random.normal(ks[1], (B, S, D), dtype=jnp.float32), 'values': jax.random.normal(ks[2], (B, S, D), dtype=jnp.float32), 'Wq': jax.random.uniform(ks[3], (D, D), jnp.float32, -scale, scale), 'bq': jax.random.uniform(ks[4], (D,), jnp.float32, -scale, scale), 'Wk': jax.random.uniform(ks[5], (D, D), jnp.float32, -scale, scale), 'bk': jax.random.uniform(ks[6], (D,), jnp.float32, -scale, scale), 'Wv': jax.random.uniform(ks[7], (D, D), jnp.float32, -scale, scale), 'bv': jax.random.uniform(ks[8], (D,), jnp.float32, -scale, scale)}
    _L1_xattn_all = _L1_xattn_setup()
    _L1_xattn_in = {k: v for k, v in _L1_xattn_all.items() if k in ('Wq', 'bq', 'Wk', 'bk', 'Wv', 'bv')}
    del _L1_xattn_all

    def _L1_ffn_setup():
        import jax, jax.numpy as jnp
        import numpy as np
        B, S, D, F, E, K = (2, 256, 128, 256, 8, 2)
        key = jax.random.key(seed)
        ks = jax.random.split(key, 5)
        scale = 0.02
        return {'x': jax.random.normal(ks[0], (B, S, D), dtype=jnp.float32), 'Wg': jax.random.normal(ks[1], (E, D), dtype=jnp.float32) * scale, 'W1': jax.random.normal(ks[2], (E, F, D), dtype=jnp.float32) * scale, 'W2': jax.random.normal(ks[3], (E, F, D), dtype=jnp.float32) * scale, 'W3': jax.random.normal(ks[4], (E, D, F), dtype=jnp.float32) * scale}
    _L1_ffn_all = _L1_ffn_setup()
    _L1_ffn_in = {k: v for k, v in _L1_ffn_all.items() if k in ('Wg', 'W1', 'W2', 'W3')}
    del _L1_ffn_all

    def _L2_attn_setup():
        import jax, jax.numpy as jnp
        import numpy as np
        HIDDEN_DIM = 128
        NUM_HEADS = 16
        LN_EPS = 1e-06

        def _layernorm(x, scale, bias):
            mu = jnp.mean(x, axis=-1, keepdims=True)
            var = jnp.mean(jnp.square(x - mu), axis=-1, keepdims=True)
            return (x - mu) * jax.lax.rsqrt(var + LN_EPS) * scale + bias
        key = jax.random.key(seed)
        ks = jax.random.split(key, 4)
        B, S, D = (2, 256, HIDDEN_DIM)
        x = jax.random.normal(ks[0], (B, S, D), dtype=jnp.float32)
        scale = 1.0 / np.sqrt(D)
        wq = jax.random.normal(ks[1], (D, HIDDEN_DIM), dtype=jnp.float32) * scale
        wk = jax.random.normal(ks[2], (D, HIDDEN_DIM), dtype=jnp.float32) * scale
        wv = jax.random.normal(ks[3], (D, HIDDEN_DIM), dtype=jnp.float32) * scale
        ln_scale = jnp.ones((D,), dtype=jnp.float32)
        ln_bias = jnp.zeros((D,), dtype=jnp.float32)
        return {'x': x, 'ln_scale': ln_scale, 'ln_bias': ln_bias, 'wq': wq, 'wk': wk, 'wv': wv}
    _L2_attn_all = _L2_attn_setup()
    _L2_attn_in = {k: v for k, v in _L2_attn_all.items() if k in ('ln_scale', 'ln_bias', 'wq', 'wk', 'wv')}
    del _L2_attn_all

    def _L2_xattn_setup():
        import jax, jax.numpy as jnp
        import numpy as np
        B, SQ, SK, D = (4, 256, 256, 128)
        key = jax.random.key(seed)
        ks = jax.random.split(key, 8)
        s = 1.0 / np.sqrt(D)
        return {'input_seq': jax.random.normal(ks[0], (B, SQ, D), jnp.float32), 'condition_seq': jax.random.normal(ks[1], (B, SK, D), jnp.float32), 'Wq': jax.random.normal(ks[2], (D, D), jnp.float32) * s, 'bq': jnp.zeros((D,), jnp.float32), 'Wk': jax.random.normal(ks[3], (D, D), jnp.float32) * s, 'bk': jnp.zeros((D,), jnp.float32), 'Wv': jax.random.normal(ks[4], (D, D), jnp.float32) * s, 'bv': jnp.zeros((D,), jnp.float32)}
    _L2_xattn_all = _L2_xattn_setup()
    _L2_xattn_in = {k: v for k, v in _L2_xattn_all.items() if k in ('Wq', 'bq', 'Wk', 'bk', 'Wv', 'bv')}
    del _L2_xattn_all

    def _L2_ffn_setup():
        import math
        import jax, jax.numpy as jnp
        import numpy as np
        D_MODEL = 128
        D_FF = 512
        E = 8
        K = 2
        CF = 1.25
        CLAMP = 10000.0
        key = jax.random.key(seed)
        k0, k1, k2, k3 = jax.random.split(key, 4)
        B, S = (4, 256)
        x = jax.random.normal(k0, (B, S, D_MODEL), dtype=jnp.float32)
        ln_gamma = jnp.ones((D_MODEL,), jnp.float32)
        ln_beta = jnp.zeros((D_MODEL,), jnp.float32)
        rb = 0.02 * math.sqrt(3.0)
        Wr = jax.random.uniform(k1, (E, D_MODEL), jnp.float32, -rb, rb)
        b12 = math.sqrt(6.0 / (D_MODEL + 2 * D_FF))
        W12 = jax.random.uniform(k2, (E, 2 * D_FF, D_MODEL), jnp.float32, -b12, b12)
        b3 = math.sqrt(6.0 / (D_FF + D_MODEL))
        W3 = jax.random.uniform(k3, (E, D_MODEL, D_FF), jnp.float32, -b3, b3)
        return {'x': x, 'ln_gamma': ln_gamma, 'ln_beta': ln_beta, 'Wr': Wr, 'W12': W12, 'W3': W3}
    _L2_ffn_all = _L2_ffn_setup()
    _L2_ffn_in = {k: v for k, v in _L2_ffn_all.items() if k in ('ln_gamma', 'ln_beta', 'Wr', 'W12', 'W3')}
    del _L2_ffn_all

    def _L3_attn_setup():
        import jax, jax.numpy as jnp
        import numpy as np
        D_MODEL = 128
        N_HEADS = 16
        D_HEAD = 64
        ROTARY_DIM = 64
        ROTARY_BASE = 10000.0
        ATTN_SCALE = 8.0

        def _rope_sin_cos(n_pos, rotary_dim):
            pos = jnp.arange(n_pos, dtype=jnp.float32)
            dim = jnp.arange(rotary_dim // 2, dtype=jnp.float32)
            freq = ROTARY_BASE ** (dim / (rotary_dim / 2))
            freq = jnp.concatenate([freq, freq])
            angles = pos[:, None] / freq[None, :]
            return (jnp.sin(angles), jnp.cos(angles))

        def _apply_rotary(x, sin, cos):
            n = x.shape[-1] // 2
            x_flip = jnp.concatenate([-x[..., n:], x[..., :n]], axis=-1)
            return x * cos[None, :, None, :] + x_flip * sin[None, :, None, :]
        key = jax.random.key(seed)
        ks = jax.random.split(key, 9)
        std = 0.02
        x = jax.random.normal(ks[0], (2, 256, D_MODEL), dtype=jnp.float32)
        W_Q = jax.random.normal(ks[1], (N_HEADS, D_MODEL, D_HEAD), dtype=jnp.float32) * std
        W_K = jax.random.normal(ks[2], (N_HEADS, D_MODEL, D_HEAD), dtype=jnp.float32) * std
        W_V = jax.random.normal(ks[3], (N_HEADS, D_MODEL, D_HEAD), dtype=jnp.float32) * std
        W_O = jax.random.normal(ks[4], (N_HEADS, D_HEAD, D_MODEL), dtype=jnp.float32) * std
        b_Q = jnp.zeros((N_HEADS, D_HEAD), dtype=jnp.float32)
        b_K = jnp.zeros((N_HEADS, D_HEAD), dtype=jnp.float32)
        b_V = jnp.zeros((N_HEADS, D_HEAD), dtype=jnp.float32)
        b_O = jnp.zeros((D_MODEL,), dtype=jnp.float32)
        return {'x': x, 'W_Q': W_Q, 'b_Q': b_Q, 'W_K': W_K, 'b_K': b_K, 'W_V': W_V, 'b_V': b_V, 'W_O': W_O, 'b_O': b_O}
    _L3_attn_all = _L3_attn_setup()
    _L3_attn_in = {k: v for k, v in _L3_attn_all.items() if k in ('W_Q', 'b_Q', 'W_K', 'b_K', 'W_V', 'b_V', 'W_O', 'b_O')}
    del _L3_attn_all

    def _L3_xattn_setup():
        import jax, jax.numpy as jnp
        import numpy as np
        NEG_INF = -10000000000.0
        key = jax.random.key(seed)
        ks = jax.random.split(key, 8)
        B, S, D = (4, 256, 128)
        scale = 1.0 / np.sqrt(D)
        return {'query': jax.random.normal(ks[0], (B, S, D), jnp.float32), 'key': jax.random.normal(ks[1], (B, S, D), jnp.float32), 'value': jax.random.normal(ks[2], (B, S, D), jnp.float32), 'key_padding_mask': jnp.ones((B, S), dtype=bool), 'Wq': jax.random.normal(ks[3], (D, D), jnp.float32) * scale, 'Wk': jax.random.normal(ks[4], (D, D), jnp.float32) * scale, 'Wv': jax.random.normal(ks[5], (D, D), jnp.float32) * scale, 'Wo': jax.random.normal(ks[6], (D, D), jnp.float32) * scale, 'bo': jnp.zeros((D,), jnp.float32)}
    _L3_xattn_all = _L3_xattn_setup()
    _L3_xattn_in = {k: v for k, v in _L3_xattn_all.items() if k in ('Wq', 'Wk', 'Wv', 'Wo', 'bo')}
    del _L3_xattn_all

    def _L3_ffn_setup():
        import jax, jax.numpy as jnp
        import numpy as np
        HIDDEN = 128
        INNER = 512

        def _weight_quant(w):
            scale = 1.0 / jnp.clip(jnp.mean(jnp.abs(w)), 1e-05)
            wq = jnp.clip(jnp.round(w * scale), -1.0, 1.0) / scale
            return w + jax.lax.stop_gradient(wq - w)

        def _act_quant(x):
            scale = 127.0 / jnp.clip(jnp.max(jnp.abs(x), axis=-1, keepdims=True), 1e-05)
            xq = jnp.clip(jnp.round(x * scale), -128.0, 127.0) / scale
            return x + jax.lax.stop_gradient(xq - x)

        def _bitlinear(x, w):
            return jnp.einsum('bsi,oi->bso', _act_quant(x), _weight_quant(w))
        key = jax.random.key(seed)
        k0, k1, k2, k3 = jax.random.split(key, 4)
        x = jax.random.normal(k0, (4, 256, HIDDEN), dtype=jnp.float32)
        w_gate = jax.random.normal(k1, (INNER, HIDDEN), dtype=jnp.float32) / np.sqrt(HIDDEN)
        w_up = jax.random.normal(k2, (INNER, HIDDEN), dtype=jnp.float32) / np.sqrt(HIDDEN)
        w_down = jax.random.normal(k3, (HIDDEN, INNER), dtype=jnp.float32) / np.sqrt(INNER)
        return {'x': x, 'w_gate': w_gate, 'w_up': w_up, 'w_down': w_down}
    _L3_ffn_all = _L3_ffn_setup()
    _L3_ffn_in = {k: v for k, v in _L3_ffn_all.items() if k in ('w_gate', 'w_up', 'w_down')}
    del _L3_ffn_all
    return {'x': x, 'ctx_1024': ctx_1024, 'mask_BxS2_bf1': mask_BxS2_bf1, 'L0_attn_W_dq': _L0_attn_in['W_dq'], 'L0_attn_W_uq': _L0_attn_in['W_uq'], 'L0_attn_W_dkv': _L0_attn_in['W_dkv'], 'L0_attn_W_uk': _L0_attn_in['W_uk'], 'L0_attn_W_uv': _L0_attn_in['W_uv'], 'L0_attn_W_o': _L0_attn_in['W_o'], 'L0_xattn_wq': _L0_xattn_in['wq'], 'L0_xattn_wk': _L0_xattn_in['wk'], 'L0_xattn_wv': _L0_xattn_in['wv'], 'L0_xattn_fc_w': _L0_xattn_in['fc_w'], 'L0_xattn_fc_b': _L0_xattn_in['fc_b'], 'L0_xattn_rel_table': _L0_xattn_in['rel_table'], 'L0_ffn_W': _L0_ffn_in['W'], 'L0_ffn_b': _L0_ffn_in['b'], 'L0_ffn_lora_down': _L0_ffn_in['lora_down'], 'L0_ffn_lora_up': _L0_ffn_in['lora_up'], 'L0_ffn_down_aux': _L0_ffn_in['down_aux'], 'L0_ffn_up_aux': _L0_ffn_in['up_aux'], 'L1_attn_delta': _L1_attn_in['delta'], 'L1_attn_alpha': _L1_attn_in['alpha'], 'L1_attn_beta': _L1_attn_in['beta'], 'L1_attn_gamma': _L1_attn_in['gamma'], 'L1_attn_omega': _L1_attn_in['omega'], 'L1_xattn_Wq': _L1_xattn_in['Wq'], 'L1_xattn_bq': _L1_xattn_in['bq'], 'L1_xattn_Wk': _L1_xattn_in['Wk'], 'L1_xattn_bk': _L1_xattn_in['bk'], 'L1_xattn_Wv': _L1_xattn_in['Wv'], 'L1_xattn_bv': _L1_xattn_in['bv'], 'L1_ffn_Wg': _L1_ffn_in['Wg'], 'L1_ffn_W1': _L1_ffn_in['W1'], 'L1_ffn_W2': _L1_ffn_in['W2'], 'L1_ffn_W3': _L1_ffn_in['W3'], 'L2_attn_ln_scale': _L2_attn_in['ln_scale'], 'L2_attn_ln_bias': _L2_attn_in['ln_bias'], 'L2_attn_wq': _L2_attn_in['wq'], 'L2_attn_wk': _L2_attn_in['wk'], 'L2_attn_wv': _L2_attn_in['wv'], 'L2_xattn_Wq': _L2_xattn_in['Wq'], 'L2_xattn_bq': _L2_xattn_in['bq'], 'L2_xattn_Wk': _L2_xattn_in['Wk'], 'L2_xattn_bk': _L2_xattn_in['bk'], 'L2_xattn_Wv': _L2_xattn_in['Wv'], 'L2_xattn_bv': _L2_xattn_in['bv'], 'L2_ffn_ln_gamma': _L2_ffn_in['ln_gamma'], 'L2_ffn_ln_beta': _L2_ffn_in['ln_beta'], 'L2_ffn_Wr': _L2_ffn_in['Wr'], 'L2_ffn_W12': _L2_ffn_in['W12'], 'L2_ffn_W3': _L2_ffn_in['W3'], 'L3_attn_W_Q': _L3_attn_in['W_Q'], 'L3_attn_b_Q': _L3_attn_in['b_Q'], 'L3_attn_W_K': _L3_attn_in['W_K'], 'L3_attn_b_K': _L3_attn_in['b_K'], 'L3_attn_W_V': _L3_attn_in['W_V'], 'L3_attn_b_V': _L3_attn_in['b_V'], 'L3_attn_W_O': _L3_attn_in['W_O'], 'L3_attn_b_O': _L3_attn_in['b_O'], 'L3_xattn_Wq': _L3_xattn_in['Wq'], 'L3_xattn_Wk': _L3_xattn_in['Wk'], 'L3_xattn_Wv': _L3_xattn_in['Wv'], 'L3_xattn_Wo': _L3_xattn_in['Wo'], 'L3_xattn_bo': _L3_xattn_in['bo'], 'L3_ffn_w_gate': _L3_ffn_in['w_gate'], 'L3_ffn_w_up': _L3_ffn_in['w_up'], 'L3_ffn_w_down': _L3_ffn_in['w_down']}

def reference(x, ctx_1024, mask_BxS2_bf1, L0_attn_W_dq, L0_attn_W_uq, L0_attn_W_dkv, L0_attn_W_uk, L0_attn_W_uv, L0_attn_W_o, L0_xattn_wq, L0_xattn_wk, L0_xattn_wv, L0_xattn_fc_w, L0_xattn_fc_b, L0_xattn_rel_table, L0_ffn_W, L0_ffn_b, L0_ffn_lora_down, L0_ffn_lora_up, L0_ffn_down_aux, L0_ffn_up_aux, L1_attn_delta, L1_attn_alpha, L1_attn_beta, L1_attn_gamma, L1_attn_omega, L1_xattn_Wq, L1_xattn_bq, L1_xattn_Wk, L1_xattn_bk, L1_xattn_Wv, L1_xattn_bv, L1_ffn_Wg, L1_ffn_W1, L1_ffn_W2, L1_ffn_W3, L2_attn_ln_scale, L2_attn_ln_bias, L2_attn_wq, L2_attn_wk, L2_attn_wv, L2_xattn_Wq, L2_xattn_bq, L2_xattn_Wk, L2_xattn_bk, L2_xattn_Wv, L2_xattn_bv, L2_ffn_ln_gamma, L2_ffn_ln_beta, L2_ffn_Wr, L2_ffn_W12, L2_ffn_W3, L3_attn_W_Q, L3_attn_b_Q, L3_attn_W_K, L3_attn_b_K, L3_attn_W_V, L3_attn_b_V, L3_attn_W_O, L3_attn_b_O, L3_xattn_Wq, L3_xattn_Wk, L3_xattn_Wv, L3_xattn_Wo, L3_xattn_bo, L3_ffn_w_gate, L3_ffn_w_up, L3_ffn_w_down):
    import jax
    import jax.numpy as jnp

    def _L0_attn_ref(x, W_dq, W_uq, W_dkv, W_uk, W_uv, W_o):
        import math
        import jax, jax.numpy as jnp
        import numpy as np
        D_MODEL = 128
        N_HEADS = 16
        D_K = D_MODEL // N_HEADS
        D_C = 32
        B, S = (2, 256)
        Bx, Sx, _ = x.shape
        c_q = x @ W_dq
        Q = (c_q @ W_uq).reshape(Bx, Sx, N_HEADS, D_K)
        c_kv = x @ W_dkv
        K = (c_kv @ W_uk).reshape(Bx, Sx, N_HEADS, D_K)
        V = (c_kv @ W_uv).reshape(Bx, Sx, N_HEADS, D_K)
        scores = jnp.einsum('bqhd,bkhd->bhqk', Q, K) / math.sqrt(D_K)
        causal = jnp.tril(jnp.ones((Sx, Sx), dtype=bool))
        scores = jnp.where(causal, scores, -jnp.inf)
        attn = jax.nn.softmax(scores, axis=-1)
        out = jnp.einsum('bhqk,bkhd->bqhd', attn, V).reshape(Bx, Sx, N_HEADS * D_K)
        return out @ W_o

    def _L0_xattn_ref(key, query, value, wq, wk, wv, fc_w, fc_b, rel_table):
        import jax, jax.numpy as jnp
        import numpy as np
        import math
        B, S, E = (2, 256, 128)
        H = 16
        DK = E // H
        MAX_DIST = 256

        def _split_heads(x):
            b, s, _ = x.shape
            return x.reshape(b, s, H, DK).transpose(0, 2, 1, 3)
        b, s, _ = query.shape
        k = _split_heads(key @ wk.T)
        q = _split_heads(query @ wq.T)
        v = _split_heads(value @ wv.T)
        ctx = jnp.arange(s)[:, None]
        mem = jnp.arange(s)[None, :]
        rel = jnp.clip(mem - ctx, -MAX_DIST + 1, MAX_DIST - 1) + MAX_DIST - 1
        bias = rel_table[rel]
        bias = bias.transpose(2, 0, 1)[None]
        scores = jnp.einsum('bhqd,bhkd->bhqk', q, k) / math.sqrt(DK)
        scores = scores + bias
        attn = jax.nn.softmax(scores, axis=-1)
        out = jnp.einsum('bhqk,bhkd->bhqd', attn, v)
        out = out.transpose(0, 2, 1, 3).reshape(b, s, E)
        return out @ fc_w.T + fc_b

    def _L0_ffn_ref(hidden_states, W, b, lora_down, lora_up, down_aux, up_aux):
        import jax, jax.numpy as jnp
        import numpy as np
        ALPHA = 1.0
        lilora_weight = up_aux @ (lora_up @ (lora_down @ down_aux))
        base = jnp.einsum('bsi,oi->bso', hidden_states, W) + b
        delta = jnp.einsum('bsi,oi->bso', hidden_states, lilora_weight)
        return base + ALPHA * delta

    def _L1_attn_ref(x, delta, alpha, beta, gamma, omega):
        import jax, jax.numpy as jnp
        import numpy as np
        L, B, D, N = (512, 4, 128, 16)
        seq_len = x.shape[0]
        scale = (1.0 / gamma.shape[1]) ** 0.5
        p = jax.nn.sigmoid(delta)
        q = 1.0 - p * jax.nn.sigmoid(alpha)
        t = jnp.arange(seq_len, dtype=x.dtype)
        vander = t[None, None, :] * jnp.log(q)
        kernel = p * beta * jnp.exp(vander)
        k = jnp.einsum('dnl,dn->dl', kernel, gamma * scale)
        residual = x * omega
        xt = jnp.transpose(x, (1, 2, 0))
        n_fft = 2 * seq_len
        k_f = jnp.fft.rfft(k.astype(jnp.float32), n=n_fft)
        x_f = jnp.fft.rfft(xt.astype(jnp.float32), n=n_fft)
        out = jnp.fft.irfft(x_f * k_f, n=n_fft)[..., :seq_len]
        out = out.astype(x.dtype)
        out = jax.nn.silu(jnp.transpose(out, (2, 0, 1)) + residual)
        return out

    def _L1_xattn_ref(queries, keys, values, Wq, bq, Wk, bk, Wv, bv):
        import jax, jax.numpy as jnp
        import numpy as np
        D = 128
        B, S = (4, 256)
        Q = jnp.einsum('bsd,ed->bse', queries, Wq) + bq
        K = jnp.einsum('bsd,ed->bse', keys, Wk) + bk
        V = jnp.einsum('bsd,ed->bse', values, Wv) + bv
        scores = jax.nn.relu(jnp.einsum('bqd,bkd->bqk', Q, K))
        return jnp.einsum('bqk,bkd->bqd', scores, V)

    def _L1_ffn_ref(x, Wg, W1, W2, W3):
        import jax, jax.numpy as jnp
        import numpy as np
        B, S, D, F, E, K = (2, 256, 128, 256, 8, 2)
        k = K
        scores = jnp.einsum('bsd,ed->bse', x, Wg)
        topk_scores, topk_idx = jax.lax.top_k(scores, k)
        topk_probs = jax.nn.softmax(topk_scores, axis=-1)
        h1 = jnp.einsum('bsd,efd->bsef', x, W1)
        h2 = jnp.einsum('bsd,efd->bsef', x, W2)
        hidden = jax.nn.silu(h1) * h2
        expert_out = jnp.einsum('bsef,edf->bsed', hidden, W3)
        onehot = jax.nn.one_hot(topk_idx, scores.shape[-1], dtype=x.dtype)
        gating = jnp.einsum('bsk,bske->bse', topk_probs, onehot)
        return jnp.einsum('bse,bsed->bsd', gating, expert_out)

    def _L2_attn_ref(x, ln_scale, ln_bias, wq, wk, wv):
        import jax, jax.numpy as jnp
        import numpy as np
        HIDDEN_DIM = 128
        NUM_HEADS = 16
        LN_EPS = 1e-06

        def _layernorm(x, scale, bias):
            mu = jnp.mean(x, axis=-1, keepdims=True)
            var = jnp.mean(jnp.square(x - mu), axis=-1, keepdims=True)
            return (x - mu) * jax.lax.rsqrt(var + LN_EPS) * scale + bias
        bs, sl, fdim = x.shape
        h, hd = (NUM_HEADS, HIDDEN_DIM // NUM_HEADS)
        xn = _layernorm(x, ln_scale, ln_bias)
        q = (xn @ wq).reshape(bs, sl, h, hd).transpose(0, 2, 1, 3)
        k = (xn @ wk).reshape(bs, sl, h, hd).transpose(0, 2, 1, 3)
        v = (xn @ wv).reshape(bs, sl, h, hd).transpose(0, 2, 1, 3)
        scores = jnp.einsum('bhid,bhjd->bhij', q, k)
        probs = jax.nn.softmax(scores / jnp.sqrt(jnp.float32(HIDDEN_DIM)), axis=-1)
        out = jnp.einsum('bhij,bhjd->bhid', probs, v)
        out = out.transpose(0, 2, 1, 3).reshape(bs, sl, -1) + xn
        return out

    def _L2_xattn_ref(input_seq, condition_seq, Wq, bq, Wk, bk, Wv, bv):
        import jax, jax.numpy as jnp
        import numpy as np
        B, SQ, SK, D = (4, 256, 256, 128)
        q = jnp.einsum('bsd,ed->bse', input_seq, Wq) + bq
        k = jnp.einsum('btd,ed->bte', condition_seq, Wk) + bk
        v = jnp.einsum('btd,ed->bte', condition_seq, Wv) + bv
        scores = jnp.einsum('bse,bte->bst', q, k)
        attn = jax.nn.softmax(scores, axis=-1)
        attended = jnp.einsum('bst,bte->bse', attn, v)
        return attended

    def _L2_ffn_ref(x, ln_gamma, ln_beta, Wr, W12, W3):
        import math
        import jax, jax.numpy as jnp
        import numpy as np
        D_MODEL = 128
        D_FF = 512
        E = 8
        K = 2
        CF = 1.25
        CLAMP = 10000.0
        B, S, D = x.shape
        T = B * S
        xf = x.reshape(T, D)
        mu = xf.mean(-1, keepdims=True)
        var = ((xf - mu) ** 2).mean(-1, keepdims=True)
        xn = (xf - mu) / jnp.sqrt(var + 1e-05) * ln_gamma + ln_beta
        logits = jnp.clip(xn @ Wr.T, -CLAMP, CLAMP)
        m = logits.max(-1, keepdims=True)
        ex = jnp.exp(logits - m)
        probs = ex / (ex.sum(-1, keepdims=True) + 1e-12)
        top_p, top_i = jax.lax.top_k(probs, K)
        Sslots = T * K
        experts = top_i.reshape(-1)
        weights = top_p.reshape(-1)
        tokens = jnp.repeat(jnp.arange(T, dtype=jnp.int32), K)
        order = jnp.argsort(experts, stable=True)
        e_s = experts[order]
        w_s = weights[order]
        t_s = tokens[order]
        counts = jnp.bincount(e_s, length=E)
        offsets = jnp.concatenate([jnp.zeros((1,), counts.dtype), jnp.cumsum(counts)])
        rank = jnp.arange(Sslots, dtype=counts.dtype) - offsets[e_s]
        cap = max(1, math.ceil(math.ceil(T * K * CF) / E))
        kept = rank < cap
        pos = jnp.where(kept, rank, cap)
        buf = jnp.zeros((E, cap, D), x.dtype).at[e_s, pos].set(xn[t_s], mode='drop')
        gu = jnp.einsum('ecd,efd->ecf', buf, W12)
        g, u = (gu[..., :D_FF], gu[..., D_FF:])
        h = jax.nn.silu(g) * u
        y = jnp.einsum('ecf,edf->ecd', h, W3)
        y_slot = y[e_s, jnp.minimum(pos, cap - 1)] * (w_s * kept.astype(x.dtype))[:, None]
        out = jnp.zeros((T, D), x.dtype).at[t_s].add(y_slot)
        return out.reshape(B, S, D)

    def _L3_attn_ref(x, W_Q, b_Q, W_K, b_K, W_V, b_V, W_O, b_O):
        import jax, jax.numpy as jnp
        import numpy as np
        D_MODEL = 128
        N_HEADS = 16
        D_HEAD = 64
        ROTARY_DIM = 64
        ROTARY_BASE = 10000.0
        ATTN_SCALE = 8.0

        def _rope_sin_cos(n_pos, rotary_dim):
            pos = jnp.arange(n_pos, dtype=jnp.float32)
            dim = jnp.arange(rotary_dim // 2, dtype=jnp.float32)
            freq = ROTARY_BASE ** (dim / (rotary_dim / 2))
            freq = jnp.concatenate([freq, freq])
            angles = pos[:, None] / freq[None, :]
            return (jnp.sin(angles), jnp.cos(angles))

        def _apply_rotary(x, sin, cos):
            n = x.shape[-1] // 2
            x_flip = jnp.concatenate([-x[..., n:], x[..., :n]], axis=-1)
            return x * cos[None, :, None, :] + x_flip * sin[None, :, None, :]
        B, S, _ = x.shape
        q = jnp.einsum('bsd,hdk->bshk', x, W_Q) + b_Q
        k = jnp.einsum('bsd,hdk->bshk', x, W_K) + b_K
        v = jnp.einsum('bsd,hdk->bshk', x, W_V) + b_V
        sin, cos = _rope_sin_cos(S, ROTARY_DIM)
        q = _apply_rotary(q, sin, cos)
        k = _apply_rotary(k, sin, cos)
        scores = jnp.einsum('bqhd,bkhd->bhqk', q, k) / ATTN_SCALE
        causal = jnp.tril(jnp.ones((S, S), dtype=bool))
        scores = jnp.where(causal[None, None], scores, -jnp.inf)
        pattern = jax.nn.softmax(scores, axis=-1)
        pattern = jnp.where(jnp.isnan(pattern), jnp.zeros_like(pattern), pattern)
        z = jnp.einsum('bhqk,bkhd->bqhd', pattern, v)
        out = jnp.einsum('bqhd,hdm->bqm', z, W_O) + b_O
        return out

    def _L3_xattn_ref(query, key, value, key_padding_mask, Wq, Wk, Wv, Wo, bo):
        import jax, jax.numpy as jnp
        import numpy as np
        NEG_INF = -10000000000.0
        nheads = 16
        B, Sq, D = query.shape
        d_k = D // nheads
        scale = 1.0 / jnp.sqrt(jnp.asarray(d_k, query.dtype))
        q = query @ Wq.T
        k = key @ Wk.T
        v = value @ Wv.T
        q = q.reshape(B, Sq, nheads, d_k)
        k = k.reshape(B, -1, nheads, d_k)
        v = v.reshape(B, -1, nheads, d_k)
        scores = jnp.einsum('bqhd,bkhd->bhqk', q, k) * scale
        mask = key_padding_mask[:, None, None, :]
        scores = jnp.where(mask, scores, jnp.asarray(NEG_INF, scores.dtype))
        attn = jax.nn.softmax(scores, axis=-1)
        out = jnp.einsum('bhqk,bkhd->bqhd', attn, v)
        out = out.reshape(B, Sq, D)
        return out @ Wo.T + bo

    def _L3_ffn_ref(x, w_gate, w_up, w_down):
        import jax, jax.numpy as jnp
        import numpy as np
        HIDDEN = 128
        INNER = 512

        def _weight_quant(w):
            scale = 1.0 / jnp.clip(jnp.mean(jnp.abs(w)), 1e-05)
            wq = jnp.clip(jnp.round(w * scale), -1.0, 1.0) / scale
            return w + jax.lax.stop_gradient(wq - w)

        def _act_quant(x):
            scale = 127.0 / jnp.clip(jnp.max(jnp.abs(x), axis=-1, keepdims=True), 1e-05)
            xq = jnp.clip(jnp.round(x * scale), -128.0, 127.0) / scale
            return x + jax.lax.stop_gradient(xq - x)

        def _bitlinear(x, w):
            return jnp.einsum('bsi,oi->bso', _act_quant(x), _weight_quant(w))
        gate = jax.nn.silu(_bitlinear(x, w_gate))
        up = _bitlinear(x, w_up)
        return _bitlinear(gate * up, w_down)
    x = x + _L0_attn_ref(_layernorm(x, axis=-1), L0_attn_W_dq, L0_attn_W_uq, L0_attn_W_dkv, L0_attn_W_uk, L0_attn_W_uv, L0_attn_W_o)
    x = x + _L0_xattn_ref(ctx_1024, _layernorm(x, axis=-1), ctx_1024, L0_xattn_wq, L0_xattn_wk, L0_xattn_wv, L0_xattn_fc_w, L0_xattn_fc_b, L0_xattn_rel_table)
    x = x + _L0_ffn_ref(_layernorm(x, axis=-1), L0_ffn_W, L0_ffn_b, L0_ffn_lora_down, L0_ffn_lora_up, L0_ffn_down_aux, L0_ffn_up_aux)
    x = x + _L1_attn_ref(_layernorm(x, axis=-1), L1_attn_delta, L1_attn_alpha, L1_attn_beta, L1_attn_gamma, L1_attn_omega)
    x = x + _L1_xattn_ref(_layernorm(x, axis=-1), ctx_1024, ctx_1024, L1_xattn_Wq, L1_xattn_bq, L1_xattn_Wk, L1_xattn_bk, L1_xattn_Wv, L1_xattn_bv)
    x = x + _L1_ffn_ref(_layernorm(x, axis=-1), L1_ffn_Wg, L1_ffn_W1, L1_ffn_W2, L1_ffn_W3)
    x = x + _L2_attn_ref(_layernorm(x, axis=-1), L2_attn_ln_scale, L2_attn_ln_bias, L2_attn_wq, L2_attn_wk, L2_attn_wv)
    x = x + _L2_xattn_ref(_layernorm(x, axis=-1), ctx_1024, L2_xattn_Wq, L2_xattn_bq, L2_xattn_Wk, L2_xattn_bk, L2_xattn_Wv, L2_xattn_bv)
    x = x + _L2_ffn_ref(_layernorm(x, axis=-1), L2_ffn_ln_gamma, L2_ffn_ln_beta, L2_ffn_Wr, L2_ffn_W12, L2_ffn_W3)
    x = x + _L3_attn_ref(_layernorm(x, axis=-1), L3_attn_W_Q, L3_attn_b_Q, L3_attn_W_K, L3_attn_b_K, L3_attn_W_V, L3_attn_b_V, L3_attn_W_O, L3_attn_b_O)
    x = x + _L3_xattn_ref(_layernorm(x, axis=-1), ctx_1024, ctx_1024, mask_BxS2_bf1, L3_xattn_Wq, L3_xattn_Wk, L3_xattn_Wv, L3_xattn_Wo, L3_xattn_bo)
    x = x + _L3_ffn_ref(_layernorm(x, axis=-1), L3_ffn_w_gate, L3_ffn_w_up, L3_ffn_w_down)
    return x

_drawn_inputs = setup_inputs


def setup_inputs(seed=0):
    import zlib

    import numpy as np

    out = dict(_drawn_inputs(seed))
    spreads = {'L2_attn_ln_scale': (1.0, 0.6),
     'L2_attn_ln_bias': (0.0, 0.8),
     'L2_xattn_bq': (0.0, 0.8),
     'L2_xattn_bk': (0.0, 2.0),
     'L2_xattn_bv': (0.0, 0.8),
     'L2_ffn_ln_gamma': (1.0, 0.6),
     'L2_ffn_ln_beta': (0.0, 0.8),
     'L3_attn_b_Q': (0.0, 0.8),
     'L3_attn_b_K': (0.0, 2.0),
     'L3_attn_b_V': (0.0, 0.8),
     'L3_attn_b_O': (0.0, 2.0),
     'L3_xattn_bo': (0.0, 2.0)}
    factors = {'L0_attn_W_dq': 8.0,
     'L0_attn_W_uq': 8.0,
     'L0_attn_W_uk': 8.0,
     'L0_xattn_rel_table': 8.0,
     'L0_ffn_b': 3.449,
     'L0_ffn_lora_down': 7.032,
     'L0_ffn_lora_up': 6.994,
     'L0_ffn_down_aux': 6.376,
     'L0_ffn_up_aux': 6.54,
     'L1_attn_delta': 2.84,
     'L1_attn_alpha': 4.015,
     'L1_attn_beta': 8.0,
     'L1_ffn_Wg': 8.0,
     'L1_ffn_W1': 8.0,
     'L1_ffn_W2': 8.0,
     'L1_ffn_W3': 8.0,
     'L2_attn_wq': 8.0,
     'L2_attn_wk': 8.0,
     'L2_attn_wv': 2.681,
     'L2_xattn_Wq': 2.713,
     'L2_ffn_Wr': 8.0,
     'L2_ffn_W12': 8.0,
     'L2_ffn_W3': 8.0,
     'L3_attn_W_Q': 8.0,
     'L3_attn_W_K': 8.0,
     'L3_attn_W_V': 8.0,
     'L3_attn_W_O': 8.0,
     'L3_xattn_Wq': 8.0,
     'L3_xattn_Wk': 8.0,
     'L3_xattn_Wv': 4.224,
     'L3_xattn_Wo': 4.399,
     'L3_ffn_w_gate': 8.0,
     'L3_ffn_w_up': 8.0,
     'L3_ffn_w_down': 8.0}
    for name, (base, spread) in spreads.items():
        noise = np.random.default_rng([zlib.crc32(name.encode()), seed]).standard_normal(out[name].shape)
        drawn = base * np.exp(spread * noise) if base else spread * noise
        out[name] = jnp.asarray(drawn.astype(out[name].dtype))
    for name, factor in factors.items():
        out[name] = (out[name] * factor).astype(out[name].dtype)
    return out
```

```python
from contextlib import ExitStack

import numpy as np

import concourse.bass as bass
from concourse import mybir

F32 = mybir.dt.float32
BF16 = mybir.dt.bfloat16
I32 = mybir.dt.int32
U32 = mybir.dt.uint32
U8 = mybir.dt.uint8
ALU = mybir.AluOpType
ACT = mybir.ActivationFunctionType
AX = mybir.AxisListType

P = 128
D = 128
B, S = 16, 64
T = B * S
TILES = T // P
HALF = T // 2
HT = TILES // 2
HB = B // 2
HEADS, DH = 16, 8
HH = HEADS // 2
E = 8
F1, F2 = 256, 512
F3 = 512
HD3 = 64
CAP = -(-(-(-T * 2 * 5 // 4)) // E)
BIG = 1e30
NEG = 1e10
ROUND = 12582912.0

A0, X0, A2, A3, X3 = range(5)

COLS_A = [("ident", 128), ("dqkv", 64), ("uq", 128), ("uk", 128), ("uv", 128), ("wo0", 128),
          ("wq0", 128), ("wk0", 128), ("wv0", 128), ("fc0", 128),
          ("ffW", 128), ("lordT", 4), ("dauxT", 128), ("loruT", 50), ("uauxT", 128),
          ("hm", 8), ("mhalf", 4), ("iota", 8), ("padc", 1), ("mean", 128)]
COLS_B = [("delta", 16), ("alpha", 16), ("beta", 16), ("gamma", 16), ("omega", 1),
          ("wq1", 128), ("wk1", 128), ("wv1", 128), ("bq1", 1), ("bk1", 1), ("wg1", 8), ("blk", 128),
          ("wqa2", 128), ("wka2", 128), ("wva2", 128), ("lns2", 1), ("lnb2", 1),
          ("wq2", 128), ("wk2", 128), ("wv2", 128), ("bq2", 1), ("bk2", 1),
          ("gam2", 1), ("bet2", 1), ("wr2", 8),
          ("wq3", 128), ("wk3", 128), ("wv3", 128), ("wo3", 128),
          ("bQ3", 8), ("bK3", 8), ("bV3", 8), ("cos", 64), ("sin", 64), ("lgrid", 16)]
COLS_H = [("identb", 128), ("causal", 64), ("offblk", 128), ("before", 128), ("ones", 128)]
ROWS = [("fcb", 128), ("ffb", 128), ("bv1", 128), ("bv2", 128), ("bO3", 128), ("bo3", 128)]


def offsets(cols):
    at, out = 0, {}
    for name, n in cols:
        out[name] = (at, n)
        at += n
    return out, at


OFF_A, N_A = offsets(COLS_A)
OFF_B, N_B = offsets(COLS_B)
OFF_H, N_H = offsets(COLS_H)
OFF_R, N_R = offsets(ROWS)


def spread(ap, dims):
    return bass.AP(ap.tensor, ap.offset, [list(ap.ap[0])] + [list(d) for d in dims])


def bass_decoder_kernel(nc, x_in, ctxT_in, pad_in, packA, packB, packH, rows, relb, w1_in, w13_in, w2_in, w23_in,
                        w3qkv_in, w3o_in, wf3_in, out):
    with ExitStack() as ctx:
        def sb(name, shape, dt=F32):
            return ctx.enter_context(nc.sbuf_tensor(name, shape, dt))

        def ps(name):
            return ctx.enter_context(nc.psum_tensor(name, [P, 512], F32))

        def sem(name):
            return ctx.enter_context(nc.semaphore(name))

        sA = sb("sA", [P, N_A])
        sB = sb("sB", [P, N_B])
        sH = sb("sH", [P, N_H], BF16)
        sR = sb("sR", [P, N_R])

        def A(name, p=P):
            o, n = OFF_A[name]
            return sA[0:p, o:o + n]

        def Bc(name):
            o, n = OFF_B[name]
            return sB[:, o:o + n]

        def Hc(name, p=P):
            o, n = OFF_H[name]
            return sH[0:p, o:o + n]

        def row(name):
            o, n = OFF_R[name]
            return sR[:, o:o + n]

        moe1 = sb("moe1", [P, E * (2 * F1 + F1)])
        w1 = moe1[:, 0:E * 2 * F1].rearrange("p (e f) -> p e f", e=E)
        w13 = moe1[:, E * 2 * F1:].rearrange("p (e c d) -> p e c d", e=E, c=F1 // P)
        w3qkv = moe1[:, 0:3 * 1024].rearrange("p (w n) -> p w n", w=3)
        w3o = moe1[:, 3 * 1024:4 * 1024].rearrange("p (c d) -> p c d", c=8)
        zT = moe1[:, 4 * 1024:6 * 1024].rearrange("p (r c q) -> p r c q", r=2, c=8)
        moe2 = sb("moe2", [P, E * (2 * F2 + F2)])
        w2 = moe2[:, 0:E * 2 * F2].rearrange("p (e f) -> p e f", e=E)
        w23 = moe2[:, E * 2 * F2:].rearrange("p (e c d) -> p e c d", e=E, c=F2 // P)
        qsw = moe2[:, 0:4096].rearrange("p (c q) -> p c q", c=8)
        ksw = moe2[:, 4096:8192].rearrange("p (c q) -> p c q", c=8)
        v3 = moe2[:, 8192:12288].rearrange("p (b n) -> p b n", b=HB)
        wf3 = moe1[:, 0:3 * F3]
        wf3q = sb("wf3q", [P, 3 * F3], BF16)
        rel = moe1[:, 3 * F3:3 * F3 + 512]
        relh = sb("relh", [P, 4, 512], BF16)

        x = sb("x", [P, TILES, D])
        y = sb("y", [P, TILES, D])
        yT = sb("yT", [P, T])
        ctxT = sb("ctxT", [P, T])
        kT = y[:, :, :].rearrange("p t d -> p (t d)")
        oT = sb("oT", [P, T])
        qbd = sb("qbd", [P, B, P])
        km = sb("km", [P, HH, T])
        vb = sb("vb", [P, B, 512])
        pr = sb("pr", [P, 4, 512])
        pT = sb("pT", [P, 2, 512])
        qf = km[:, 0, :]
        hid = km[:, :, :].rearrange("p a b -> p (a b)")[:, 0:4096].rearrange("p (s c q) -> p s c q", s=2, c=4)
        sg = km[:, :, :].rearrange("p a b -> p (a b)")[:, 4096:5120].rearrange("p (s q) -> p s q", s=2)
        qraw = km[:, 0:4, :].rearrange("p a b -> p (a b)").rearrange("p (c q) -> p c q", c=8)
        kraw = km[:, 4:8, :].rearrange("p a b -> p (a b)").rearrange("p (c q) -> p c q", c=8)
        vt = oT[:, :].rearrange("p (t d) -> p t d", t=TILES)

        bst = sb("bst", [P, TILES, 6])
        mv = sb("mv", [P, TILES, 2])
        ve = sb("ve", [P, TILES])
        rstd = sb("rstd", [P, TILES])
        mx = sb("mx", [P, 4, 8])
        sm = sb("sm", [P, 4, 8])
        rc = sb("rc", [P, 4, 8])
        a4 = sb("a4", [4, P])
        a50 = sb("a50", [50, P])
        weff = sb("weff", [P, D])
        ex1 = sb("ex1", [P, 2, 16])
        pq = sb("pq", [P, 4, 16])
        kg = pT[:, 0, :].rearrange("p (i n l) -> p i n l", i=2, n=16)
        kl = sb("kl", [P, 17])
        lg = sb("lg", [P, TILES, E])
        m8 = sb("m8", [P, TILES, E])
        i8 = sb("i8", [P, TILES, E], U32)
        f8 = sb("f8", [P, TILES, E])
        g8 = sb("g8", [P, 4, TILES])
        e8 = sb("e8", [P, 2, TILES, E])
        gw = sb("gw", [P, TILES, E])
        selb = sb("selb", [P, TILES, E], BF16)
        pad8 = moe1[0:3, 2048:2304].bitcast(U8)
        addm = relh[0:3, 0:2, :].rearrange("p a b -> p (a b)")
        padb = relh[0:1, 2:4, :].rearrange("p a b -> p (a b)")
        q8 = sb("q8", [P, 6, TILES])
        ws = sb("ws", [P, 4, 4])
        xqT = moe2[:, 0:512].bitcast(BF16)
        hb = moe2[:, 512:1024].bitcast(BF16).rearrange("p (r f) -> p r f", r=2)
        hqT = moe2[:, 1024:1536].bitcast(BF16).rearrange("p (r c q) -> p r c q", r=2, c=4)

        score = [ps(f"score{i}") for i in range(4)]
        ptb = [ps(f"ptb{i}") for i in range(2)]
        ub = [ps(f"unit{i}") for i in range(2)]

        ld_a, ld_b, ld_h, ld_r = sem("ld_a"), sem("ld_b"), sem("ld_h"), sem("ld_r")
        ld_x, ld_ctx, ld_pad, ld_rel = sem("ld_x"), sem("ld_ctx"), sem("ld_pad"), sem("ld_rel")
        ld_w1, ld_w2, ld_w3a, ld_wf3 = sem("ld_w1"), sem("ld_w2"), sem("ld_w3a"), sem("ld_wf3")
        stored = sem("stored")
        zeroed = sem("zeroed")
        unit_full = sem("unit_full")
        unit_read = [sem("unit_read0"), sem("unit_read1")]
        ln_stat, ln_mv, ln_ve, ln_rstd, ln_y = (sem(n) for n in ("ln_stat", "ln_mv", "ln_ve", "ln_rstd", "ln_y"))
        keys_spread = sem("keys_spread")
        sc_full = sem("sc_full")
        row_max, shifted, row_sum, row_rcp = (sem(n) for n in ("row_max", "shifted", "row_sum", "row_rcp"))
        exped = sem("exped")
        normed = sem("normed")
        turned = sem("turned")
        turn_read = sem("turn_read")
        x_biased = sem("x_biased")
        bias_split = sem("bias_split")
        pad_ready = sem("pad_ready")
        abs_sum = sem("abs_sum")
        ternary = sem("ternary")
        chosen = sem("chosen")
        sig_exp, pq_done, log_q, tap_arg, tap_exp = (sem(n) for n in ("sig_exp", "pq_done", "log_q", "tap_arg", "tap_exp"))
        conv = sem("conv")
        convact = sem("convact")
        gate_arg, gate_exp = sem("gate_arg"), sem("gate_exp")
        gu_full = sem("gu_full")
        silued = sem("silued")
        hidden = sem("hidden")
        small_a = sem("small_a")
        added = sem("added")
        swapped = [sem(f"swapped{i}") for i in range(4)]
        rot_c, rot_s, rot = sem("rot_c"), sem("rot_s"), sem("rot")
        quant_x, quant_t, quant_arg = sem("quant_x"), sem("quant_t"), sem("quant_arg")
        dve_step = sem("dve_step")

        block = ctx.enter_context(nc.Block())
        unit = {}
        padB = km[:, 0, :]

        def full(eng, key):
            eng.wait_ge(unit_full, unit[key] + 1)

        def read(eng, key):
            n = unit[key]
            eng.wait_ge(unit_read[n % 2], n // 2 + 1)

        def bank(key):
            return ub[unit[key] % 2]

        def done(ins, key):
            return ins.then_inc(unit_read[unit[key] % 2], 1)

        SOFT = [A0, X0, A2, X3]
        g0 = {a: 16 * a for a in (A0, X0, A2, A3, X3)}
        TOTAL_SPREAD = {a: 16 * n for n, a in enumerate(SOFT)}
        NGU1, NGU2 = 2 * E * (F1 // P), 2 * E * (F2 // P)

        def value_parts(key, c):
            for b2 in range(2):
                for hh in range(2):
                    for half in range(2):
                        src = bank(key)[64 * b2:64 * b2 + 64, 64 * half + 8 * hh:]
                        dst = vb[64 * hh:64 * hh + 64, HB * c + b2, 64 * half + 8 * hh:]
                        yield (spread(dst, [[2 * 512, HT], [P + 16, 4], [1, DH]]),
                               spread(src, [[P, HT], [16, 4], [1, DH]]))

        def value_parts3(key, i, h):
            for b2 in range(2):
                for hp in range(2):
                    src = bank(key)[64 * b2:64 * b2 + 64, hp * P:]
                    dst = v3[64 * hp:64 * hp + 64, 2 * i + b2, 2 * h * P:]
                    yield spread(dst, [[P, 2], [1, P]]), spread(src, [[2 * P, 2], [1, P]])

        @block.tensor
        def _(pe):
            def new(key):
                n = len(unit)
                unit[key] = n
                if n >= 2:
                    pe.wait_ge(unit_read[n % 2], n // 2)
                return ub[n % 2]

            def mm(o, l, r, first=True, last=True):
                return nc.tensor.matmul(o, l, r, start=first, stop=last)

            def ln_turn(L):
                for c in range(2):
                    u = new(("yT", L, c))
                    pe.wait_ge(ln_y, TILES * L + HT * (c + 1))
                    for i in range(HT):
                        m = nc.tensor.transpose(u[:, i * P:(i + 1) * P], y[:, HT * c + i, :], A("ident"))
                    m.then_inc(unit_full, 1)

            def project(name, w, src, wait=None, m=D, k=slice(0, P)):
                for c in range(2):
                    u = new((name, c))
                    if wait:
                        wait(c)
                    mm(u[0:m, :], w, src[k, c * HALF:(c + 1) * HALF]).then_inc(unit_full, 1)

            def to_tokens(name, w, src, wait=None, k=slice(0, P)):
                for c in range(2):
                    u = new((name, c))
                    if wait:
                        wait(c)
                    for i in range(HT):
                        t = HT * c + i
                        last = mm(u[:, i * P:(i + 1) * P], src[k, t * P:(t + 1) * P], w)
                    last.then_inc(unit_full, 1)

            def soft(a, extra=None):
                g = g0[a]

                def scores(b):
                    if g + b >= 4:
                        pe.wait_ge(shifted, g + b - 3)
                    if b % HB == 0:
                        read(pe, (("q", a), b // HB))
                        pe.wait_ge(keys_spread, TOTAL_SPREAD[a] + 8 * (b // HB + 1))
                    bk = score[(g + b) % 4]
                    last = mm(bk[:, :], qbd[:, b, :], km[:, :, b * S:(b + 1) * S], True, extra is None)
                    if extra:
                        last = extra(bk, b)
                    last.then_inc(sc_full, 1)

                for b in range(3):
                    scores(b)
                for b in range(B):
                    if b + 3 < B:
                        scores(b + 3)
                    pe.wait_ge(normed, g + b + 1)
                    if g + b >= 2:
                        pe.wait_ge(turn_read, g + b - 1)
                    tb = ptb[(g + b) % 2]
                    for j in range(4):
                        last = nc.tensor.transpose(tb[:, j * P:(j + 1) * P], pr[:, (g + b) % 4, j * P:(j + 1) * P],
                                                   A("ident"))
                    last.then_inc(turned, 1)
                    if b % 4 == 0:
                        u = new((("O", a), b // 4))
                    if b % HB == 0:
                        read(pe, (("v", a), b // HB))
                    pe.wait_ge(turn_read, g + b + 1)
                    for j in range(4):
                        last = mm(u[:, (b % 4) * P:(b % 4 + 1) * P], vb[:, b, j * P:(j + 1) * P],
                                  pT[:, (g + b) % 2, j * P:(j + 1) * P], j == 0, j == 3)
                    if b % 4 == 3:
                        last.then_inc(unit_full, 1)

            def wait_yT(L):
                return lambda c: read(pe, ("yT", L, c))

            def causal_mask(bk, b):
                return mm(bk[:, :], Hc("identb"), spread(Hc("causal"), [[0, HH], [1, S]]), False, True)

            def wait_O(a):
                def w(c):
                    read(pe, (("O", a), 2 * c))
                    read(pe, (("O", a), 2 * c + 1))
                return w

            def experts(name, L, wa, wb, fn, base):
                nf = fn // P
                n = [0]

                def gate_up(e, c):
                    for f in range(nf):
                        k = base + n[0]
                        n[0] += 1
                        if n[0] > 2:
                            pe.wait_ge(hidden, k - 1)
                        for h in range(2):
                            m = mm(score[2 * (k % 2) + h][:, :], wa[:, e, h * fn + f * P:h * fn + (f + 1) * P],
                                   yT[:, c * HALF:(c + 1) * HALF])
                        m.then_inc(gu_full, 1)

                def down(e, c):
                    u = new((name, e, c))
                    k = base + nf * (2 * e + c + 1)
                    pe.wait_ge(hidden, k)
                    for i in range(HT):
                        for f in range(nf):
                            m = mm(u[:, i * P:(i + 1) * P], hid[:, (2 * e + c) % 2, f, i * P:(i + 1) * P],
                                   wb[:, e, f, :], f == 0, f == nf - 1)
                    m.then_inc(unit_full, 1)

                steps = [(e, c) for e in range(E) for c in range(2)]
                gate_up(*steps[0])
                for k, st in enumerate(steps):
                    if k + 1 < len(steps):
                        gate_up(*steps[k + 1])
                    down(*st)

            pe.wait_ge(ld_a, 16)
            pe.wait_ge(ld_h, 16)
            pe.wait_ge(zeroed, 1)
            ln_turn(0)
            project("c0", A("dqkv"), yT, wait_yT(0), m=64)
            wait_c = lambda c: read(pe, ("c0", c))
            project(("q", A0), A("uq", 32), oT, wait_c, k=slice(0, 32))
            ouk, ouv = OFF_A["uk"][0], OFF_A["uv"][0]
            project(("k", A0), sA[32:64, ouk:ouk + D], oT, wait_c, k=slice(32, 64))
            to_tokens(("v", A0), sA[32:64, ouv:ouv + D], oT, wait_c, k=slice(32, 64))
            soft(A0, causal_mask)
            to_tokens("o0", A("wo0"), oT, wait_O(A0))

            ln_turn(1)
            project(("q", X0), A("wq0"), yT, wait_yT(1))
            pe.wait_ge(ld_ctx, 16)
            project(("k", X0), A("wk0"), ctxT)
            to_tokens(("v", X0), A("wv0"), ctxT)

            def rel_bias(bk, b):
                if b == 0:
                    pe.wait_ge(bias_split, 1)
                for i in range(3):
                    m = mm(bk[:, :], Hc("identb"), relh[:, i, :], False, i == 2)
                return m

            soft(X0, rel_bias)
            to_tokens("o0x", A("fc0"), oT, wait_O(X0))

            ln_turn(2)
            u = new("lo1")
            mm(u[0:4, 0:P], A("lordT", 100), A("dauxT", 100)).then_inc(unit_full, 1)
            u = new("lo2")
            read(pe, "lo1")
            mm(u[0:50, 0:P], A("loruT", 4), a4[:, :]).then_inc(unit_full, 1)
            u = new("lo3")
            read(pe, "lo2")
            mm(u[:, 0:P], a50[:, :], A("uauxT", 50)).then_inc(unit_full, 1)
            to_tokens("f0", weff[:, :], yT, lambda c: (read(pe, "lo3"), read(pe, ("yT", 2, c))))

            u = new("wsum")
            pe.wait_ge(abs_sum, 1)
            mm(u[:, 0:3], A("mean"), ws[:, 0, 0:3]).then_inc(unit_full, 1)

            ln_turn(3)
            pe.wait_ge(convact, 1)
            for c in range(2):
                u = new(("cv", c))
                for i in range(HT):
                    t = HT * c + i
                    m = nc.tensor.transpose(u[:, i * P:(i + 1) * P], oT[:, t * P:(t + 1) * P], A("ident"))
                m.then_inc(unit_full, 1)

            ln_turn(4)
            pe.wait_ge(ld_b, 16)
            project("q1", Bc("wq1"), yT, wait_yT(4))
            project("k1", Bc("wk1"), ctxT)
            to_tokens("v1", Bc("wv1"), ctxT)
            for c in range(2):
                u = new(("s1", c))
                read(pe, ("q1", c))
                read(pe, ("k1", c))
                for i in range(HT):
                    sl = slice((HT * c + i) * P, (HT * c + i + 1) * P)
                    m = mm(u[:, i * P:(i + 1) * P], kT[:, sl], qf[:, sl])
                m.then_inc(unit_full, 1)
            for c in range(2):
                u = new(("o1", c))
                read(pe, ("s1", c))
                read(pe, ("v1", c))
                for i in range(HT):
                    m = mm(u[:, i * P:(i + 1) * P], pr[:, c, i * P:(i + 1) * P], vt[:, HT * c + i, :])
                m.then_inc(unit_full, 1)

            ln_turn(5)
            u = new("g1")
            for c in range(2):
                read(pe, ("yT", 5, c))
            for t in range(TILES):
                m = mm(u[:, t * E:(t + 1) * E], yT[:, t * P:(t + 1) * P], Bc("wg1"))
            m.then_inc(unit_full, 1)
            pe.wait_ge(ld_w1, 32)
            experts("m1", 5, w1, w13, F1, 0)

            ln_turn(6 + 1)
            project(("q", A2), Bc("wqa2"), yT, wait_yT(7))
            project(("k", A2), Bc("wka2"), yT)
            to_tokens(("v", A2), Bc("wva2"), yT)
            soft(A2)
            for c in range(2):
                u = new(("o2", c))
                pe.wait_ge(added, c + 1)
                for i in range(HT):
                    t = HT * c + i
                    m = nc.tensor.transpose(u[:, i * P:(i + 1) * P], oT[:, t * P:(t + 1) * P], A("ident"))
                m.then_inc(unit_full, 1)

            ln_turn(8)
            project("q2", Bc("wq2"), yT, wait_yT(8))
            project("k2", Bc("wk2"), ctxT)
            to_tokens("v2", Bc("wv2"), ctxT)
            for c in range(2):
                u = new(("s2", c))
                read(pe, ("q2", c))
                read(pe, ("k2", c))
                mm(u[:, :], Hc("identb"), spread(Hc("offblk"), [[0, HT], [1, P]]), True, False)
                for i in range(HT):
                    sl = slice((HT * c + i) * P, (HT * c + i + 1) * P)
                    m = mm(u[:, i * P:(i + 1) * P], qf[:, sl], kT[:, sl], False, i == HT - 1)
                m.then_inc(unit_full, 1)
            for c in range(2):
                u = new(("p2", c))
                pe.wait_ge(small_a, c + 1)
                for i in range(HT):
                    m = nc.tensor.transpose(u[:, i * P:(i + 1) * P], pr[:, c, i * P:(i + 1) * P], A("ident"))
                m.then_inc(unit_full, 1)
            for c in range(2):
                u = new(("o2x", c))
                read(pe, ("p2", c))
                read(pe, ("v2", c))
                for i in range(HT):
                    m = mm(u[:, i * P:(i + 1) * P], pT[:, c, i * P:(i + 1) * P], vt[:, HT * c + i, :])
                m.then_inc(unit_full, 1)

            ln_turn(9 + 1)
            u = new("g2")
            for c in range(2):
                read(pe, ("yT", 10, c))
            for t in range(TILES):
                m = mm(u[:, t * E:(t + 1) * E], yT[:, t * P:(t + 1) * P], Bc("wr2"))
            m.then_inc(unit_full, 1)
            u = new("rank")
            pe.wait_ge(chosen, 1)
            sf = selb[:, :, :].rearrange("p t e -> p (t e)")
            mm(u[:, 0:TILES * E], Hc("before"), sf, True, False)
            for t in range(TILES - 1):
                n = TILES - 1 - t
                m = mm(u[:, (t + 1) * E:TILES * E], Hc("ones"), spread(selb[:, t, :], [[0, n], [1, E]]), False,
                       t == TILES - 2)
            m.then_inc(unit_full, 1)
            pe.wait_ge(ld_w2, 32)
            experts("m2", 10, w2, w23, F2, NGU1)

            ln_turn(11)
            pe.wait_ge(ld_w3a, 32)
            for c in range(2):
                read(pe, ("yT", 11, c))
                for w in range(2):
                    for i in range(8):
                        u = new(("qk3", c, w, i))
                        mm(u[:, :], w3qkv[:, w, i * P:(i + 1) * P], yT[:, c * HALF:(c + 1) * HALF])\
                            .then_inc(unit_full, 1)
                for i in range(HT):
                    for h in range(2):
                        u = new(("v3", c, i, h))
                        t = HT * c + i
                        mm(u[:, :], yT[:, t * P:(t + 1) * P], w3qkv[:, 2, h * 512:(h + 1) * 512])\
                            .then_inc(unit_full, 1)

                def scores(b):
                    gb = g0[A3] + HB * c + b
                    pe.wait_ge(shifted, gb - 3)
                    if b == 0:
                        pe.wait_ge(rot, 16 * (c + 1))
                    bk = score[gb % 4]
                    mm(bk[:, :], Hc("identb"), spread(Hc("causal"), [[0, HH], [1, S]]), True, False)
                    for h in range(8):
                        for s in range(2):
                            m = mm(bk[64 * s:64 * s + 64, h * S:(h + 1) * S], qraw[64 * s:64 * s + 64, h, b * S:(b + 1) * S],
                                   kraw[64 * s:64 * s + 64, h, b * S:(b + 1) * S], False, h == 7)
                    m.then_inc(sc_full, 1)

                for b in range(3):
                    scores(b)
                for b in range(HB):
                    gb = g0[A3] + HB * c + b
                    if b + 3 < HB:
                        scores(b + 3)
                    pe.wait_ge(normed, gb + 1)
                    pe.wait_ge(turn_read, gb - 1)
                    for j in range(4):
                        m = nc.tensor.transpose(ptb[gb % 2][:, j * P:(j + 1) * P], pr[:, gb % 4, j * P:(j + 1) * P],
                                                A("ident"))
                    m.then_inc(turned, 1)
                    u = new(("z3", HB * c + b))
                    pe.wait_ge(turn_read, gb + 1)
                    read(pe, ("v3", c, b // 2, 0))
                    read(pe, ("v3", c, b // 2, 1))
                    for j in range(4):
                        for hp in range(2):
                            for s in range(2):
                                m = mm(u[64 * hp:64 * hp + 64, (2 * j + s) * S:(2 * j + s + 1) * S],
                                       v3[64 * hp:64 * hp + 64, b, j * P + s * S:j * P + (s + 1) * S],
                                       pT[64 * hp:64 * hp + 64, gb % 2, j * P + s * S:j * P + (s + 1) * S])
                    m.then_inc(unit_full, 1)
                    if b % 2 == 1:
                        t = HT * c + b // 2
                        u = new(("o3", t))
                        read(pe, ("z3", HB * c + b))
                        for i in range(8):
                            m = mm(u[:, 0:P], zT[:, t % 2, i, :], w3o[:, i, :], i == 0, i == 7)
                        m.then_inc(unit_full, 1)

            ln_turn(12)
            pe.wait_ge(pad_ready, 1)
            for c in range(2):
                u = new(("pad", c))
                mm(u[:, :], Hc("ones", 1), padb[0:1, c * HALF:(c + 1) * HALF]).then_inc(unit_full, 1)
            project(("q", X3), Bc("wq3"), yT, wait_yT(12))
            project(("k", X3), Bc("wk3"), ctxT)
            to_tokens(("v", X3), Bc("wv3"), ctxT)

            def padding(bk, b):
                return mm(bk[:, :], Hc("ones", 3), spread(addm[0:3, b * S:(b + 1) * S], [[0, HH], [1, S]]), False, True)

            soft(X3, padding)
            to_tokens("o3x", Bc("wo3"), oT, wait_O(X3))

            for c in range(2):
                u = new(("xq", c))
                pe.wait_ge(quant_x, c + 1)
                for i in range(HT):
                    m = nc.tensor.transpose(u[:, i * P:(i + 1) * P], y[:, HT * c + i, :], A("ident"))
                m.then_inc(unit_full, 1)

            def gate_up3(t):
                k = NGU1 + NGU2 + t
                pe.wait_ge(hidden, k - 1)
                for h in range(2):
                    m = mm(score[2 * (k % 2) + h][:, :], xqT[:, t * P:(t + 1) * P], wf3q[:, h * F3:(h + 1) * F3])
                m.then_inc(gu_full, 1)

            pe.wait_ge(ternary, 3)
            for c in range(2):
                read(pe, ("xq", c))
            gate_up3(0)
            for t in range(TILES):
                if t + 1 < TILES:
                    gate_up3(t + 1)
                pe.wait_ge(quant_t, t + 1)
                pe.wait_ge(turn_read, 80 + t - 1)
                tb = ptb[t % 2][:, 0:256].bitcast(BF16)
                for f in range(4):
                    m = nc.tensor.transpose(tb[:, f * P:(f + 1) * P], hb[:, t % 2, f * P:(f + 1) * P], Hc("identb"))
                m.then_inc(turned, 1)
                u = new(("y3", t))
                pe.wait_ge(turn_read, 80 + t + 1)
                for f in range(4):
                    m = mm(u[:, 0:P], hqT[:, t % 2, f, :], wf3q[:, 2 * F3 + f * P:2 * F3 + (f + 1) * P],
                           f == 0, f == 3)
                m.then_inc(unit_full, 1)

        @block.vector
        def _(dve):
            v = nc.vector
            steps = [0]

            def link(ins):
                steps[0] += 1
                ins.then_inc(dve_step, 1)
                dve.wait_ge(dve_step, steps[0])

            def norm(L, src, eps, ready):
                for c in range(2):
                    t0 = HT * c
                    ready(c)
                    for t in range(t0, t0 + HT):
                        v.bn_stats(bst[:, t, :], src[:, t, :]).then_inc(ln_stat, 1)
                    for t in range(t0, t0 + HT):
                        dve.wait_ge(ln_stat, TILES * L + t + 1)
                        v.bn_aggr(mv[:, t, :], bst[:, t, :]).then_inc(ln_mv, 1)
                    dve.wait_ge(ln_mv, TILES * L + t0 + HT)
                    v.tensor_scalar(ve[:, t0:t0 + HT], mv[:, t0:t0 + HT, 1], eps, None, ALU.add).then_inc(ln_ve, 1)
                for c in range(2):
                    dve.wait_ge(ln_rstd, 2 * L + c + 1)
                    for t in range(HT * c, HT * c + HT):
                        v.tensor_scalar(y[:, t, :], src[:, t, :], mv[:, t, 0:1], rstd[:, t:t + 1],
                                        ALU.subtract, ALU.mult).then_inc(ln_y, 1)

            def after(name):
                return lambda c: read(dve, (name, c))

            def add_x(name, biased=0):
                for c in range(2):
                    key = (name, c)
                    full(dve, key)
                    if biased:
                        dve.wait_ge(x_biased, biased)
                    xs = x[:, HT * c:HT * (c + 1), :].rearrange("p t d -> p (t d)")
                    done(v.tensor_tensor(xs, bank(key)[:, :], xs, ALU.add), key)

            def spread_keys(a):
                for c in range(2):
                    read(dve, (("k", a), c))
                    for h in range(HH):
                        v.tensor_scalar(km[:, h, c * HALF:(c + 1) * HALF], kT[:, c * HALF:(c + 1) * HALF],
                                        A("hm")[:, h:h + 1], None, ALU.mult).then_inc(keys_spread, 1)

            def spread_values(a, c):
                key = (("v", a), c)
                full(dve, key)
                for o, i in value_parts(key, c):
                    last = v.tensor_copy(o, i)
                done(last, key)

            def softmax(a, lo, hi, tail=None, first=0):
                for i in range(lo, hi + 1):
                    if tail and i >= lo + 4:
                        tail(i - 4 - first)
                    g = g0[a] + i
                    s3 = score[g % 4][:, :].rearrange("p (h k) -> p h k", h=8)
                    if i < hi:
                        dve.wait_ge(sc_full, g + 1)
                        v.tensor_reduce(mx[:, g % 4, :], s3, AX.X, ALU.max).then_inc(row_max, 1)
                    if i > lo:
                        dve.wait_ge(exped, g)
                        v.tensor_reduce(sm[:, (g - 1) % 4, :], pr[:, (g - 1) % 4, :].rearrange("p (h k) -> p h k", h=8),
                                        AX.X, ALU.add).then_inc(row_sum, 1)
                    if i < hi:
                        dve.wait_ge(row_max, g + 1)
                        if g >= 4:
                            dve.wait_ge(turned, g - 3)
                        v.tensor_tensor(pr[:, g % 4, :].rearrange("p (h k) -> p h k", h=8), s3,
                                        spread(mx[:, g % 4, :], [[1, 8], [0, S]]), ALU.subtract).then_inc(shifted, 1)
                    if i > lo:
                        dve.wait_ge(row_sum, g)
                        v.reciprocal(rc[:, (g - 1) % 4, :], sm[:, (g - 1) % 4, :]).then_inc(row_rcp, 1)
                if tail:
                    for i in range(hi - 3, hi):
                        tail(i - first)

            def mark_two():
                link(v.tensor_copy(f8[:, :, :], i8[:, :, :]))
                for k in range(2):
                    it = spread(A("iota"), [[0, TILES], [1, E]])
                    ix = spread(f8[:, :, k:k + 1], [[E, TILES], [0, E]])
                    last = v.tensor_tensor(e8[:, k, :, :], it, ix, ALU.is_equal)
                    if k == 0:
                        link(last)
                return last

            def weigh(p1, p2):
                for k, p in enumerate((p1, p2)):
                    link(v.tensor_tensor(e8[:, k, :, :], e8[:, k, :, :], p, ALU.mult))
                link(v.tensor_tensor(gw[:, :, :], e8[:, 0, :, :], e8[:, 1, :, :], ALU.add))

            def best_two(src):
                for t in range(TILES):
                    last = v.max(m8[:, t, :], src[:, t, :])
                link(last)
                for t in range(TILES):
                    last = v.max_index(i8[:, t, :], m8[:, t, :], src[:, t, :])
                link(last)

            def experts(name, fn, base):
                nf = fn // P
                steps = [(e, c) for e in range(E) for c in range(2)]

                def hide(n):
                    e, c = steps[n]
                    for f in range(nf):
                        k = base + nf * n + f
                        dve.wait_ge(silued, k + 1)
                        if n >= 2:
                            full(dve, (name,) + steps[n - 2])
                        v.tensor_tensor(hid[:, n % 2, f, :], score[2 * (k % 2) + 1][:, :], sg[:, k % 2, :],
                                        ALU.mult).then_inc(hidden, 1)

                hide(0)
                for n, (e, c) in enumerate(steps):
                    if n + 1 < len(steps):
                        hide(n + 1)
                    key = (name, e, c)
                    full(dve, key)
                    if e:
                        read(dve, (name, e - 1, c))
                    for i in range(HT):
                        t = HT * c + i
                        last = v.scalar_tensor_tensor(x[:, t, :], bank(key)[:, i * P:(i + 1) * P], gw[:, t, e:e + 1],
                                                      x[:, t, :], ALU.mult, ALU.add)
                    done(last, key)

            dve.wait_ge(ld_x, 16)
            dve.wait_ge(ld_a, 16)
            norm(0, x, 1e-5, lambda c: None)
            dve.wait_ge(zeroed, 1)
            spread_keys(A0)
            spread_values(A0, 1)
            softmax(A0, 0, B)
            dve.wait_ge(ld_rel, 16)
            for i in range(3):
                link(v.tensor_copy(relh[:, i, :], rel[:, :]))
                if i < 2:
                    link(v.tensor_tensor(rel[:, :], rel[:, :], relh[:, i, :], ALU.subtract))
            v.sem_inc(bias_split, 1)
            add_x("o0")

            norm(1, x, 1e-5, after("o0"))
            spread_keys(X0)
            spread_values(X0, 1)
            softmax(X0, 0, B)
            dve.wait_ge(ld_pad, 16)
            link(v.tensor_copy(padb[0:1, :], pad8[0:1, :]))
            v.tensor_scalar(addm[0:3, :], pad8[0:3, :], 1.0, A("padc", 3), ALU.subtract, ALU.mult).then_inc(pad_ready, 1)
            dve.wait_ge(ld_wf3, 16)
            v.tensor_reduce(ws[:, 0, 0:3], wf3[:, :].rearrange("p (w n) -> p w n", w=3), AX.X, ALU.add,
                            apply_absolute_value=True).then_inc(abs_sum, 1)
            dve.wait_ge(ld_r, 16)
            add_x("o0x", 1)

            norm(2, x, 1e-5, after("o0x"))
            full(dve, "lo3")
            done(v.tensor_tensor(weff[:, :], bank("lo3")[:, 0:P], A("ffW"), ALU.add), "lo3")
            add_x("f0", 2)

            full(dve, "wsum")
            done(v.tensor_scalar(ws[:, 1, 0:3], bank("wsum")[:, 0:3], 1e-5, None, ALU.max), "wsum")
            read(dve, "wsum")
            link(v.reciprocal(ws[:, 2, 0:3], ws[:, 1, 0:3]))
            for w in range(3):
                wv = wf3[:, w * F3:(w + 1) * F3]
                link(v.tensor_scalar(wv, wv, ws[:, 2, w:w + 1], -1.0, ALU.mult, ALU.max))
                link(v.tensor_scalar(wv, wv, 1.0, ROUND, ALU.min, ALU.add))
                v.tensor_scalar(wf3q[:, w * F3:(w + 1) * F3], wv, ROUND, None, ALU.subtract).then_inc(ternary, 1)

            dve.wait_ge(ld_b, 16)
            dve.wait_ge(sig_exp, 2)
            link(v.tensor_scalar(ex1[:, :, :], ex1[:, :, :], 1.0, None, ALU.add))
            link(v.reciprocal(pq[:, 0:2, :], ex1[:, :, :]))
            link(v.tensor_tensor(pq[:, 2, :], pq[:, 0, :], pq[:, 1, :], ALU.mult))
            v.tensor_scalar(pq[:, 2, :], pq[:, 2, :], -1.0, 1.0, ALU.mult, ALU.add).then_inc(pq_done, 1)
            link(v.tensor_tensor(pq[:, 0, :], pq[:, 0, :], Bc("beta"), ALU.mult))
            link(v.scalar_tensor_tensor(pq[:, 0, :], pq[:, 0, :], 0.25, Bc("gamma"), ALU.mult, ALU.mult))
            dve.wait_ge(log_q, 1)
            v.tensor_tensor(kg[:, 0, :, :], spread(pq[:, 3, :], [[1, 16], [0, 16]]), spread(Bc("lgrid"), [[0, 16], [1, 16]]),
                            ALU.mult).then_inc(tap_arg, 1)
            dve.wait_ge(tap_exp, 1)
            link(v.tensor_tensor(kg[:, 1, :, :], kg[:, 0, :, :], spread(pq[:, 0, :], [[1, 16], [0, 16]]), ALU.mult))
            link(v.tensor_reduce(kl[:, 0:16], spread(kg[:, 1, :, :], [[1, 16], [16, 16]]), AX.X, ALU.add))
            link(v.tensor_tensor(kl[:, 0:1], kl[:, 0:1], Bc("omega"), ALU.add))

            norm(3, x, 1e-5, after("f0"))
            read(dve, ("yT", 3, 0))
            read(dve, ("yT", 3, 1))
            v.tensor_scalar(oT[:, :], yT[:, :], kl[:, 0:1], None, ALU.mult).then_inc(conv, 1)
            for l in range(1, B):
                dve.wait_ge(conv, l)
                v.scalar_tensor_tensor(oT[:, l * S:], yT[:, 0:T - l * S], kl[:, l:l + 1], oT[:, l * S:],
                                       ALU.mult, ALU.add).then_inc(conv, 1)
            add_x("cv")

            norm(4, x, 1e-5, after("cv"))

            def values(name, r):
                for c in range(2):
                    key = (name, c)
                    full(dve, key)
                    done(v.tensor_tensor(vt[:, HT * c:HT * (c + 1), :],
                                         bank(key)[:, :].rearrange("p (t d) -> p t d", t=HT),
                                         spread(row(r), [[0, HT], [1, D]]), ALU.add), key)

            values("v1", "bv1")
            for c in range(2):
                key = ("s1", c)
                full(dve, key)
                done(v.scalar_tensor_tensor(pr[:, c, :].rearrange("p (t q) -> p t q", t=HT),
                                            bank(key)[:, :].rearrange("p (t q) -> p t q", t=HT), 0.0,
                                            spread(Bc("blk"), [[0, HT], [1, P]]), ALU.max, ALU.mult), key)
            add_x("o1")

            norm(5, x, 1e-5, after("o1"))
            full(dve, "g1")
            done(v.tensor_copy(lg[:, :, :].rearrange("p t e -> p (t e)"), bank("g1")[:, 0:TILES * E]), "g1")
            read(dve, "g1")
            best_two(lg)
            v.tensor_tensor(g8[:, 0, :], m8[:, :, 1], m8[:, :, 0], ALU.subtract).then_inc(gate_arg, 1)
            link(mark_two())
            dve.wait_ge(gate_exp, 1)
            link(v.tensor_scalar(g8[:, 2, :], g8[:, 1, :], 1.0, None, ALU.add))
            link(v.reciprocal(g8[:, 2, :], g8[:, 2, :]))
            link(v.tensor_tensor(g8[:, 3, :], g8[:, 1, :], g8[:, 2, :], ALU.mult))
            weigh(spread(g8[:, 2, :], [[1, TILES], [0, E]]), spread(g8[:, 3, :], [[1, TILES], [0, E]]))
            experts("m1", F1, 0)

            norm(6, x, 1e-5, lambda c: read(dve, ("m1", E - 1, c)))
            norm(7, y, 1e-6, lambda c: dve.wait_ge(ln_y, TILES * 6 + HT * (c + 1)))
            spread_keys(A2)
            spread_values(A2, 1)
            softmax(A2, 0, B)
            add_x("o2")

            norm(8, x, 1e-5, after("o2"))
            values("v2", "bv2")
            for c in range(2):
                key = ("s2", c)
                full(dve, key)
                s3 = bank(key)[:, :].rearrange("p (t k) -> p t k", t=HT)
                link(v.tensor_reduce(mx[:, c, 0:HT], s3, AX.X, ALU.max))
                done(v.tensor_tensor(pr[:, c, :].rearrange("p (t k) -> p t k", t=HT), s3,
                                     spread(mx[:, c, 0:HT], [[1, HT], [0, P]]), ALU.subtract), key)
            for c in range(2):
                dve.wait_ge(small_a, c + 1)
                link(v.tensor_reduce(sm[:, c, 0:HT], pr[:, c, :].rearrange("p (t k) -> p t k", t=HT), AX.X, ALU.add))
                link(v.reciprocal(rc[:, c, 0:HT], sm[:, c, 0:HT]))
            for c in range(2):
                key = ("o2x", c)
                full(dve, key)
                for i in range(HT):
                    t = HT * c + i
                    last = v.scalar_tensor_tensor(x[:, t, :], bank(key)[:, i * P:(i + 1) * P], rc[:, c, i:i + 1],
                                                  x[:, t, :], ALU.mult, ALU.add)
                done(last, key)

            norm(9, x, 1e-5, after("o2x"))
            norm(10, y, 1e-5, lambda c: dve.wait_ge(ln_y, TILES * 9 + HT * (c + 1)))
            full(dve, "g2")
            done(v.tensor_scalar(lg[:, :, :].rearrange("p t e -> p (t e)"), bank("g2")[:, 0:TILES * E], 1e4, -1e4,
                                 ALU.min, ALU.max), "g2")
            read(dve, "g2")
            link(v.tensor_reduce(g8[:, 0, :], lg[:, :, :], AX.X, ALU.max))
            v.tensor_tensor(lg[:, :, :], lg[:, :, :], spread(g8[:, 0, :], [[1, TILES], [0, E]]), ALU.subtract)\
                .then_inc(gate_arg, 1)
            dve.wait_ge(gate_exp, 2)
            link(v.tensor_reduce(g8[:, 1, :], lg[:, :, :], AX.X, ALU.add))
            link(v.tensor_scalar(g8[:, 1, :], g8[:, 1, :], 1e-12, None, ALU.add))
            link(v.reciprocal(g8[:, 1, :], g8[:, 1, :]))
            link(v.tensor_tensor(lg[:, :, :], lg[:, :, :], spread(g8[:, 1, :], [[1, TILES], [0, E]]), ALU.mult))
            best_two(lg)
            link(mark_two())
            v.tensor_tensor(selb[:, :, :], e8[:, 0, :, :], e8[:, 1, :, :], ALU.add).then_inc(chosen, 1)
            weigh(spread(m8[:, :, 0:1], [[E, TILES], [0, E]]), spread(m8[:, :, 1:2], [[E, TILES], [0, E]]))
            full(dve, "rank")
            done(v.scalar_tensor_tensor(gw[:, :, :].rearrange("p t e -> p (t e)"), bank("rank")[:, 0:TILES * E],
                                        float(CAP), gw[:, :, :].rearrange("p t e -> p (t e)"), ALU.is_lt, ALU.mult), "rank")
            read(dve, "rank")
            experts("m2", F2, NGU1)

            norm(11, x, 1e-5, lambda c: read(dve, ("m2", E - 1, c)))
            for c in range(2):
                for w, (raw, sw) in enumerate(((qraw, qsw), (kraw, ksw))):
                    for i in range(8):
                        n = 16 * c + 8 * w + i
                        dve.wait_ge(swapped[n // 4 % 4], 64 * (c + 1))
                        r = raw[:, i, :].rearrange("p (b s) -> p b s", b=HB)
                        v.tensor_tensor(r, r, spread(Bc("cos"), [[0, HB], [1, S]]), ALU.mult).then_inc(rot_c, 1)
                        dve.wait_ge(rot_c, n + 1)
                        dve.wait_ge(rot_s, n + 1)
                        v.tensor_tensor(raw[:, i, :], raw[:, i, :], sw[:, i, :], ALU.add).then_inc(rot, 1)
                for i in range(HT):
                    key = ("v3", c, i, 1)
                    full(dve, key)
                    for o, src in value_parts3(key, i, 1):
                        last = v.tensor_copy(o, src)
                    done(last, key)

                def tail(b):
                    key = ("z3", HB * c + b)
                    full(dve, key)
                    t = HT * c + b // 2
                    if b % 2 == 0 and t >= 2:
                        full(dve, ("o3", t - 2))
                    done(v.tensor_tensor(zT[:, t % 2, :, (b % 2) * S:(b % 2 + 1) * S],
                                         bank(key)[:, :].rearrange("p (h q) -> p h q", h=8),
                                         spread(Bc("bV3"), [[1, 8], [0, S]]), ALU.add), key)
                    if b % 2 == 1:
                        key = ("o3", t)
                        full(dve, key)
                        dve.wait_ge(x_biased, 3)
                        done(v.tensor_tensor(x[:, t, :], bank(key)[:, 0:P], x[:, t, :], ALU.add), key)

                softmax(A3, HB * c, HB * (c + 1), tail, HB * c)

            norm(12, x, 1e-5, lambda c: [read(dve, ("o3", HT * c + i)) for i in range(HT)])
            for c in range(2):
                key = (("k", X3), c)
                full(dve, key)
                read(dve, ("pad", c))
                done(v.tensor_tensor(kT[:, c * HALF:(c + 1) * HALF], bank(key)[:, :], padB[:, c * HALF:(c + 1) * HALF],
                                     ALU.mult), key)
            spread_keys(X3)
            spread_values(X3, 1)
            softmax(X3, 0, B)
            add_x("o3x", 4)

            norm(13, x, 1e-5, after("o3x"))

            dve.wait_ge(ln_y, TILES * 14)
            link(v.tensor_reduce(q8[:, 0, :], y[:, :, :], AX.X, ALU.max, apply_absolute_value=True))
            link(v.tensor_scalar(q8[:, 0, :], q8[:, 0, :], 1e-5, None, ALU.max))
            link(v.reciprocal(q8[:, 3, :], q8[:, 0, :]))
            link(v.tensor_scalar(q8[:, 3, :], q8[:, 3, :], 127.0, None, ALU.mult))
            for w in range(2):
                link(v.tensor_scalar(q8[:, 1 + w, :], q8[:, 0, :], 1.0 / 127.0, ws[:, 1, w:w + 1], ALU.mult, ALU.mult))
            v.sem_inc(quant_arg, 1)
            for t in range(TILES):
                last = v.tensor_scalar(y[:, t, :], y[:, t, :], q8[:, 3, t:t + 1], -128.0, ALU.mult, ALU.max)
            link(last)
            for c in range(2):
                yc = y[:, HT * c:HT * (c + 1), :].rearrange("p t d -> p (t d)")
                link(v.tensor_scalar(yc, yc, 127.0, ROUND, ALU.min, ALU.add))
                v.tensor_scalar(yc, yc, ROUND, None, ALU.subtract).then_inc(quant_x, 1)

            def finish(t):
                key = ("y3", t)
                full(dve, key)
                done(v.scalar_tensor_tensor(x[:, t, :], bank(key)[:, 0:P], q8[:, 5, t:t + 1], x[:, t, :],
                                            ALU.mult, ALU.add), key)

            for t in range(TILES):
                k = NGU1 + NGU2 + t
                hv = pr[:, t % 2, :]
                dve.wait_ge(silued, k + 1)
                v.scalar_tensor_tensor(hv, score[2 * (k % 2) + 1][:, :], q8[:, 2, t:t + 1], sg[:, k % 2, :],
                                       ALU.mult, ALU.mult).then_inc(hidden, 1)
                dve.wait_ge(hidden, k + 1)
                link(v.tensor_reduce(q8[:, 4, t:t + 1], hv, AX.X, ALU.max, apply_absolute_value=True))
                link(v.tensor_scalar(q8[:, 4, t:t + 1], q8[:, 4, t:t + 1], 1e-5, None, ALU.max))
                link(v.tensor_scalar(q8[:, 5, t:t + 1], q8[:, 4, t:t + 1], 1.0 / 127.0, ws[:, 1, 2:3], ALU.mult, ALU.mult))
                link(v.reciprocal(q8[:, 4, t:t + 1], q8[:, 4, t:t + 1]))
                link(v.tensor_scalar(q8[:, 4, t:t + 1], q8[:, 4, t:t + 1], 127.0, None, ALU.mult))
                link(v.tensor_scalar(hv, hv, q8[:, 4, t:t + 1], -128.0, ALU.mult, ALU.max))
                link(v.tensor_scalar(hv, hv, 127.0, ROUND, ALU.min, ALU.add))
                if t >= 2:
                    dve.wait_ge(turned, 80 + t - 1)
                v.tensor_scalar(hb[:, t % 2, :], hv, ROUND, None, ALU.subtract).then_inc(quant_t, 1)
                if t >= 1:
                    finish(t - 1)
            finish(TILES - 1)

        @block.scalar
        def _(act):
            a_ = nc.scalar

            def turn(L, scale=None, bias=None):
                for c in range(2):
                    key = ("yT", L, c)
                    full(act, key)
                    dst = yT[:, c * HALF:(c + 1) * HALF]
                    if scale is None:
                        done(a_.activation(dst, bank(key)[:, :], ACT.Copy), key)
                    else:
                        done(a_.activation(dst, bank(key)[:, :], ACT.Identity, scale=scale, bias=bias), key)

            def copy_unit(key, dst, src=None, **kw):
                full(act, key)
                done(a_.activation(dst, bank(key)[:, :] if src is None else src, ACT.Copy, **kw), key)

            def queries(a, scale):
                for c in range(2):
                    key = (("q", a), c)
                    full(act, key)
                    for h in range(2):
                        r = slice(64 * h, 64 * h + 64)
                        last = a_.activation(qbd[r, HB * c:HB * (c + 1), r],
                                             bank(key)[r, :].rearrange("p (b q) -> p b q", b=HB), ACT.Copy, scale=scale)
                    done(last, key)

            def keys(a):
                for c in range(2):
                    copy_unit((("k", a), c), kT[:, c * HALF:(c + 1) * HALF])

            def values(a):
                key = (("v", a), 0)
                full(act, key)
                for o, i in value_parts(key, 0):
                    last = a_.activation(o, i, ACT.Copy)
                done(last, key)

            def exps(a, lo, hi, scale=1.0, out_heads=True):
                def turns(i):
                    g = g0[a] + i
                    act.wait_ge(turned, g + 1)
                    a_.activation(pT[:, g % 2, :], ptb[g % 2][:, :], ACT.Copy).then_inc(turn_read, 1)
                    if out_heads and i % 4 == 3:
                        key = (("O", a), i // 4)
                        full(act, key)
                        for h in range(2):
                            r = slice(64 * h, 64 * h + 64)
                            last = a_.activation(oT[r, (i - 3) * S:(i + 1) * S].rearrange("p (b q) -> p b q", b=4),
                                                 bank(key)[r, :].rearrange("p (b q) -> p b q", b=4)[:, :, r], ACT.Copy)
                        done(last, key)

                for i in range(lo, hi):
                    g = g0[a] + i
                    act.wait_ge(shifted, g + 1)
                    a_.activation(pr[:, g % 4, :], pr[:, g % 4, :], ACT.Exp, scale=scale).then_inc(exped, 1)
                    if i >= lo + 2:
                        turns(i - 2)
                turns(hi - 2)
                turns(hi - 1)

            def experts(fn, base, scales=None):
                for k in range(base, base + fn):
                    act.wait_ge(gu_full, k + 1)
                    if k >= base + 2:
                        act.wait_ge(hidden, k - 1)
                    a_.activation(sg[:, k % 2, :], score[2 * (k % 2)][:, :], ACT.Silu).then_inc(silued, 1)

            act.wait_ge(zeroed, 1)
            turn(0)
            for c in range(2):
                key = ("c0", c)
                full(act, key)
                done(a_.activation(oT[0:64, c * HALF:(c + 1) * HALF], bank(key)[0:64, :], ACT.Copy), key)
            queries(A0, DH ** -0.5)
            keys(A0)
            values(A0)
            exps(A0, 0, B)

            turn(1)
            queries(X0, DH ** -0.5)
            keys(X0)
            values(X0)
            exps(X0, 0, B)

            turn(2)
            copy_unit("lo1", a4[:, :], bank("lo1")[0:4, 0:P])
            copy_unit("lo2", a50[:, :], bank("lo2")[0:50, 0:P])

            act.wait_ge(ld_b, 16)
            a_.activation(ex1[:, 0, :], Bc("delta"), ACT.Exp, scale=-1.0).then_inc(sig_exp, 1)
            a_.activation(ex1[:, 1, :], Bc("alpha"), ACT.Exp, scale=-1.0).then_inc(sig_exp, 1)
            act.wait_ge(pq_done, 1)
            a_.activation(pq[:, 3, :], pq[:, 2, :], ACT.Ln).then_inc(log_q, 1)
            act.wait_ge(tap_arg, 1)
            a_.activation(kg[:, 0, :, :], kg[:, 0, :, :], ACT.Exp).then_inc(tap_exp, 1)
            turn(3)
            act.wait_ge(conv, B)
            a_.activation(oT[:, :], oT[:, :], ACT.Silu).then_inc(convact, 1)

            def one_headed(n):
                for nm, dst in (("q", qf), ("k", kT)):
                    for c in range(2):
                        key = (f"{nm}{n}", c)
                        full(act, key)
                        done(a_.activation(dst[:, c * HALF:(c + 1) * HALF], bank(key)[:, :], ACT.Identity,
                                           bias=Bc(f"b{nm}{n}")), key)

            turn(4)
            one_headed(1)
            turn(5)
            act.wait_ge(gate_arg, 1)
            a_.activation(g8[:, 1, :], g8[:, 0, :], ACT.Exp).then_inc(gate_exp, 1)
            experts(NGU1, 0)

            turn(7, Bc("lns2"), Bc("lnb2"))
            queries(A2, float(D) ** -0.5)
            keys(A2)
            values(A2)
            exps(A2, 0, B)

            turn(8)
            one_headed(2)
            for c in range(2):
                read(act, ("s2", c))
                a_.activation(pr[:, c, :], pr[:, c, :], ACT.Exp).then_inc(small_a, 1)
            for c in range(2):
                copy_unit(("p2", c), pT[:, c, :])
            turn(10, Bc("gam2"), Bc("bet2"))
            act.wait_ge(gate_arg, 2)
            a_.activation(lg[:, :, :], lg[:, :, :], ACT.Exp).then_inc(gate_exp, 1)
            experts(NGU2, NGU1)

            turn(11)
            for c in range(2):
                for w, (raw, bias) in enumerate(((qraw, "bQ3"), (kraw, "bK3"))):
                    for i in range(8):
                        key = ("qk3", c, w, i)
                        full(act, key)
                        done(a_.activation(raw[:, i, :], bank(key)[:, :], ACT.Identity, bias=Bc(bias)[:, i:i + 1]), key)
                for i in range(HT):
                    key = ("v3", c, i, 0)
                    full(act, key)
                    for o, src in value_parts3(key, i, 0):
                        last = a_.activation(o, src, ACT.Copy)
                    done(last, key)
                exps(A3, HB * c, HB * (c + 1), HD3 ** -0.5, False)

            turn(12)
            for c in range(2):
                copy_unit(("pad", c), padB[:, c * HALF:(c + 1) * HALF])
            queries(X3, DH ** -0.5)
            values(X3)
            exps(X3, 0, B)

            for c in range(2):
                copy_unit(("xq", c), xqT[:, c * HALF:(c + 1) * HALF])
            act.wait_ge(quant_arg, 1)

            def turns3(t):
                act.wait_ge(turned, 80 + t + 1)
                a_.activation(hqT[:, t % 2, :, :].rearrange("p c q -> p (c q)"), ptb[t % 2][:, 0:256].bitcast(BF16),
                              ACT.Copy).then_inc(turn_read, 1)

            for t in range(TILES):
                k = NGU1 + NGU2 + t
                act.wait_ge(gu_full, k + 1)
                act.wait_ge(hidden, k - 1)
                a_.activation(sg[:, k % 2, :], score[2 * (k % 2)][:, :], ACT.Silu, scale=q8[:, 1, t:t + 1])\
                    .then_inc(silued, 1)
                if t >= 1:
                    turns3(t - 1)
            turns3(TILES - 1)

        @block.gpsimd
        def _(pool):
            p_ = nc.gpsimd
            p_.memset(qbd[:, :, :], 0.0)
            p_.memset(vb[:, :, :], 0.0).then_inc(zeroed, 1)

            def rsqrt(L):
                for c in range(2):
                    pool.wait_ge(ln_ve, 2 * L + c + 1)
                    sl = slice(HT * c, HT * (c + 1))
                    p_.tensor_tensor(rstd[:, sl], ve[:, sl], A("mhalf"), ALU.pow).then_inc(ln_rstd, 1)

            def bias_x(L, name):
                pool.wait_ge(ln_y, TILES * (L + 1))
                p_.tensor_tensor(x[:, :, :], x[:, :, :], spread(row(name), [[0, TILES], [1, D]]), ALU.add)\
                    .then_inc(x_biased, 1)

            def probabilities(a, lo, hi):
                for i in range(lo, hi):
                    g = g0[a] + i
                    pool.wait_ge(row_rcp, g + 1)
                    p3 = pr[:, g % 4, :].rearrange("p (h k) -> p h k", h=8)
                    p_.tensor_tensor(p3, p3, spread(rc[:, g % 4, :], [[1, 8], [0, S]]), ALU.mult).then_inc(normed, 1)

            pool.wait_ge(ld_a, 16)
            rsqrt(0)
            probabilities(A0, 0, B)
            rsqrt(1)
            pool.wait_ge(ld_r, 16)
            bias_x(1, "fcb")
            probabilities(X0, 0, B)
            rsqrt(2)
            bias_x(2, "ffb")
            for L in range(3, 8):
                rsqrt(L)
            probabilities(A2, 0, B)
            for c in range(2):
                read(pool, (("O", A2), 2 * c))
                read(pool, (("O", A2), 2 * c + 1))
                sl = slice(c * HALF, (c + 1) * HALF)
                p_.tensor_tensor(oT[:, sl], oT[:, sl], yT[:, sl], ALU.add).then_inc(added, 1)
            for L in range(8, 12):
                rsqrt(L)
            bias_x(11, "bO3")
            for c in range(2):
                for w, sw in enumerate((qsw, ksw)):
                    for i in range(8):
                        n = 16 * c + 8 * w + i
                        pool.wait_ge(swapped[n // 4 % 4], 64 * (c + 1))
                        r = sw[:, i, :].rearrange("p (b s) -> p b s", b=HB)
                        p_.tensor_tensor(r, r, spread(Bc("sin"), [[0, HB], [1, S]]), ALU.mult).then_inc(rot_s, 1)
                probabilities(A3, HB * c, HB * (c + 1))
            rsqrt(12)
            bias_x(12, "bo3")
            probabilities(X3, 0, B)
            rsqrt(13)

        @block.sync
        def _(sp):
            xv = x_in.rearrange("(t p) d -> p t d", p=P)
            sp.dma_start(x[:, :, :], xv).then_inc(ld_x, 16)
            sp.dma_start(sA[:, :], packA).then_inc(ld_a, 16)
            sp.dma_start(sH[:, :], packH).then_inc(ld_h, 16)
            sp.dma_start(ctxT[:, :], ctxT_in).then_inc(ld_ctx, 16)
            sp.dma_start(rel[:, :], relb).then_inc(ld_rel, 16)
            sp.dma_start(sR[:, :], spread_rows(rows)).then_inc(ld_r, 16)
            sp.dma_start(wf3[:, :], wf3_in).then_inc(ld_wf3, 16)
            sp.dma_start(sB[:, :], packB).then_inc(ld_b, 16)
            sp.dma_start(pad8[0:3, :], spread_rows(pad_in, 3)).then_inc(ld_pad, 16)
            sp.dma_start(w2, w2_in).then_inc(ld_w2, 16)
            sp.dma_start(w23, w23_in).then_inc(ld_w2, 16)
            sp.wait_ge(ternary, 3)
            sp.wait_ge(bias_split, 1)
            sp.dma_start(w1, w1_in).then_inc(ld_w1, 16)
            sp.dma_start(w13, w13_in).then_inc(ld_w1, 16)
            full(sp, ("m1", E - 1, 1))
            sp.dma_start(w3qkv, w3qkv_in).then_inc(ld_w3a, 16)
            sp.dma_start(w3o, w3o_in).then_inc(ld_w3a, 16)
            full(sp, ("m2", E - 1, 1))
            for c in range(2):
                for w, (raw, sw) in enumerate(((qraw, qsw), (kraw, ksw))):
                    for k in range(2):
                        read(sp, ("qk3", c, w, 4 * k + 2))
                        read(sp, ("qk3", c, w, 4 * k + 3))
                        if c == 1 and w == 0 and k == 0:
                            sp.wait_ge(rot, 16)
                        for qd in range(4):
                            o, i = 32 * qd, 32 * (qd ^ 1)
                            sp.dma_start(sw[o:o + 32, 4 * k:4 * k + 4, :], raw[i:i + 32, 4 * k:4 * k + 4, :])\
                                .then_inc(swapped[2 * w + k], 16)
            for c in range(2):
                for t in range(HT * c, HT * (c + 1)):
                    read(sp, ("y3", t))
                sp.dma_start(out.rearrange("(t p) d -> p t d", p=P)[:, HT * c:HT * (c + 1), :],
                             x[:, HT * c:HT * (c + 1), :]).then_inc(stored, 16)
            sp.wait_ge(stored, 32)


def spread_rows(ap, n=P):
    return bass.AP(ap.tensor, ap.offset, [[0, n], [1, ap.shape[-1]]])


def kernel(**inputs):
    import ml_dtypes
    import concourse.bacc as _bacc
    from concourse.bass_utils import run_bass_kernel_spmd as _run

    I = {k: np.asarray(v) for k, v in inputs.items()}
    f32 = np.float32

    def pack(cols, parts, dt=f32):
        out = np.zeros((P, sum(n for _, n in cols)), dt)
        o = 0
        for name, n in cols:
            r0, a = parts[name]
            a = a.reshape(a.shape[0], -1)
            out[r0:r0 + a.shape[0], o:o + n] = a
            o += n
        return out

    def col(name):
        return (0, I[name].reshape(D, 1))

    f = np.arange(P)
    hm = ((f[:, None] % 64) // DH == np.arange(HH)[None, :]).astype(f32)
    bf = ml_dtypes.bfloat16
    n1 = bf(NEG)
    n2 = bf(NEG - float(n1))
    n3 = bf(NEG - float(n1) - float(n2))
    padc = np.array([[float(n1)], [float(n2)], [float(n3)]], f32)
    A_ = dict(
        ident=(0, np.eye(P, dtype=f32)), dqkv=(0, np.concatenate([I["L0_attn_W_dq"], I["L0_attn_W_dkv"]], 1)),
        uq=(0, I["L0_attn_W_uq"]), uk=(32, I["L0_attn_W_uk"]), uv=(32, I["L0_attn_W_uv"]), wo0=(0, I["L0_attn_W_o"]),
        wq0=(0, I["L0_xattn_wq"].T), wk0=(0, I["L0_xattn_wk"].T), wv0=(0, I["L0_xattn_wv"].T), fc0=(0, I["L0_xattn_fc_w"].T),
        ffW=(0, I["L0_ffn_W"].T), lordT=(0, I["L0_ffn_lora_down"].T), dauxT=(0, I["L0_ffn_down_aux"]),
        loruT=(0, I["L0_ffn_lora_up"].T), uauxT=(0, I["L0_ffn_up_aux"].T),
        hm=(0, hm), mhalf=(0, np.full((P, 4), -0.5, f32)), iota=(0, np.tile(np.arange(E, dtype=f32), (P, 1))),
        padc=(0, padc), mean=(0, np.full((P, P), 1.0 / (D * F3), f32)))
    pos = np.arange(S, dtype=f32)
    dim = np.arange(HD3 // 2, dtype=f32)
    freq = (f32(10000.0) ** (dim / f32(HD3 // 2))).astype(f32)
    ang = (pos[None, :] / np.concatenate([freq, freq])[:, None]).astype(f32)
    sign = np.where(np.arange(HD3) < HD3 // 2, -1.0, 1.0).astype(f32)[:, None]
    by_output = lambda w: w.reshape(4, 2, 2, HD3, -1).transpose(1, 3, 0, 2, 4)
    heads = lambda n: (0, I[n].reshape(8, P).T)
    B_ = dict(
        delta=(0, I["L1_attn_delta"]), alpha=(0, I["L1_attn_alpha"]), beta=(0, I["L1_attn_beta"]),
        gamma=(0, I["L1_attn_gamma"]), omega=col("L1_attn_omega"),
        wq1=(0, I["L1_xattn_Wq"].T), wk1=(0, I["L1_xattn_Wk"].T), wv1=(0, I["L1_xattn_Wv"].T),
        bq1=col("L1_xattn_bq"), bk1=col("L1_xattn_bk"), wg1=(0, I["L1_ffn_Wg"].T),
        blk=(0, (f[:, None] // S == f[None, :] // S).astype(f32)),
        wqa2=(0, I["L2_attn_wq"]), wka2=(0, I["L2_attn_wk"]), wva2=(0, I["L2_attn_wv"]),
        lns2=col("L2_attn_ln_scale"), lnb2=col("L2_attn_ln_bias"),
        wq2=(0, I["L2_xattn_Wq"].T), wk2=(0, I["L2_xattn_Wk"].T), wv2=(0, I["L2_xattn_Wv"].T),
        bq2=col("L2_xattn_bq"), bk2=col("L2_xattn_bk"), gam2=col("L2_ffn_ln_gamma"), bet2=col("L2_ffn_ln_beta"),
        wr2=(0, I["L2_ffn_Wr"].T),
        wq3=(0, I["L3_xattn_Wq"].T), wk3=(0, I["L3_xattn_Wk"].T), wv3=(0, I["L3_xattn_Wv"].T), wo3=(0, I["L3_xattn_Wo"].T),
        bQ3=heads("L3_attn_b_Q"), bK3=heads("L3_attn_b_K"), bV3=(0, by_output(I["L3_attn_b_V"]).reshape(P, 8)),
        cos=(0, np.tile(np.cos(ang), (2, 1)).astype(f32)), sin=(0, np.tile(np.sin(ang) * sign, (2, 1)).astype(f32)),
        lgrid=(0, np.tile(np.arange(16, dtype=f32), (P, 1))))
    q, k = f[:, None] % S, np.arange(S)[None, :]
    H_ = dict(
        identb=(0, np.eye(P, dtype=bf)), causal=(0, np.where(k <= q, 0.0, -BIG).astype(bf)),
        offblk=(0, np.where(f[:, None] // S == f[None, :] // S, 0.0, -BIG).astype(bf)),
        before=(0, (f[:, None] < f[None, :]).astype(bf)), ones=(0, np.ones((P, P), bf)))
    table = I["L0_xattn_rel_table"]
    relq = np.stack([table[255 - i:255 - i + S] for i in range(S)])
    relq = relq.transpose(0, 2, 1).reshape(S, 2, HH * S).transpose(1, 0, 2).reshape(P, HH * S)
    rows = np.concatenate([I[n].reshape(1, -1) for n in (
        "L0_xattn_fc_b", "L0_ffn_b", "L1_xattn_bv", "L2_xattn_bv", "L3_attn_b_O", "L3_xattn_bo")], 1)

    def inner(w):
        return w.transpose(2, 0, 1)

    def outer(w):
        e, d, n = w.shape
        return w.transpose(2, 0, 1).reshape(n // P, P, e, d).transpose(1, 2, 0, 3)

    feeds = dict(
        x=I["x"].reshape(T, D), ctxT=I["ctx_1024"].reshape(T, D).T, pad=I["mask_BxS2_bf1"].reshape(1, T).view(np.uint8),
        packA=pack(COLS_A, A_), packB=pack(COLS_B, B_), packH=pack(COLS_H, H_, bf), rows=rows, relb=relq,
        w1=np.concatenate([inner(I["L1_ffn_W1"]), inner(I["L1_ffn_W2"])], 2), w13=outer(I["L1_ffn_W3"]),
        w2=inner(I["L2_ffn_W12"]), w23=outer(I["L2_ffn_W3"]),
        w3qkv=np.stack([I[f"L3_attn_W_{n}"].transpose(1, 0, 2).reshape(D, 1024) for n in "QKV"], 1),
        w3o=by_output(I["L3_attn_W_O"]).reshape(P, 8, D),
        wf3=np.concatenate([I["L3_ffn_w_gate"].T, I["L3_ffn_w_up"].T,
                            I["L3_ffn_w_down"].T.reshape(4, P, D).transpose(1, 0, 2).reshape(P, F3)], 1))
    nc = _bacc.Bacc("TRN2", target_bir_lowering=False, num_devices=1)
    arrays, args = {}, []
    for name, a in feeds.items():
        a = np.ascontiguousarray(a)
        arrays[f"in_{name}"] = a
        args.append(nc.dram_tensor(f"in_{name}", a.shape, mybir.dt.from_np(a.dtype), kind="ExternalInput").ap())
    out = nc.dram_tensor("out_x", (T, D), F32, kind="ExternalOutput").ap()
    bass_decoder_kernel(nc, *args, out)
    r = _run(nc, [arrays], core_ids=[0])
    return r.results[0]["out_x"].reshape(B, S, D)
```

```python
from contextlib import ExitStack

import numpy as np

import concourse.bass as bass
from concourse import mybir

F32 = mybir.dt.float32
F32R = mybir.dt.float32r
BF16 = mybir.dt.bfloat16
I32 = mybir.dt.int32
U32 = mybir.dt.uint32
U8 = mybir.dt.uint8
ALU = mybir.AluOpType
ACT = mybir.ActivationFunctionType
AX = mybir.AxisListType

P = 128
D = 128
B, S = 16, 64
T = B * S
TILES = T // P
HALF = T // 2
HT = TILES // 2
HB = B // 2
HEADS, DH = 16, 8
HH = HEADS // 2
E = 8
F1, F2 = 256, 512
F3 = 512
HD3 = 64
CAP = -(-(-(-T * 2 * 5 // 4)) // E)
BIG = 1e30
NEG = 1e10
ROUND = 12582912.0

A0, X0, A2, A3, X3 = range(5)

COLS_A = [("ident", 128), ("dqkv", 64), ("uq", 128), ("uk", 128), ("uv", 128), ("wo0", 128),
          ("wq0", 128), ("wk0", 128), ("wv0", 128), ("fc0", 128),
          ("ffW", 128), ("lordT", 4), ("dauxT", 128), ("loruT", 50), ("uauxT", 128),
          ("hm", 8), ("iota", 8), ("padc", 1), ("mean", 128)]
COLS_B = [("delta", 16), ("alpha", 16), ("beta", 16), ("gamma", 16), ("omega", 1),
          ("wq1", 128), ("wk1", 128), ("wv1", 128), ("bq1", 1), ("bk1", 1), ("wg1", 8), ("blk", 128),
          ("wqa2", 128), ("wka2", 128), ("wva2", 128), ("lns2", 1), ("lnb2", 1),
          ("wq2", 128), ("wk2", 128), ("wv2", 128), ("bq2", 1), ("bk2", 1),
          ("gam2", 1), ("bet2", 1), ("wr2", 8),
          ("wq3", 128), ("wk3", 128), ("wv3", 128), ("wo3", 128),
          ("bQ3", 8), ("bK3", 8), ("bV3", 8), ("cos", 64), ("sin", 64), ("lgrid", 16)]
COLS_H = [("identb", 128), ("causal", 64), ("offblk", 128), ("before", 128), ("ones", 128)]
ROWS = [("fcb", 128), ("ffb", 128), ("bv1", 128), ("bv2", 128), ("bO3", 128), ("bo3", 128)]


def offsets(cols):
    at, out = 0, {}
    for name, n in cols:
        out[name] = (at, n)
        at += n
    return out, at


OFF_A, N_A = offsets(COLS_A)
OFF_B, N_B = offsets(COLS_B)
OFF_H, N_H = offsets(COLS_H)
OFF_R, N_R = offsets(ROWS)


def spread(ap, dims):
    return bass.AP(ap.tensor, ap.offset, [list(ap.ap[0])] + [list(d) for d in dims])



SLOTS = 4
Q = 4
QB = B // Q
QN = T // Q
NF = {1: F1 // P, 2: F2 // P}

AFTER = {1: ("o", A0), 2: ("o", X0), 3: ("f0",), 4: ("cv",), 5: ("o1", 1), 8: ("o2",), 9: ("o1", 2), 13: ("o", X3)}
EPS = {7: 1e-6}
FROM_Y = (7, 10)


CUT1, CUT2 = 12, 6
PLACES = {
    "A0 input, half 1": [0, 1],
    "A0 queries keys values, half 1": [2, 3, 4],
    "taps, bias, low rank": [4, 4, 6, 7],
    "M1 first weights": [9],
    "X0 keys 0": [7, 8],
    "A0 output, X0 queries 0": [10, 11, 12, 13, 14],
    "X0 values 0": [11],
    "X0 keys 1": [14, 16],
    "A0 output, X0 queries 1": [18, 20, 21, 22, 23],
    "X0 values 1": [19],
    "small L0 L1, half 0": [26, 27, 28, 29, 30, 31, 31, 32, 33, 34, 35, 36, 39, 39, 40, 41, 42, 43, 44, 45, 45],
    "M1 first splits": [30, 31, 33],
    "small L0 L1, half 1 begins": [34, 35, 36, 37, 39, 40, 41, 42, 43, 44, 45, 46],
    "M1 gates, half 0": [1],
    "small L0 L1, half 1 goes on": [3, 4, 5, 6, 7, 8, 10, 10, 11, 12, 13],
    "padding mask": [5],
    "M1 gates, half 1": [1],
    "A2 input, half 0": [3, 4, 5, 6, 7, 8, 9, 10],
    "A2 input, half 1": [0, 1, 2, 3, 4, 5, 6, 7],
    "small L2, half 0": [10, 11, 12, 13, 14, 15, 16, 17, 18, 19, 20, 21, 22, 23],
    "M2 first splits": [14, 19, 19],
    "small L2, half 1 begins": [18, 19, 20, 21, 23, 24],
    "M2 gates, half 0": [1, 4, 4],
    "small L2, half 1 goes on": [3, 4, 5, 6, 7, 7, 9, 10],
    "L3 constants": [7, 8, 10, 10, 11, 12],
    "M2 gates, half 1": [1, 2, 3],
    "A3 norm, half 0": [3, 4, 5, 6],
    "A3 input, quarter 0": [8, 8, 9, 9, 9, 9, 10, 10, 10, 11, 11, 12, 12, 12],
    "A3 input, quarter 1": [16, 16, 17, 17, 17, 17, 18, 18, 18, 19, 19, 19, 20, 20],
    "A3 norm, half 1": [0, 1, 2, 5],
    "key mask": [1],
    "A3 input, quarter 2": [3, 3, 4, 4, 4, 4, 5, 5, 5, 6, 6, 7, 7, 7],
    "A3 input, quarter 3": [7, 7, 7, 7, 7, 7, 8, 8, 8, 9, 9, 10, 10, 10],
    "X3 clear values 0": [9, 11],
    "A3 output, X3 input, half 0": [11, 12, 13, 14, 15, 16],
    "X3 clear values 1": [13, 14],
    "A3 output, X3 input, half 1": [19, 20, 21, 22, 23, 24],
    "last norm, half 0": [26, 27, 28, 29, 31],
    "last gates 0": [32],
    "last norm, half 1": [34, 34],
    "last pair 2": [36],
    "last pair 3": [37],
    "last pair 4": [38],
    "last sums": [39],
}


def make_schedule():
    out = []

    def ln(L, c, turn=True):
        return [[("stats", L, c)], [("apply", L, c)]] + ([[("lnT", L, c)]] if turn else [])

    def place(fills, name, chain):
        at = PLACES[name]
        assert len(at) == len(chain), name
        for n, group in zip(at, chain):
            fills.setdefault(n, []).extend(group)

    def attend(items, fills):
        n = 0
        while n < len(items) + 3 or n <= max(fills, default=0):
            if 0 <= n - 3 < len(items):
                out.append(("turn",) + items[n - 3])
            if n < len(items):
                out.append(("S",) + items[n])
            cur = items[n - 1] if 1 <= n <= len(items) else None
            prev = items[n - 2] if 2 <= n <= len(items) + 1 else None
            if cur or prev:
                out.append(("soft", cur, prev))
            if 0 <= n - 3 < len(items):
                a, b = items[n - 3]
                out.append(("val", a, b))
            if 0 <= n - 4 < len(items) and items[n - 4][0] == A3 and n % 2 == 1:
                out.append(("o3", items[n - 4][1] // 2))
            out.extend(fills.get(n, []))
            n += 1

    def experts(m, c, fills):
        n, end = 0, E * NF[m]
        while n <= end + 1 or n <= max(fills, default=0):
            if n < end:
                out.append(("GU", m, c, n))
                if n % NF[m] == 0 and n + E * NF[m] * c > 0 and E * c + n // NF[m] + 1 < 2 * E:
                    out.append(("split", m, E * c + n // NF[m] + 1))
            out.extend(fills.get(n, []))
            if 2 <= n <= end + 1:
                out.append(("DN", m, c, n - 2))
                if (n - 1) % NF[m] == 0 and E * c + (n - 2) // NF[m] + SLOTS < 2 * E:
                    out.append(("load", m, E * c + (n - 2) // NF[m] + SLOTS))
            n += 1

    def project(a, c):
        return [[("q", a, c), ("k", a, c)], [("spread", a, c)], [("v", a, c)]]

    def small1(c):
        return ([[("o", X0, c)]] + ln(2, c) + [[("bias", 2, c), ("f0", c)]] + ln(3, c)
                + [[("conv", c, i)] for i in range(2 * (c + 1))] + [[("cv", c)]]
                + ln(4, c) + [[("qkv1", 1, c)], [("s1", c)], [("o1", 1, c)]] + ln(5, c) + [[("ysplit", 1, c)]])

    def small2(c):
        return ([[("o2", c)]] + ln(8, c) + [[("qkv1", 2, c)], [("s2", c)], [("p2", c)], [("o1", 2, c)]]
                + ln(9, c, False) + ln(10, c) + [[("ysplit", 2, c)]])

    def queries3(G):
        q = lambda w, i: ("qk3", G, w, i)
        rotate, rope, swap = (lambda w, h, kind=kind: (kind, G, w, h) for kind in ("rotate", "rope", "swap"))
        return [[q(0, 0), q(0, 2), swap(0, 0)], [q(0, 4)],
                [q(0, 6), swap(0, 1)], [rotate(0, 0)], [q(1, 0)], [q(1, 2), swap(1, 0)],
                [rotate(0, 1), rope(0, 0)], [q(1, 4)], [q(1, 6), swap(1, 1)],
                [rotate(1, 0), rope(0, 1)], [("v3", G, 0)],
                [rotate(1, 1), rope(1, 0)], [("v3", G, 1)], [rope(1, 1)]]

    for group in ln(0, 0) + [[("stats", 0, 1)], [("c0", 0)], [("q", A0, 0), ("k", A0, 0)], [("apply", 0, 1)],
                             [("spread", A0, 0)], [("v", A0, 0)]]:
        out.extend(group)
    fills = {}
    place(fills, "A0 input, half 1", [[("lnT", 0, 1)], [("c0", 1)]])
    place(fills, "A0 queries keys values, half 1", project(A0, 1))
    out.extend(("load", 2, k) for k in range(SLOTS))
    place(fills, "taps, bias, low rank", [[("lora",)], [("taps", 0), ("split_rel", 0)], [("taps", 1), ("split_rel", 1)], [("taps", 2)]])
    place(fills, "M1 first weights", [[("load", 1, k) for k in range(SLOTS)]])
    for c in range(2):
        n = 8 * c
        place(fills, f"X0 keys {c}", [[("k", X0, c)], [("spread", X0, c)]])
        place(fills, f"A0 output, X0 queries {c}", [[("o", A0, c)], *ln(1, c), [("bias", 1, c), ("q", X0, c)]])
        place(fills, f"X0 values {c}", [[("v", X0, c)]])
    place(fills, "small L0 L1, half 0", small1(0))
    place(fills, "M1 first splits", [[("split", 1, 0)], [], [("split", 1, 1)]])
    place(fills, "small L0 L1, half 1 begins", small1(1)[:CUT1])
    attend([(A0, b) for b in range(B)] + [(X0, b) for b in range(B)], fills)
    fills = {}
    place(fills, "M1 gates, half 0", [[("gate", 1, 0)]])
    place(fills, "small L0 L1, half 1 goes on", small1(1)[CUT1:])
    place(fills, "padding mask", [[("pad_setup",)]])
    experts(1, 0, fills)
    fills = {}
    place(fills, "M1 gates, half 1", [[("gate", 1, 1)]])
    place(fills, "A2 input, half 0", ln(6, 0, False) + ln(7, 0) + project(A2, 0))
    experts(1, 1, fills)
    fills = {}
    place(fills, "A2 input, half 1", ln(6, 1, False) + ln(7, 1) + project(A2, 1))
    place(fills, "small L2, half 0", small2(0))
    place(fills, "M2 first splits", [[("split", 2, 0)], [], [("split", 2, 1)]])
    place(fills, "small L2, half 1 begins", small2(1)[:CUT2])
    attend([(A2, b) for b in range(B)], fills)
    fills = {}
    place(fills, "M2 gates, half 0", [[("gate", 2, 0)], [], [("rank", 0)]])
    place(fills, "small L2, half 1 goes on", small2(1)[CUT2:])
    place(fills, "L3 constants", [[("bvo",)], [("abs3",)], [("wsum",)], [("ternary", 0)], [("ternary", 1)], [("ternary", 2)]])
    experts(2, 0, fills)
    fills = {}
    place(fills, "M2 gates, half 1", [[("gate", 2, 1)], [], [("rank", 1)]])
    place(fills, "A3 norm, half 0", ln(11, 0) + [[("bias", 11, 0)]])
    for G in range(2):
        place(fills, f"A3 input, quarter {G}", queries3(G))
    experts(2, 1, fills)
    fills = {}
    place(fills, "A3 norm, half 1", ln(11, 1) + [[("bias", 11, 1)]])
    place(fills, "key mask", [[("pad",)]])
    place(fills, "A3 input, quarter 2", queries3(2))
    place(fills, "A3 input, quarter 3", queries3(3))
    for c in range(2):
        n = 8 * c
        place(fills, f"X3 clear values {c}", [[("zero_v", c, 0)], [("zero_v", c, 1)]])
        place(fills, f"A3 output, X3 input, half {c}", [*ln(12, c), [("bias", 12, c), ("k", X3, c)], [("q", X3, c), ("spread", X3, c)], [("v", X3, c)]])
    place(fills, "last norm, half 0", [[("o", X3, 0)], *ln(13, 0, False), [("quant", 0)], [("xq", 0)]])
    gate_up3 = lambda p: [("gu3", 2 * p), ("gu3", 2 * p + 1)]
    turn3 = lambda p: [("turn3", 2 * p), ("turn3", 2 * p + 1)]
    down3 = lambda p: [("down3", 2 * p), ("down3", 2 * p + 1)]
    place(fills, "last gates 0", [gate_up3(0)])
    place(fills, "last norm, half 1", [[("o", X3, 1), ("stats", 13, 1), ("hid3", 0)],
                             [("apply", 13, 1), *gate_up3(1), ("scale3", 0), ("quant", 1), ("clip3", 0), ("hid3", 1),
                              ("round3", 0), ("xq", 1)]])
    for p in range(2, 5):
        place(fills, f"last pair {p}", [[*(gate_up3(p) if p < 4 else []), *turn3(p - 2), ("scale3", p - 1), *down3(p - 2),
                                          *([("hid3", p)] if p < 4 else []), ("clip3", p - 1), ("round3", p - 1),
                                          ("add3", p - 2)]])
    place(fills, "last sums", [turn3(3) + down3(3) + [("add3", 3)]])
    attend([(A3, b) for b in range(B)] + [(X3, b) for b in range(B)], fills)
    return out


SCHEDULE = make_schedule()
_seen, NTH = {}, {}
for _step in SCHEDULE:
    assert _step not in NTH, _step
    NTH[_step] = _seen.get(_step[0], 0)
    _seen[_step[0]] = NTH[_step] + 1


def nth(*step):
    return NTH[step]


def bass_decoder_kernel(nc, x_in, ctxT_in, pad_in, packA, packB, packH, rows, relb, w1_in, w2_in,
                        w3qkv_in, w3o_in, wf3_in, out):
    with ExitStack() as ctx:
        def sb(name, shape, dt=F32):
            return ctx.enter_context(nc.sbuf_tensor(name, shape, dt))

        def ps(name):
            return ctx.enter_context(nc.psum_tensor(name, [P, 512], F32))

        def sem(name):
            return ctx.enter_context(nc.semaphore(name))

        sA = sb("sA", [P, N_A])
        sB = sb("sB", [P, N_B])
        sH = sb("sH", [P, N_H], BF16)
        sR = sb("sR", [P, N_R])

        def A(name, p=P):
            o, n = OFF_A[name]
            return sA[0:p, o:o + n]

        def Bc(name):
            o, n = OFF_B[name]
            return sB[:, o:o + n]

        def Hc(name, p=P):
            o, n = OFF_H[name]
            return sH[0:p, o:o + n]

        def row(name):
            o, n = OFF_R[name]
            return sR[:, o:o + n]

        moe1 = sb("moe1", [P, E * (2 * F1 + F1)])
        w3qkv = moe1[:, 0:3 * 1024].rearrange("p (w n) -> p w n", w=3)
        w3o = moe1[:, 3 * 1024:4 * 1024].rearrange("p (c d) -> p c d", c=8)
        zT = moe1[:, 4 * 1024:6 * 1024].rearrange("p (r c q) -> p r c q", r=2, c=8)
        moe2 = sb("moe2", [P, SLOTS * (2 * F2 + F2)])
        wf3q = sb("wf3q", [P, 3 * F3], BF16)
        rel = moe1[:, 0:512]
        relh = sb("relh", [P, 4, 512], BF16)

        x = sb("x", [P, TILES, D])
        y = sb("y", [P, TILES, D])
        yT = sb("yT", [P, T])
        ctxT = sb("ctxT", [P, T])
        slots = {m: mo[:, 0:SLOTS * 3 * NF[m] * P].rearrange("p (s n) -> p s n", s=SLOTS) for m, mo in ((1, moe1), (2, moe2))}
        wraw = {m: slots[m][:, :, 0:2 * NF[m] * P] for m in (1, 2)}
        wdn = {m: slots[m][:, :, 2 * NF[m] * P:3 * NF[m] * P].rearrange("p s (c d) -> p s c d", d=D) for m in (1, 2)}
        parts = sb("parts", [P, 6144], F32R)
        yhi, ylo = parts[:, 0:T], parts[:, T:2 * T]
        wparts = parts[:, 2 * T:].rearrange("p (s n) -> p s n", s=2)
        whi = {m: wparts[:, :, 0:2 * NF[m] * P] for m in (1, 2)}
        wlo = {m: wparts[:, :, F2 * 2:F2 * 2 + 2 * NF[m] * P] for m in (1, 2)}
        kT = y[:, :, :].rearrange("p t d -> p (t d)")
        oT = sb("oT", [P, T])
        qbd = sb("qbd", [P, B, P])
        km = sb("km", [P, HH, T])
        vb = sb("vb", [P, B, 512])
        pr = sb("pr", [P, 4, 512])
        pT = sb("pT", [P, 2, 512])
        qf, p1, p1T, ycv = km[:, 0, :], km[:, 1, :], km[:, 2, :], km[:, 3, :]
        sg = pT
        qraw = [km[:, :, 512 * (G % 2):512 * (G % 2) + QN] for G in range(4)]
        kraw = [km[:, :, 512 * (G % 2) + QN:512 * (G % 2) + 2 * QN] for G in range(4)]
        v3 = ([vb[:, QB * G:QB * (G + 1), :] for G in range(2)]
              + [moe2[:, 2048 + 2048 * G:4096 + 2048 * G].rearrange("p (b n) -> p b n", b=QB) for G in range(2)])
        swv = vb[:, HB:B, :].rearrange("p b n -> p (b n)").rearrange("p (w c q) -> p w c q", w=2, c=8)
        swaps = [swv] * 4
        vt = oT[:, :].rearrange("p (t d) -> p t d", t=TILES)

        bst = sb("bst", [P, TILES, 6])
        mv = sb("mv", [P, TILES, 2])
        ve = sb("ve", [P, TILES])
        mhalf = sb("mhalf", [P, HT])
        wf3 = km[:, 6:8, :].rearrange("p a b -> p (a b)")[:, 0:3 * F3]
        rstd = sb("rstd", [P, TILES])
        mx = sb("mx", [P, 4, 8])
        sm = sb("sm", [P, 4, 8])
        rc = sb("rc", [P, 4, 8])
        a4, a50 = moe1[0:4, 3072:3200], moe1[0:50, 3200:3328]
        weff = sb("weff", [P, D])
        ex1 = sb("ex1", [P, 2, 16])
        pq = sb("pq", [P, 4, 16])
        kg = moe1[:, 2560:3072].rearrange("p (i n l) -> p i n l", i=2, n=16)
        kl = sb("kl", [P, 17])
        lg = sb("lg", [P, TILES, E])
        m8 = sb("m8", [P, TILES, E])
        i8 = sb("i8", [P, TILES, E], U32)
        f8 = sb("f8", [P, TILES, E])
        g8 = sb("g8", [P, 4, TILES])
        e8 = sb("e8", [P, 2, TILES, E])
        gw = sb("gw", [P, TILES, E])
        selb = sb("selb", [P, TILES, E], BF16)
        pad8 = sb("pad8", [3, T], U8)
        sg3 = moe2[:, 2048:3072].rearrange("p (r f) -> p r f", r=2)
        hv3 = moe2[:, 3072:5120].rearrange("p (r f) -> p r f", r=4)
        addm = relh[0:3, 0:2, :].rearrange("p a b -> p (a b)")
        padb = relh[0:1, 2:4, :].rearrange("p a b -> p (a b)")
        q8 = sb("q8", [P, 6, TILES])
        omx = sb("omx", [P, 3, 2, HT])
        padB = moe2[:, 1024:2048]
        ws = sb("ws", [P, 4, 4])
        xqT = moe2[:, 0:512].bitcast(BF16)
        hb = moe2[:, 512:1024].bitcast(BF16).rearrange("p (r f) -> p r f", r=2)
        hqT = moe2[:, 1024:1536].bitcast(BF16).rearrange("p (r c q) -> p r c q", r=2, c=4)

        score = [ps(f"score{i}") for i in range(4)]
        ptb = [ps(f"ptb{i}") for i in range(2)]
        ub = [ps(f"unit{i}") for i in range(2)]

        ld_a, ld_b, ld_h, ld_r = sem("ld_a"), sem("ld_b"), sem("ld_h"), sem("ld_r")
        ld_x = [sem("ld_x0"), sem("ld_x1")]
        ld_ctx, ld_pad, ld_rel = sem("ld_ctx"), sem("ld_pad"), sem("ld_rel")
        ld_w3a, ld_wf3 = sem("ld_w3a"), sem("ld_wf3")
        ld_slot = {m: [sem(f"ld_expert{m}_{s}") for s in range(SLOTS)] for m in (1, 2)}
        w_high, w_low = sem("w_high"), sem("w_low")
        y_high, y_low = sem("y_high"), sem("y_low")
        stored = sem("stored")
        zeroed = sem("zeroed")
        unit_full = sem("unit_full")
        unit_read = [sem("unit_read0"), sem("unit_read1")]
        ln_stat, ln_mv, ln_ve, ln_rstd, ln_y = (sem(n) for n in ("ln_stat", "ln_mv", "ln_ve", "ln_rstd", "ln_y"))
        keys_spread = sem("keys_spread")
        sc_full = sem("sc_full")
        row_max, shifted, row_sum, row_rcp = (sem(n) for n in ("row_max", "shifted", "row_sum", "row_rcp"))
        exped = sem("exped")
        normed = sem("normed")
        turned = sem("turned")
        copied = sem("copied")
        valued = sem("valued")
        turned3, copied3, down3 = sem("turned3"), sem("copied3"), sem("down3")
        turn_free = [sem("turn_free0"), sem("turn_free1")]
        downed = sem("downed")
        x_biased = sem("x_biased")
        bias_split = sem("bias_split")
        pad_ready = sem("pad_ready")
        abs_sum = sem("abs_sum")
        ternary = sem("ternary")
        chosen = sem("chosen")
        sig_exp, pq_done, log_q, tap_arg, tap_exp = (sem(n) for n in ("sig_exp", "pq_done", "log_q", "tap_arg", "tap_exp"))
        conv = sem("conv")
        convact = sem("convact")
        gate_arg, gate_exp = sem("gate_arg"), sem("gate_exp")
        gu_full = sem("gu_full")
        silued = sem("silued")
        hidden = sem("hidden")
        small_a = sem("small_a")
        added = sem("added")
        swapped = [sem(f"swapped{i}") for i in range(4)]
        rot_c, rot_s, rot = sem("rot_c"), sem("rot_s"), sem("rot")
        gu3_full, silued3, hidden3, scaled3, shifted3, rounded3 = (sem(n) for n in (
            "gu3_full", "silued3", "hidden3", "scaled3", "shifted3", "rounded3"))
        half_set = sem("half_set")
        keys_spread_a = sem("keys_spread_a")
        tapped = sem("tapped")
        vb_clear = sem("vb_clear")
        quant_x, quant_t, quant_arg = sem("quant_x"), sem("quant_t"), sem("quant_arg")
        dve_step = sem("dve_step")

        block = ctx.enter_context(nc.Block())
        unit = {}
        use = {}

        def full(eng, key):
            eng.wait_ge(unit_full, unit[key] + 1)

        def read(eng, key):
            n = unit[key]
            eng.wait_ge(unit_read[n % 2], n // 2 + 1)

        def bank(key):
            return ub[unit[key] % 2]

        def done(ins, key):
            return ins.then_inc(unit_read[unit[key] % 2], 1)

        def freed(eng, key):
            n = use[key]
            eng.wait_ge(turn_free[n % 2], n // 2 + 1)

        def tbank(key):
            return ptb[use[key] % 2]

        def free(ins, key):
            return ins.then_inc(turn_free[use[key] % 2], 1)

        def half(c):
            return slice(c * HALF, (c + 1) * HALF)

        def value_parts(key, c):
            for b2 in range(2):
                for hh in range(2):
                    for h in range(2):
                        src = bank(key)[64 * b2:64 * b2 + 64, 64 * h + 8 * hh:]
                        dst = vb[64 * hh:64 * hh + 64, HB * c + b2, 64 * h + 8 * hh:]
                        yield (spread(dst, [[2 * 512, HT], [P + 16, 4], [1, DH]]),
                               spread(src, [[P, HT], [16, 4], [1, DH]]))

        def value_parts3(key, G, i, h):
            for b2 in range(2):
                for hp in range(2):
                    src = bank(key)[64 * b2:64 * b2 + 64, hp * P:]
                    dst = v3[G][64 * hp:64 * hp + 64, 2 * i + b2, 2 * h * P:]
                    yield spread(dst, [[P, 2], [1, P]]), spread(src, [[2 * P, 2], [1, P]])

        QSRC = {X0: ("wq0", 1), A2: ("wqa2", 7), X3: ("wq3", 12)}
        KV = {X0: ("wk0", "wv0"), A2: ("wka2", "wva2"), X3: ("wk3", "wv3")}
        OUTW = {A0: "wo0", X0: "fc0", X3: "wo3"}

        DVE_HEADS = 6

        def W(name):
            return A(name) if name in OFF_A else Bc(name)

        @block.tensor
        def _(pe):
            def new(key):
                n = len(unit)
                unit[key] = n
                if n >= 2:
                    pe.wait_ge(unit_read[n % 2], n // 2)
                return ub[n % 2]

            def take(key):
                n = len(use)
                use[key] = n
                if n >= 2:
                    pe.wait_ge(turn_free[n % 2], n // 2)
                return ptb[n % 2]

            def mm(o, l, r, first=True, last=True, **kw):
                return nc.tensor.matmul(o, l, r, start=first, stop=last, **kw)

            def turn_tiles(key, src):
                u = new(key)
                for i in range(HT):
                    m = nc.tensor.transpose(u[:, i * P:(i + 1) * P], src(i), A("ident"))
                m.then_inc(unit_full, 1)

            def project(key, w, src, m=D):
                u = new(key)
                mm(u[0:m, :], w, src).then_inc(unit_full, 1)

            def to_tokens(key, w, src, c):
                u = new(key)
                for i in range(HT):
                    t = HT * c + i
                    last = mm(u[:, i * P:(i + 1) * P], src[:, t * P:(t + 1) * P], w)
                last.then_inc(unit_full, 1)

            holder = [None] * 4

            def scores(a, b):
                g, c = nth("S", a, b), b // HB
                if holder[g % 4]:
                    pe.wait_ge(*holder[g % 4])
                holder[g % 4] = (shifted, g + 1)
                bk = score[g % 4]
                if a == A3:
                    G, bb = b // QB, b % QB
                    if bb == 0:
                        pe.wait_ge(rot, nth("rope", G, 1, 1) + 1)
                    mm(bk[:, :], Hc("identb"), spread(Hc("causal"), [[0, HH], [1, S]]), True, False)
                    for h in range(8):
                        for s in range(2):
                            m = mm(bk[64 * s:64 * s + 64, h * S:(h + 1) * S],
                                   qraw[G][64 * s:64 * s + 64, h, bb * S:(bb + 1) * S],
                                   kraw[G][64 * s:64 * s + 64, h, bb * S:(bb + 1) * S], False, h == 7)
                    m.then_inc(sc_full, 1)
                    return
                if b % HB == 0:
                    read(pe, ("q", a, c))
                    pe.wait_ge(keys_spread, DVE_HEADS * (nth("spread", a, c) + 1))
                    pe.wait_ge(keys_spread_a, (HH - DVE_HEADS) * (nth("spread", a, c) + 1))
                if a == X0 and b == 0:
                    pe.wait_ge(bias_split, 1)
                m = mm(bk[:, :], qbd[:, b, :], km[:, :, b * S:(b + 1) * S], True, a == A2)
                if a == A0:
                    m = mm(bk[:, :], Hc("identb"), spread(Hc("causal"), [[0, HH], [1, S]]), False, True)
                if a == X0:
                    for i in range(3):
                        m = mm(bk[:, :], Hc("identb"), relh[:, i, :], False, i == 2)
                if a == X3:
                    m = mm(bk[:, :], Hc("ones", 3), spread(addm[0:3, b * S:(b + 1) * S], [[0, HH], [1, S]]), False, True)
                m.then_inc(sc_full, 1)

            def values(a, b):
                g = nth("val", a, b)
                tb = tbank(("T", a, b))
                if a == A3:
                    G, bb = b // QB, b % QB
                    read(pe, ("v3", G, bb // 2, 0))
                    read(pe, ("v3", G, bb // 2, 1))
                elif b % HB == 0:
                    read(pe, ("v", a, b // HB))
                pe.wait_ge(copied, g + 1)
                pt = pT[:, use[("T", a, b)] % 2, :]
                if a == A3:
                    for j in range(4):
                        for hp in range(2):
                            for s in range(2):
                                m = mm(tb[64 * hp:64 * hp + 64, (2 * j + s) * S:(2 * j + s + 1) * S],
                                       v3[G][64 * hp:64 * hp + 64, bb, j * P + s * S:j * P + (s + 1) * S],
                                       pt[64 * hp:64 * hp + 64, j * P + s * S:j * P + (s + 1) * S])
                else:
                    for j in range(4):
                        m = mm(tb[:, 0:P], vb[:, b, j * P:(j + 1) * P], pt[:, j * P:(j + 1) * P], j == 0, j == 3)
                m.then_inc(valued, 1)

            pe.wait_ge(ld_a, 16)
            pe.wait_ge(ld_h, 16)
            for kind, *args in SCHEDULE:
                if kind == "lnT":
                    L, c = args
                    pe.wait_ge(ln_y, HT * (nth("apply", L, c) + 1))
                    turn_tiles(("lnT", L, c), lambda i: y[:, HT * c + i, :])
                elif kind == "c0":
                    c, = args
                    read(pe, ("lnT", 0, c))
                    project(("c0", c), A("dqkv"), yT[:, half(c)], 64)
                elif kind == "q":
                    a, c = args
                    if a == A0:
                        read(pe, ("c0", c))
                        project(("q", a, c), A("uq", 32), oT[0:32, half(c)])
                    else:
                        name, L = QSRC[a]
                        read(pe, ("lnT", L, c))
                        project(("q", a, c), W(name), yT[:, half(c)])
                elif kind == "k":
                    a, c = args
                    if a == A0:
                        o = OFF_A["uk"][0]
                        project(("k", a, c), sA[32:64, o:o + D], oT[32:64, half(c)])
                    else:
                        if a == X0:
                            pe.wait_ge(ld_ctx, 16)
                        project(("k", a, c), W(KV[a][0]), (yT if a == A2 else ctxT)[:, half(c)])
                elif kind == "v":
                    a, c = args
                    if a == A0:
                        o = OFF_A["uv"][0]
                        to_tokens(("v", a, c), sA[32:64, o:o + D], oT[32:64, :], c)
                    else:
                        to_tokens(("v", a, c), W(KV[a][1]), yT if a == A2 else ctxT, c)
                elif kind == "S":
                    scores(*args)
                elif kind == "turn":
                    a, b = args
                    g = nth("turn", a, b)
                    tb = take(("T", a, b))
                    pe.wait_ge(normed, g + 1)
                    for j in range(4):
                        m = nc.tensor.transpose(tb[:, j * P:(j + 1) * P], pr[:, g % 4, j * P:(j + 1) * P], A("ident"))
                    m.then_inc(turned, 1)
                elif kind == "val":
                    values(*args)
                elif kind == "o":
                    a, c = args
                    freed(pe, ("T", a, HB * c + HB - 2))
                    freed(pe, ("T", a, HB * c + HB - 1))
                    to_tokens(("o", a, c), W(OUTW[a]), oT, c)
                elif kind == "lora":
                    u = new("lo1")
                    mm(u[0:4, 0:P], A("lordT", 100), A("dauxT", 100)).then_inc(unit_full, 1)
                    u = new("lo2")
                    read(pe, "lo1")
                    mm(u[0:50, 0:P], A("loruT", 4), a4[:, :]).then_inc(unit_full, 1)
                    u = new("lo3")
                    read(pe, "lo2")
                    mm(u[:, 0:P], a50[:, :], A("uauxT", 50)).then_inc(unit_full, 1)
                elif kind == "wsum":
                    u = new("wsum")
                    pe.wait_ge(abs_sum, 1)
                    mm(u[:, 0:3], A("mean"), ws[:, 0, 0:3]).then_inc(unit_full, 1)
                elif kind == "f0":
                    c, = args
                    read(pe, "lo3")
                    read(pe, ("lnT", 2, c))
                    to_tokens(("f0", c), weff[:, :], yT, c)
                elif kind == "cv":
                    c, = args
                    pe.wait_ge(convact, c + 1)
                    turn_tiles(("cv", c), lambda i: oT[:, (HT * c + i) * P:(HT * c + i + 1) * P])
                elif kind == "qkv1":
                    n, c = args
                    pe.wait_ge(ld_b, 16)
                    read(pe, ("lnT", 4 if n == 1 else 8, c))
                    project(("q1", n, c), Bc(f"wq{n}"), yT[:, half(c)])
                    project(("k1", n, c), Bc(f"wk{n}"), ctxT[:, half(c)])
                    to_tokens(("v1", n, c), Bc(f"wv{n}"), ctxT, c)
                elif kind == "s1":
                    c, = args
                    u = new(("s1", c))
                    read(pe, ("q1", 1, c))
                    read(pe, ("k1", 1, c))
                    for i in range(HT):
                        sl = slice((HT * c + i) * P, (HT * c + i + 1) * P)
                        m = mm(u[:, i * P:(i + 1) * P], kT[:, sl], qf[:, sl])
                    m.then_inc(unit_full, 1)
                elif kind == "s2":
                    c, = args
                    u = new(("s2", c))
                    read(pe, ("q1", 2, c))
                    read(pe, ("k1", 2, c))
                    mm(u[:, :], Hc("identb"), spread(Hc("offblk"), [[0, HT], [1, P]]), True, False)
                    for i in range(HT):
                        sl = slice((HT * c + i) * P, (HT * c + i + 1) * P)
                        m = mm(u[:, i * P:(i + 1) * P], qf[:, sl], kT[:, sl], False, i == HT - 1)
                    m.then_inc(unit_full, 1)
                elif kind == "p2":
                    c, = args
                    pe.wait_ge(small_a, c + 1)
                    turn_tiles(("p2", c), lambda i: p1[:, (HT * c + i) * P:(HT * c + i + 1) * P])
                elif kind == "o1":
                    n, c = args
                    u = new(("o1", n, c))
                    read(pe, ("s1", c) if n == 1 else ("p2", c))
                    read(pe, ("v1", n, c))
                    for i in range(HT):
                        t = HT * c + i
                        m = mm(u[:, i * P:(i + 1) * P], (p1 if n == 1 else p1T)[:, t * P:(t + 1) * P], vt[:, t, :])
                    m.then_inc(unit_full, 1)
                elif kind == "o2":
                    c, = args
                    pe.wait_ge(added, c + 1)
                    turn_tiles(("o2", c), lambda i: oT[:, (HT * c + i) * P:(HT * c + i + 1) * P])
                elif kind == "gate":
                    m_, c = args
                    u = new(("gate", m_, c))
                    read(pe, ("lnT", 5 if m_ == 1 else 10, c))
                    for i in range(HT):
                        t = HT * c + i
                        m = mm(u[:, i * E:(i + 1) * E], yT[:, t * P:(t + 1) * P], Bc("wg1" if m_ == 1 else "wr2"))
                    m.then_inc(unit_full, 1)
                elif kind == "rank":
                    c, = args
                    u = new(("rank", c))
                    pe.wait_ge(chosen, c + 1)
                    t0 = HT * c
                    mm(u[:, 0:HT * E], Hc("before"), selb[:, t0:t0 + HT, :].rearrange("p t e -> p (t e)"), True, False)
                    for t in range(t0 + HT - 1):
                        i = max(t + 1 - t0, 0)
                        m = mm(u[:, i * E:HT * E], Hc("ones"), spread(selb[:, t, :], [[0, HT - i], [1, E]]), False,
                               t == t0 + HT - 2)
                    m.then_inc(unit_full, 1)
                elif kind == "GU":
                    m_, c, n = args
                    k, fn = nth("GU", m_, c, n), NF[m_] * P
                    e, f = n // NF[m_], n % NF[m_]
                    if n == 0:
                        pe.wait_ge(y_low, nth("ysplit", m_, c) + 1)
                    if f == 0:
                        pe.wait_ge(w_low, nth("split", m_, E * c + e) + 1)
                    slot = (E * c + e) % 2
                    for h in range(2):
                        i = 2 * (k % 2) + h
                        pe.wait_ge(*holder[i])
                        holder[i] = (hidden, k + 1)
                        sl = slice(h * fn + f * P, h * fn + (f + 1) * P)
                        mm(score[i][:, :], wlo[m_][:, slot, sl], yhi[:, half(c)], True, False)
                        mm(score[i][:, :], whi[m_][:, slot, sl], yhi[:, half(c)], False, False)
                        m = mm(score[i][:, :], whi[m_][:, slot, sl], ylo[:, half(c)], False, True)
                    m.then_inc(gu_full, 1)
                elif kind == "DN":
                    m_, c, n = args
                    e, f, k = n // NF[m_], n % NF[m_], nth("DN", m_, c, n)
                    if f == 0:
                        take(("m", m_, c, e))
                    pe.wait_ge(hidden, k + 1)
                    tb = tbank(("m", m_, c, e))
                    for i in range(HT):
                        m = mm(tb[:, i * P:(i + 1) * P], pr[:, k % 4, i * P:(i + 1) * P], wdn[m_][:, (E * c + e) % SLOTS, f, :],
                               f == 0 and i == 0, f == NF[m_] - 1 and i == HT - 1, skip_group_check=True)
                    m.then_inc(downed, 1)
                elif kind == "bvo":
                    pe.wait_ge(ld_w3a, 32)
                    u = new("bvo")
                    for i in range(8):
                        m = mm(u[:, 0:P], spread(Bc("bV3")[:, i:i + 1], [[0, P]]), w3o[:, i, :], i == 0, i == 7)
                    m.then_inc(unit_full, 1)
                elif kind == "qk3":
                    G, w, i = args
                    c = G // 2
                    u = new(("qk3", G, w, i))
                    if w == 0 and i == 0:
                        read(pe, ("lnT", 11, c))
                    for j in range(2):
                        m = mm(u[:, j * QN:(j + 1) * QN], w3qkv[:, w, (i + j) * P:(i + j + 1) * P],
                               yT[:, G * QN:(G + 1) * QN])
                    m.then_inc(unit_full, 1)
                elif kind == "v3":
                    G, i = args
                    t = 2 * G + i
                    for h in range(2):
                        u = new(("v3", G, i, h))
                        mm(u[:, :], yT[:, t * P:(t + 1) * P], w3qkv[:, 2, h * 512:(h + 1) * 512]).then_inc(unit_full, 1)
                elif kind == "o3":
                    t, = args
                    u = new(("o3", t))
                    freed(pe, ("T", A3, 2 * t))
                    freed(pe, ("T", A3, 2 * t + 1))
                    for i in range(8):
                        m = mm(u[:, 0:P], zT[:, t % 2, i, :], w3o[:, i, :], i == 0, i == 7)
                    m.then_inc(unit_full, 1)
                elif kind == "pad":
                    pe.wait_ge(pad_ready, 1)
                    for c in range(2):
                        u = new(("pad", c))
                        mm(u[:, :], Hc("ones", 1), padb[0:1, half(c)]).then_inc(unit_full, 1)
                elif kind == "xq":
                    c, = args
                    pe.wait_ge(quant_x, c + 1)
                    turn_tiles(("xq", c), lambda i: y[:, HT * c + i, :])
                elif kind == "gu3":
                    t, = args
                    read(pe, ("xq", t // HT))
                    for h in range(2):
                        i = 2 * (t % 2) + h
                        pe.wait_ge(*holder[i])
                        holder[i] = (hidden3, t + 1)
                        m = mm(score[i][:, :], xqT[:, t * P:(t + 1) * P], wf3q[:, h * F3:(h + 1) * F3])
                    m.then_inc(gu3_full, 1)
                elif kind == "turn3":
                    t, = args
                    tb = take(("f3", t))
                    pe.wait_ge(quant_t, t + 1)
                    for f in range(4):
                        m = nc.tensor.transpose(tb[:, 0:256].bitcast(BF16)[:, f * P:(f + 1) * P],
                                                hb[:, t % 2, f * P:(f + 1) * P], Hc("identb"))
                    m.then_inc(turned3, 1)
                elif kind == "down3":
                    t, = args
                    tb = tbank(("f3", t))
                    pe.wait_ge(copied3, t + 1)
                    for f in range(4):
                        m = mm(tb[:, 384:512], hqT[:, t % 2, f, :], wf3q[:, 2 * F3 + f * P:2 * F3 + (f + 1) * P],
                               f == 0, f == 3)
                    m.then_inc(down3, 1)

        @block.vector
        def _(dve):
            v = nc.vector
            steps = [0]

            def link(ins):
                steps[0] += 1
                ins.then_inc(dve_step, 1)
                dve.wait_ge(dve_step, steps[0])

            def add_x(key, c, biased=None):
                full(dve, key)
                if biased:
                    dve.wait_ge(x_biased, nth("bias", biased, c) + 1)
                xs = x[:, HT * c:HT * (c + 1), :].rearrange("p t d -> p (t d)")
                done(v.tensor_tensor(xs, bank(key)[:, :], xs, ALU.add), key)

            def softmax(cur, prev):
                if prev:
                    g1 = nth("S", *prev)
                    dve.wait_ge(exped, g1 + 1)
                    v.tensor_reduce(sm[:, g1 % 4, :], pr[:, g1 % 4, :].rearrange("p (h k) -> p h k", h=8),
                                    AX.X, ALU.add).then_inc(row_sum, 1)
                if cur:
                    g = nth("S", *cur)
                    s3 = score[g % 4][:, :].rearrange("p (h k) -> p h k", h=8)
                    dve.wait_ge(sc_full, g + 1)
                    v.tensor_reduce(mx[:, g % 4, :], s3, AX.X, ALU.max).then_inc(row_max, 1)
                if prev:
                    dve.wait_ge(row_sum, g1 + 1)
                    v.reciprocal(rc[:, g1 % 4, :], sm[:, g1 % 4, :]).then_inc(row_rcp, 1)
                if cur:
                    dve.wait_ge(row_max, g + 1)
                    if g >= 4:
                        dve.wait_ge(turned, g - 3)
                    v.tensor_tensor(pr[:, g % 4, :].rearrange("p (h k) -> p h k", h=8), s3,
                                    spread(mx[:, g % 4, :], [[1, 8], [0, S]]), ALU.subtract).then_inc(shifted, 1)

            def best_two(src, c):
                for t in range(HT * c, HT * (c + 1)):
                    last = v.max(m8[:, t, :], src[:, t, :])
                link(last)
                for t in range(HT * c, HT * (c + 1)):
                    last = v.max_index(i8[:, t, :], m8[:, t, :], src[:, t, :])
                link(last)

            def mark_two(c):
                sl = slice(HT * c, HT * (c + 1))
                link(v.tensor_copy(f8[:, sl, :], i8[:, sl, :]))
                for k in range(2):
                    it = spread(A("iota"), [[0, HT], [1, E]])
                    ix = spread(f8[:, HT * c, k:k + 1], [[E, HT], [0, E]])
                    last = v.tensor_tensor(e8[:, k, sl, :], it, ix, ALU.is_equal)
                    if k == 0:
                        link(last)
                return last

            def weigh(p1_, p2_, c):
                sl = slice(HT * c, HT * (c + 1))
                for k, p in enumerate((p1_, p2_)):
                    link(v.tensor_tensor(e8[:, k, sl, :], e8[:, k, sl, :], p, ALU.mult))
                link(v.tensor_tensor(gw[:, sl, :], e8[:, 0, sl, :], e8[:, 1, sl, :], ALU.add))

            for kind, *args in SCHEDULE:
                if kind == "stats":
                    L, c = args
                    n, ts = nth("stats", L, c), range(HT * c, HT * (c + 1))
                    if L in FROM_Y:
                        dve.wait_ge(ln_y, HT * (nth("apply", L - 1, c) + 1))
                    elif L in (6, 11):
                        freed(dve, ("m", 1 if L == 6 else 2, c, E - 1))
                    elif L == 12:
                        for t in ts:
                            read(dve, ("o3", t))
                    elif L:
                        read(dve, AFTER[L] + (c,))
                    else:
                        dve.wait_ge(ld_x[c], 16)
                    src = y if L in FROM_Y else x
                    for t in ts:
                        v.bn_stats(bst[:, t, :], src[:, t, :]).then_inc(ln_stat, 1)
                    for i, t in enumerate(ts):
                        dve.wait_ge(ln_stat, HT * n + i + 1)
                        v.bn_aggr(mv[:, t, :], bst[:, t, :]).then_inc(ln_mv, 1)
                    dve.wait_ge(ln_mv, HT * (n + 1))
                    sl = slice(HT * c, HT * (c + 1))
                    v.tensor_scalar(ve[:, sl], mv[:, sl, 1], EPS.get(L, 1e-5), None, ALU.add).then_inc(ln_ve, 1)
                elif kind == "apply":
                    L, c = args
                    dve.wait_ge(ln_rstd, nth("stats", L, c) + 1)
                    src = y if L in FROM_Y else x
                    for t in range(HT * c, HT * (c + 1)):
                        v.tensor_scalar(y[:, t, :], src[:, t, :], mv[:, t, 0:1], rstd[:, t:t + 1],
                                        ALU.subtract, ALU.mult).then_inc(ln_y, 1)
                elif kind == "k" and args[0] == X3:
                    a, c = args
                    full(dve, ("k", a, c))
                    read(dve, ("pad", c))
                    done(v.tensor_tensor(kT[:, half(c)], bank(("k", a, c))[:, :], padB[:, half(c)], ALU.mult), ("k", a, c))
                elif kind == "spread":
                    a, c = args
                    dve.wait_ge(ld_a, 16)
                    read(dve, ("k", a, c))
                    for h in range(DVE_HEADS):
                        v.tensor_scalar(km[:, h, half(c)], kT[:, half(c)], A("hm")[:, h:h + 1], None, ALU.mult)\
                            .then_inc(keys_spread, 1)
                elif kind == "soft":
                    softmax(*args)
                elif kind == "o":
                    a, c = args
                    add_x(("o", a, c), c, {X0: 1, X3: 12}.get(a))
                elif kind == "f0":
                    c, = args
                    add_x(("f0", c), c, 2)
                elif kind == "cv":
                    add_x(("cv", args[0]), args[0])
                elif kind == "o2":
                    add_x(("o2", args[0]), args[0])
                elif kind == "lora":
                    full(dve, "lo3")
                    done(v.tensor_tensor(weff[:, :], bank("lo3")[:, 0:P], A("ffW"), ALU.add), "lo3")
                elif kind == "split_rel":
                    if args[0] == 0:
                        dve.wait_ge(ld_rel, 16)
                        link(v.tensor_copy(relh[:, 0, :], rel[:, :]))
                        link(v.tensor_tensor(rel[:, :], rel[:, :], relh[:, 0, :], ALU.subtract))
                    else:
                        link(v.tensor_copy(relh[:, 1, :], rel[:, :]))
                        link(v.tensor_tensor(rel[:, :], rel[:, :], relh[:, 1, :], ALU.subtract))
                        v.tensor_copy(relh[:, 2, :], rel[:, :]).then_inc(bias_split, 1)
                elif kind == "pad_setup":
                    dve.wait_ge(ld_pad, 16)
                    link(v.tensor_copy(padb[0:1, :], pad8[0:1, :]))
                    v.tensor_scalar(addm[0:3, :], pad8[0:3, :], 1.0, A("padc", 3), ALU.subtract, ALU.mult)\
                        .then_inc(pad_ready, 1)
                elif kind == "abs3":
                    dve.wait_ge(ld_wf3, 16)
                    v.tensor_reduce(ws[:, 0, 0:3], wf3[:, :].rearrange("p (w n) -> p w n", w=3), AX.X, ALU.add,
                                    apply_absolute_value=True).then_inc(abs_sum, 1)
                elif kind == "ternary":
                    w, = args
                    if w == 0:
                        full(dve, "wsum")
                        done(v.tensor_scalar(ws[:, 1, 0:3], bank("wsum")[:, 0:3], 1e-5, None, ALU.max), "wsum")
                        read(dve, "wsum")
                        link(v.reciprocal(ws[:, 2, 0:3], ws[:, 1, 0:3]))
                    wv = wf3[:, w * F3:(w + 1) * F3]
                    link(v.tensor_scalar(wv, wv, ws[:, 2, w:w + 1], -1.0, ALU.mult, ALU.max))
                    link(v.tensor_scalar(wv, wv, 1.0, ROUND, ALU.min, ALU.add))
                    v.tensor_scalar(wf3q[:, w * F3:(w + 1) * F3], wv, ROUND, None, ALU.subtract).then_inc(ternary, 1)
                elif kind == "taps":
                    part, = args
                    if part == 0:
                        dve.wait_ge(ld_b, 16)
                        dve.wait_ge(sig_exp, 2)
                        link(v.tensor_scalar(ex1[:, :, :], ex1[:, :, :], 1.0, None, ALU.add))
                        link(v.reciprocal(pq[:, 0:2, :], ex1[:, :, :]))
                        link(v.tensor_tensor(pq[:, 2, :], pq[:, 0, :], pq[:, 1, :], ALU.mult))
                        v.tensor_scalar(pq[:, 2, :], pq[:, 2, :], -1.0, 1.0, ALU.mult, ALU.add).then_inc(pq_done, 1)
                    elif part == 1:
                        link(v.tensor_tensor(pq[:, 0, :], pq[:, 0, :], Bc("beta"), ALU.mult))
                        link(v.scalar_tensor_tensor(pq[:, 0, :], pq[:, 0, :], 0.25, Bc("gamma"), ALU.mult, ALU.mult))
                        dve.wait_ge(log_q, 1)
                        v.tensor_tensor(kg[:, 0, :, :], spread(pq[:, 3, :], [[1, 16], [0, 16]]),
                                        spread(Bc("lgrid"), [[0, 16], [1, 16]]), ALU.mult).then_inc(tap_arg, 1)
                    else:
                        dve.wait_ge(tap_exp, 1)
                        link(v.tensor_tensor(kg[:, 1, :, :], kg[:, 0, :, :], spread(pq[:, 0, :], [[1, 16], [0, 16]]), ALU.mult))
                        link(v.tensor_reduce(kl[:, 0:16], spread(kg[:, 1, :, :], [[1, 16], [16, 16]]), AX.X, ALU.add))
                        v.tensor_tensor(kl[:, 0:1], kl[:, 0:1], Bc("omega"), ALU.add).then_inc(tapped, 1)
                elif kind == "conv":
                    c, part = args
                    t0, t1 = c * HALF, (c + 1) * HALF
                    taps = HB * (c + 1)
                    if part == 0:
                        dve.wait_ge(tapped, 1)
                        read(dve, ("lnT", 3, c))
                        link(v.tensor_scalar(oT[:, t0:t1], ycv[:, t0:t1], kl[:, 0:1], None, ALU.mult))
                    for l in range(max(4 * part, 1), 4 * part + 4):
                        o = max(t0, l * S)
                        ins = v.scalar_tensor_tensor(oT[:, o:t1], ycv[:, o - l * S:t1 - l * S], kl[:, l:l + 1],
                                                     oT[:, o:t1], ALU.mult, ALU.add)
                        if l < taps - 1:
                            link(ins)
                        else:
                            ins.then_inc(conv, 1)
                elif kind == "qkv1":
                    n, c = args
                    key = ("v1", n, c)
                    full(dve, key)
                    dve.wait_ge(ld_r, 16)
                    done(v.tensor_tensor(vt[:, HT * c:HT * (c + 1), :],
                                         bank(key)[:, :].rearrange("p (t d) -> p t d", t=HT),
                                         spread(row(f"bv{n}"), [[0, HT], [1, D]]), ALU.add), key)
                elif kind == "s1":
                    c, = args
                    key = ("s1", c)
                    full(dve, key)
                    done(v.scalar_tensor_tensor(p1[:, half(c)].rearrange("p (t q) -> p t q", t=HT),
                                                bank(key)[:, :].rearrange("p (t q) -> p t q", t=HT), 0.0,
                                                spread(Bc("blk"), [[0, HT], [1, P]]), ALU.max, ALU.mult), key)
                elif kind == "s2":
                    c, = args
                    key = ("s2", c)
                    full(dve, key)
                    s3 = bank(key)[:, :].rearrange("p (t k) -> p t k", t=HT)
                    link(v.tensor_reduce(omx[:, 0, c, :], s3, AX.X, ALU.max))
                    done(v.tensor_tensor(p1[:, half(c)].rearrange("p (t k) -> p t k", t=HT), s3,
                                         spread(omx[:, 0, c, :], [[1, HT], [0, P]]), ALU.subtract), key)
                elif kind == "p2":
                    c, = args
                    dve.wait_ge(small_a, c + 1)
                    link(v.tensor_reduce(omx[:, 1, c, :], p1[:, half(c)].rearrange("p (t k) -> p t k", t=HT), AX.X, ALU.add))
                    link(v.reciprocal(omx[:, 2, c, :], omx[:, 1, c, :]))
                elif kind == "o1":
                    n, c = args
                    key = ("o1", n, c)
                    if n == 1:
                        add_x(key, c)
                    else:
                        full(dve, key)
                        for i in range(HT):
                            t = HT * c + i
                            last = v.scalar_tensor_tensor(x[:, t, :], bank(key)[:, i * P:(i + 1) * P], omx[:, 2, c, i:i + 1],
                                                          x[:, t, :], ALU.mult, ALU.add)
                        done(last, key)
                elif kind == "gate":
                    m_, c = args
                    key, n = ("gate", m_, c), nth("gate", m_, c)
                    sl = slice(HT * c, HT * (c + 1))
                    lf = lg[:, sl, :].rearrange("p t e -> p (t e)")
                    full(dve, key)
                    if m_ == 1:
                        done(v.tensor_copy(lf, bank(key)[:, 0:HT * E]), key)
                        read(dve, key)
                        best_two(lg, c)
                        v.tensor_tensor(g8[:, 0, sl], m8[:, sl, 1], m8[:, sl, 0], ALU.subtract).then_inc(gate_arg, 1)
                        link(mark_two(c))
                        dve.wait_ge(gate_exp, n + 1)
                        link(v.tensor_scalar(g8[:, 2, sl], g8[:, 1, sl], 1.0, None, ALU.add))
                        link(v.reciprocal(g8[:, 2, sl], g8[:, 2, sl]))
                        link(v.tensor_tensor(g8[:, 3, sl], g8[:, 1, sl], g8[:, 2, sl], ALU.mult))
                        weigh(spread(g8[:, 2, sl], [[1, HT], [0, E]]), spread(g8[:, 3, sl], [[1, HT], [0, E]]), c)
                    else:
                        done(v.tensor_scalar(lf, bank(key)[:, 0:HT * E], 1e4, -1e4, ALU.min, ALU.max), key)
                        read(dve, key)
                        link(v.tensor_reduce(g8[:, 0, sl], lg[:, sl, :], AX.X, ALU.max))
                        v.tensor_tensor(lg[:, sl, :], lg[:, sl, :], spread(g8[:, 0, sl], [[1, HT], [0, E]]), ALU.subtract)\
                            .then_inc(gate_arg, 1)
                        dve.wait_ge(gate_exp, n + 1)
                        link(v.tensor_reduce(g8[:, 1, sl], lg[:, sl, :], AX.X, ALU.add))
                        link(v.tensor_scalar(g8[:, 1, sl], g8[:, 1, sl], 1e-12, None, ALU.add))
                        link(v.reciprocal(g8[:, 1, sl], g8[:, 1, sl]))
                        link(v.tensor_tensor(lg[:, sl, :], lg[:, sl, :], spread(g8[:, 1, sl], [[1, HT], [0, E]]), ALU.mult))
                        best_two(lg, c)
                        link(mark_two(c))
                        v.tensor_tensor(selb[:, sl, :], e8[:, 0, sl, :], e8[:, 1, sl, :], ALU.add).then_inc(chosen, 1)
                        weigh(spread(m8[:, HT * c, 0:1], [[E, HT], [0, E]]), spread(m8[:, HT * c, 1:2], [[E, HT], [0, E]]), c)
                elif kind == "ysplit":
                    m_, c = args
                    dve.wait_ge(y_high, nth(kind, m_, c) + 1)
                    v.tensor_tensor(ylo[:, half(c)], yT[:, half(c)], yhi[:, half(c)].bitcast(F32), ALU.subtract)\
                        .then_inc(y_low, 1)
                elif kind == "rank":
                    c, = args
                    key = ("rank", c)
                    gf = gw[:, HT * c:HT * (c + 1), :].rearrange("p t e -> p (t e)")
                    full(dve, key)
                    done(v.scalar_tensor_tensor(gf, bank(key)[:, 0:HT * E], float(CAP), gf, ALU.is_lt, ALU.mult), key)
                    read(dve, key)
                elif kind == "GU":
                    m_, c, n = args
                    k = nth("GU", m_, c, n)
                    dve.wait_ge(silued, k + 1)
                    if k >= 4:
                        dve.wait_ge(downed, k - 3)
                    v.tensor_tensor(pr[:, k % 4, :], score[2 * (k % 2) + 1][:, :], sg[:, k % 2, :], ALU.mult)\
                        .then_inc(hidden, 1)
                elif kind == "DN":
                    m_, c, n = args
                    e, f, k = n // NF[m_], n % NF[m_], nth("DN", m_, c, n)
                    if f < NF[m_] - 1:
                        continue
                    key = ("m", m_, c, e)
                    dve.wait_ge(downed, k + 1)
                    if e:
                        freed(dve, ("m", m_, c, e - 1))
                    for i in range(HT):
                        t = HT * c + i
                        last = v.scalar_tensor_tensor(x[:, t, :], tbank(key)[:, i * P:(i + 1) * P], gw[:, t, e:e + 1],
                                                      x[:, t, :], ALU.mult, ALU.add)
                    free(last, key)
                elif kind == "bvo":
                    full(dve, "bvo")
                    done(v.tensor_tensor(row("bO3"), bank("bvo")[:, 0:P], row("bO3"), ALU.add), "bvo")
                elif kind == "rotate":
                    G, w, h = args
                    r = (qraw, kraw)[w][G][:, 4 * h:4 * h + 4, :].rearrange("p i (b s) -> p i b s", b=QB)
                    dve.wait_ge(swapped[2 * w + h], 64 * (G + 1))
                    v.tensor_tensor(r, r, spread(Bc("cos"), [[0, 4], [0, QB], [1, S]]), ALU.mult).then_inc(rot_c, 1)
                elif kind == "rope":
                    G, w, h = args
                    n = nth("rope", G, w, h)
                    r = (qraw, kraw)[w][G][:, 4 * h:4 * h + 4, :].rearrange("p i (b s) -> p i b s", b=QB)
                    sw = swaps[G][:, w, 4 * h:4 * h + 4, :].rearrange("p i (b s) -> p i b s", b=QB)
                    dve.wait_ge(rot_c, n + 1)
                    dve.wait_ge(rot_s, n + 1)
                    v.tensor_tensor(r, r, sw, ALU.add).then_inc(rot, 1)
                elif kind == "v3":
                    G, i = args
                    key = ("v3", G, i, 1)
                    full(dve, key)
                    for o, src in value_parts3(key, G, i, 1):
                        last = v.tensor_copy(o, src)
                    done(last, key)
                elif kind == "o3":
                    t, = args
                    key = ("o3", t)
                    full(dve, key)
                    dve.wait_ge(x_biased, nth("bias", 11, t // HT) + 1)
                    done(v.tensor_tensor(x[:, t, :], bank(key)[:, 0:P], x[:, t, :], ALU.add), key)
                elif kind == "quant":
                    c, = args
                    sl = slice(HT * c, HT * (c + 1))
                    dve.wait_ge(ln_y, HT * (nth("apply", 13, c) + 1))
                    link(v.tensor_reduce(q8[:, 0, sl], y[:, sl, :], AX.X, ALU.max, apply_absolute_value=True))
                    link(v.tensor_scalar(q8[:, 0, sl], q8[:, 0, sl], 1e-5, 1.0 / 127.0, ALU.max, ALU.mult))
                    link(v.reciprocal(q8[:, 3, sl], q8[:, 0, sl]))
                    for t in range(HT * c, HT * (c + 1)):
                        last = v.tensor_scalar(y[:, t, :], y[:, t, :], q8[:, 3, t:t + 1], ROUND, ALU.mult, ALU.add)
                    link(last)
                    yc = y[:, sl, :].rearrange("p t d -> p (t d)")
                    link(v.tensor_scalar(yc, yc, ROUND + 127.0, ROUND - 128.0, ALU.min, ALU.max))
                    v.tensor_scalar(yc, yc, ROUND, None, ALU.subtract).then_inc(quant_x, 1)
                    for w in range(2):
                        link(v.tensor_scalar(q8[:, 1 + w, sl], q8[:, 0, sl], ws[:, 1, w:w + 1], None, ALU.mult))
                    v.sem_inc(quant_arg, 1)
                elif kind == "hid3":
                    p, = args
                    ts = (2 * p, 2 * p + 1)
                    for t in ts:
                        dve.wait_ge(silued3, t + 1)
                        if t >= 4:
                            dve.wait_ge(quant_t, t - 3)
                        v.scalar_tensor_tensor(hv3[:, t % 4, :], score[2 * (t % 2) + 1][:, :], q8[:, 2, t:t + 1],
                                               sg3[:, t % 2, :], ALU.mult, ALU.mult).then_inc(hidden3, 1)
                    for t in ts:
                        dve.wait_ge(hidden3, t + 1)
                        last = v.tensor_reduce(q8[:, 4, t:t + 1], hv3[:, t % 4, :], AX.X, ALU.max,
                                               apply_absolute_value=True)
                    link(last)
                    tt = slice(2 * p, 2 * p + 2)
                    link(v.tensor_scalar(q8[:, 4, tt], q8[:, 4, tt], 1e-5, 1.0 / 127.0, ALU.max, ALU.mult))
                    link(v.reciprocal(q8[:, 3, tt], q8[:, 4, tt]))
                    v.sem_inc(scaled3, 1)
                    link(v.tensor_scalar(q8[:, 5, tt], q8[:, 4, tt], ws[:, 1, 2:3], None, ALU.mult))
                elif kind == "clip3":
                    for t in (2 * args[0], 2 * args[0] + 1):
                        dve.wait_ge(shifted3, t + 1)
                        v.tensor_scalar(hv3[:, t % 4, :], hv3[:, t % 4, :], ROUND + 127.0, ROUND - 128.0,
                                        ALU.min, ALU.max).then_inc(rounded3, 1)
                elif kind == "add3":
                    for t in (2 * args[0], 2 * args[0] + 1):
                        key = ("f3", t)
                        dve.wait_ge(down3, t + 1)
                        free(v.scalar_tensor_tensor(x[:, t, :], tbank(key)[:, 384:512], q8[:, 5, t:t + 1], x[:, t, :],
                                                    ALU.mult, ALU.add), key)

        @block.scalar
        def _(act):
            a_ = nc.scalar

            def copy_unit(key, dst, src=None, **kw):
                full(act, key)
                done(a_.activation(dst, bank(key)[:, :] if src is None else src, ACT.Copy, **kw), key)

            for kind, *args in SCHEDULE:
                if kind == "lnT":
                    L, c = args
                    key = ("lnT", L, c)
                    if L in FROM_Y:
                        s, o = ("lns2", "lnb2") if L == 7 else ("gam2", "bet2")
                        full(act, key)
                        done(a_.activation(yT[:, half(c)], bank(key)[:, :], ACT.Identity, scale=Bc(s), bias=Bc(o)), key)
                    else:
                        copy_unit(key, (ycv if L == 3 else yT)[:, half(c)])
                elif kind == "c0":
                    c, = args
                    key = ("c0", c)
                    copy_unit(key, oT[0:64, half(c)], bank(key)[0:64, :])
                elif kind == "q":
                    a, c = args
                    key = ("q", a, c)
                    full(act, key)
                    act.wait_ge(zeroed, 1)
                    for h in range(2):
                        r = slice(64 * h, 64 * h + 64)
                        last = a_.activation(qbd[r, HB * c:HB * (c + 1), r],
                                             bank(key)[r, :].rearrange("p (b q) -> p b q", b=HB), ACT.Copy,
                                             scale=float(D) ** -0.5 if a == A2 else DH ** -0.5)
                    done(last, key)
                elif kind == "k" and args[0] != X3:
                    a, c = args
                    copy_unit(("k", a, c), kT[:, half(c)])
                elif kind == "spread":
                    a, c = args
                    read(act, ("k", a, c))
                    for h in range(DVE_HEADS, HH):
                        a_.activation(km[:, h, half(c)], kT[:, half(c)], ACT.Copy, scale=A("hm")[:, h:h + 1])\
                            .then_inc(keys_spread_a, 1)
                elif kind == "v":
                    a, c = args
                    key = ("v", a, c)
                    full(act, key)
                    if a == A0:
                        act.wait_ge(zeroed, 2 + c)
                    if a == X3:
                        act.wait_ge(vb_clear, 2 * (c + 1))
                    for o, i in value_parts(key, c):
                        last = a_.activation(o, i, ACT.Copy)
                    done(last, key)
                elif kind == "turn":
                    a, b = args
                    n = use[("T", a, b)]
                    act.wait_ge(turned, nth("turn", a, b) + 1)
                    a_.activation(pT[:, n % 2, :], ptb[n % 2][:, :], ACT.Copy).then_inc(copied, 1)
                elif kind == "soft":
                    if args[0]:
                        g = nth("S", *args[0])
                        act.wait_ge(shifted, g + 1)
                        a_.activation(pr[:, g % 4, :], pr[:, g % 4, :], ACT.Exp,
                                      scale=HD3 ** -0.5 if args[0][0] == A3 else 1.0).then_inc(exped, 1)
                elif kind == "val":
                    a, b = args
                    key = ("T", a, b)
                    act.wait_ge(valued, nth("val", a, b) + 1)
                    if a == A3:
                        t = b // 2
                        if b % 2 == 0 and t >= 2:
                            full(act, ("o3", t - 2))
                        free(a_.activation(zT[:, t % 2, :, (b % 2) * S:(b % 2 + 1) * S],
                                           tbank(key)[:, :].rearrange("p (h q) -> p h q", h=8), ACT.Copy), key)
                    else:
                        for h in range(2):
                            r = slice(64 * h, 64 * h + 64)
                            last = a_.activation(oT[r, b * S:(b + 1) * S], tbank(key)[r, r], ACT.Copy)
                        free(last, key)
                elif kind == "lora":
                    copy_unit("lo1", a4[:, :], bank("lo1")[0:4, 0:P])
                    copy_unit("lo2", a50[:, :], bank("lo2")[0:50, 0:P])
                elif kind == "taps":
                    if args[0] == 0:
                        act.wait_ge(ld_b, 16)
                        a_.activation(ex1[:, 0, :], Bc("delta"), ACT.Exp, scale=-1.0).then_inc(sig_exp, 1)
                        a_.activation(ex1[:, 1, :], Bc("alpha"), ACT.Exp, scale=-1.0).then_inc(sig_exp, 1)
                    elif args[0] == 1:
                        act.wait_ge(pq_done, 1)
                        a_.activation(pq[:, 3, :], pq[:, 2, :], ACT.Ln).then_inc(log_q, 1)
                    else:
                        act.wait_ge(tap_arg, 1)
                        a_.activation(kg[:, 0, :, :], kg[:, 0, :, :], ACT.Exp).then_inc(tap_exp, 1)
                elif kind == "conv" and args[1] == 2 * args[0] + 1:
                    c = args[0]
                    act.wait_ge(conv, c + 1)
                    a_.activation(oT[:, half(c)], oT[:, half(c)], ACT.Silu).then_inc(convact, 1)
                elif kind == "qkv1":
                    n, c = args
                    for nm, dst in (("q", qf), ("k", kT)):
                        key = (nm + "1", n, c)
                        full(act, key)
                        done(a_.activation(dst[:, half(c)], bank(key)[:, :], ACT.Identity, bias=Bc(f"b{nm}{n}")), key)
                elif kind == "s2":
                    c, = args
                    read(act, ("s2", c))
                    a_.activation(p1[:, half(c)], p1[:, half(c)], ACT.Exp).then_inc(small_a, 1)
                elif kind == "p2":
                    copy_unit(("p2", args[0]), p1T[:, half(args[0])])
                elif kind == "ysplit":
                    m_, c = args
                    read(act, ("lnT", 5 if m_ == 1 else 10, c))
                    a_.activation(yhi[:, half(c)], yT[:, half(c)], ACT.Copy).then_inc(y_high, 1)
                elif kind == "split":
                    m_, k = args
                    act.wait_ge(ld_slot[m_][k % SLOTS], 16 * (k // SLOTS + 1))
                    if k >= 2:
                        j = k - 2
                        act.wait_ge(gu_full, nth("GU", m_, j // E, (j % E + 1) * NF[m_] - 1) + 1)
                    a_.activation(whi[m_][:, k % 2, :], wraw[m_][:, k % SLOTS, :], ACT.Copy).then_inc(w_high, 1)
                elif kind == "gate":
                    m_, c = args
                    sl = slice(HT * c, HT * (c + 1))
                    act.wait_ge(gate_arg, nth("gate", m_, c) + 1)
                    o, i = (g8[:, 1, sl], g8[:, 0, sl]) if m_ == 1 else (lg[:, sl, :], lg[:, sl, :])
                    a_.activation(o, i, ACT.Exp).then_inc(gate_exp, 1)
                elif kind == "GU":
                    k = nth(kind, *args)
                    act.wait_ge(gu_full, k + 1)
                    if k >= 2:
                        act.wait_ge(hidden, k - 1)
                    a_.activation(sg[:, k % 2, :], score[2 * (k % 2)][:, :], ACT.Silu).then_inc(silued, 1)
                elif kind == "qk3":
                    G, w, i = args
                    key = ("qk3", G, w, i)
                    full(act, key)
                    for j in range(2):
                        last = a_.activation((qraw, kraw)[w][G][:, i + j, :], bank(key)[:, j * QN:(j + 1) * QN],
                                             ACT.Identity, bias=Bc(("bQ3", "bK3")[w])[:, i + j:i + j + 1])
                    done(last, key)
                elif kind == "v3":
                    G, i = args
                    key = ("v3", G, i, 0)
                    full(act, key)
                    for o, src in value_parts3(key, G, i, 0):
                        last = a_.activation(o, src, ACT.Copy)
                    done(last, key)
                elif kind == "pad":
                    for c in range(2):
                        copy_unit(("pad", c), padB[:, half(c)])
                elif kind == "xq":
                    copy_unit(("xq", args[0]), xqT[:, half(args[0])])
                elif kind == "gu3":
                    t, = args
                    act.wait_ge(quant_arg, t // HT + 1)
                    act.wait_ge(gu3_full, t + 1)
                    if t >= 2:
                        act.wait_ge(hidden3, t - 1)
                    a_.activation(sg3[:, t % 2, :], score[2 * (t % 2)][:, :], ACT.Silu, scale=q8[:, 1, t:t + 1])\
                        .then_inc(silued3, 1)
                elif kind == "scale3":
                    act.wait_ge(scaled3, args[0] + 1)
                    for t in (2 * args[0], 2 * args[0] + 1):
                        a_.activation(hv3[:, t % 4, :], hv3[:, t % 4, :], ACT.Copy, scale=q8[:, 3, t:t + 1], bias=ROUND)\
                            .then_inc(shifted3, 1)
                elif kind == "round3":
                    for t in (2 * args[0], 2 * args[0] + 1):
                        act.wait_ge(rounded3, t + 1)
                        if t >= 2:
                            act.wait_ge(turned3, t - 1)
                        a_.activation(hb[:, t % 2, :], hv3[:, t % 4, :], ACT.Copy, bias=-ROUND).then_inc(quant_t, 1)
                elif kind == "turn3":
                    t, = args
                    act.wait_ge(turned3, t + 1)
                    a_.activation(hqT[:, t % 2, :, :].rearrange("p c q -> p (c q)"),
                                  tbank(("f3", t))[:, 0:256].bitcast(BF16), ACT.Copy).then_inc(copied3, 1)

        @block.gpsimd
        def _(pool):
            p_ = nc.gpsimd
            p_.memset(qbd[:, :, :], 0.0).then_inc(zeroed, 1)
            p_.memset(mhalf[:, :], -0.5).then_inc(half_set, 1)
            pool.wait_ge(half_set, 1)
            for kind, *args in SCHEDULE:
                if kind == "stats":
                    L, c = args
                    sl = slice(HT * c, HT * (c + 1))
                    pool.wait_ge(ln_ve, nth("stats", L, c) + 1)
                    p_.tensor_tensor(rstd[:, sl], ve[:, sl], mhalf[:, :], ALU.pow).then_inc(ln_rstd, 1)
                elif kind == "c0":
                    c, = args
                    p_.memset(vb[:, HB * c:HB * (c + 1), :], 0.0).then_inc(zeroed, 1)
                elif kind == "bias":
                    L, c = args
                    pool.wait_ge(ld_r, 16)
                    if L == 11 and c == 0:
                        read(pool, "bvo")
                    pool.wait_ge(ln_y, HT * (nth("apply", L, c) + 1))
                    xs = x[:, HT * c:HT * (c + 1), :]
                    name = {1: "fcb", 2: "ffb", 11: "bO3", 12: "bo3"}[L]
                    p_.tensor_tensor(xs, xs, spread(row(name), [[0, HT], [1, D]]), ALU.add).then_inc(x_biased, 1)
                elif kind == "soft":
                    if args[1]:
                        g = nth("S", *args[1])
                        pool.wait_ge(row_rcp, g + 1)
                        p3 = pr[:, g % 4, :].rearrange("p (h k) -> p h k", h=8)
                        p_.tensor_tensor(p3, p3, spread(rc[:, g % 4, :], [[1, 8], [0, S]]), ALU.mult).then_inc(normed, 1)
                elif kind == "o2":
                    c, = args
                    freed(pool, ("T", A2, HB * c + HB - 2))
                    freed(pool, ("T", A2, HB * c + HB - 1))
                    p_.tensor_tensor(oT[:, half(c)], oT[:, half(c)], yT[:, half(c)], ALU.add).then_inc(added, 1)
                elif kind == "rotate":
                    G, w, h = args
                    pool.wait_ge(swapped[2 * w + h], 64 * (G + 1))
                    r = swaps[G][:, w, 4 * h:4 * h + 4, :].rearrange("p i (b s) -> p i b s", b=QB)
                    p_.tensor_tensor(r, r, spread(Bc("sin"), [[0, 4], [0, QB], [1, S]]), ALU.mult).then_inc(rot_s, 1)
                elif kind == "split":
                    m_, k = args
                    pool.wait_ge(w_high, nth(kind, m_, k) + 1)
                    p_.tensor_tensor(wlo[m_][:, k % 2, :], wraw[m_][:, k % SLOTS, :],
                                     whi[m_][:, k % 2, :].bitcast(F32), ALU.subtract).then_inc(w_low, 1)
                elif kind == "zero_v":
                    c, part = args
                    if c == 0:
                        pool.wait_ge(valued, nth("val", A3, QB * part + QB - 1) + 1)
                    else:
                        pool.wait_ge(rot, nth("rope", 3, 1, 1) + 1)
                    b0 = HB * c + QB * part
                    p_.memset(vb[:, b0:b0 + QB, :], 0.0).then_inc(vb_clear, 1)

        @block.sync
        def _(sp):
            xv = x_in.rearrange("(t p) d -> p t d", p=P)
            sp.dma_start(x[:, 0:HT, :], xv[:, 0:HT, :]).then_inc(ld_x[0], 16)
            sp.dma_start(sA[:, :], packA).then_inc(ld_a, 16)
            sp.dma_start(x[:, HT:TILES, :], xv[:, HT:TILES, :]).then_inc(ld_x[1], 16)
            sp.dma_start(sH[:, :], packH).then_inc(ld_h, 16)
            sp.dma_start(ctxT[:, :], ctxT_in).then_inc(ld_ctx, 16)
            sp.dma_start(sR[:, :], spread_rows(rows)).then_inc(ld_r, 16)
            sp.dma_start(rel[:, :], relb).then_inc(ld_rel, 16)
            sp.dma_start(sB[:, :], packB).then_inc(ld_b, 16)
            sp.dma_start(pad8[0:3, :], spread_rows(pad_in, 3)).then_inc(ld_pad, 16)
            for kind, *args in SCHEDULE:
                if kind == "load":
                    m_, k = args
                    if m_ == 1 and k == 0:
                        sp.wait_ge(bias_split, 1)
                        sp.wait_ge(tapped, 1)
                        read(sp, "lo3")
                    if k >= SLOTS:
                        j = k - SLOTS
                        sp.wait_ge(downed, nth("DN", m_, j // E, (j % E + 1) * NF[m_] - 1) + 1)
                    n = 3 * NF[m_] * P
                    sp.dma_start(slots[m_][:, k % SLOTS, 0:n], (w1_in if m_ == 1 else w2_in)[:, (k % E) * n:(k % E + 1) * n])\
                        .then_inc(ld_slot[m_][k % SLOTS], 16)
                elif kind == "GU" and args == [2, 0, 0]:
                    sp.wait_ge(downed, nth("DN", 1, 1, E * NF[1] - 1) + 1)
                    sp.dma_start(w3qkv, w3qkv_in).then_inc(ld_w3a, 16)
                    sp.dma_start(w3o, w3o_in).then_inc(ld_w3a, 16)
                    sp.wait_ge(sc_full, nth("S", A2, B - 1) + 1)
                    sp.dma_start(wf3[:, :], wf3_in).then_inc(ld_wf3, 16)
                elif kind == "swap":
                    G, w, h = args
                    read(sp, ("qk3", G, w, 4 * h))
                    read(sp, ("qk3", G, w, 4 * h + 2))
                    if G:
                        sp.wait_ge(rot, nth("rope", G - 1, w, h) + 1)
                    raw, sw = (qraw, kraw)[w][G], swaps[G]
                    for qd in range(4):
                        o, i = 32 * qd, 32 * (qd ^ 1)
                        sp.dma_start(sw[o:o + 32, w, 4 * h:4 * h + 4, :], raw[i:i + 32, 4 * h:4 * h + 4, :])\
                            .then_inc(swapped[2 * w + h], 16)
            for c in range(2):
                for t in range(HT * c, HT * (c + 1)):
                    freed(sp, ("f3", t))
                sp.dma_start(out.rearrange("(t p) d -> p t d", p=P)[:, HT * c:HT * (c + 1), :],
                             x[:, HT * c:HT * (c + 1), :]).then_inc(stored, 16)
            sp.wait_ge(stored, 32)


def spread_rows(ap, n=P):
    return bass.AP(ap.tensor, ap.offset, [[0, n], [1, ap.shape[-1]]])


def kernel(**inputs):
    import ml_dtypes
    import concourse.bacc as _bacc
    from concourse.bass_utils import run_bass_kernel_spmd as _run

    I = {k: np.asarray(v) for k, v in inputs.items()}
    f32 = np.float32

    def pack(cols, parts, dt=f32):
        out = np.zeros((P, sum(n for _, n in cols)), dt)
        o = 0
        for name, n in cols:
            r0, a = parts[name]
            a = a.reshape(a.shape[0], -1)
            out[r0:r0 + a.shape[0], o:o + n] = a
            o += n
        return out

    def col(name):
        return (0, I[name].reshape(D, 1))

    f = np.arange(P)
    hm = ((f[:, None] % 64) // DH == np.arange(HH)[None, :]).astype(f32)
    bf = ml_dtypes.bfloat16
    n1 = bf(NEG)
    n2 = bf(NEG - float(n1))
    n3 = bf(NEG - float(n1) - float(n2))
    padc = np.array([[float(n1)], [float(n2)], [float(n3)]], f32)
    A_ = dict(
        ident=(0, np.eye(P, dtype=f32)), dqkv=(0, np.concatenate([I["L0_attn_W_dq"], I["L0_attn_W_dkv"]], 1)),
        uq=(0, I["L0_attn_W_uq"]), uk=(32, I["L0_attn_W_uk"]), uv=(32, I["L0_attn_W_uv"]), wo0=(0, I["L0_attn_W_o"]),
        wq0=(0, I["L0_xattn_wq"].T), wk0=(0, I["L0_xattn_wk"].T), wv0=(0, I["L0_xattn_wv"].T), fc0=(0, I["L0_xattn_fc_w"].T),
        ffW=(0, I["L0_ffn_W"].T), lordT=(0, I["L0_ffn_lora_down"].T), dauxT=(0, I["L0_ffn_down_aux"]),
        loruT=(0, I["L0_ffn_lora_up"].T), uauxT=(0, I["L0_ffn_up_aux"].T),
        hm=(0, hm), iota=(0, np.tile(np.arange(E, dtype=f32), (P, 1))),
        padc=(0, padc), mean=(0, np.full((P, P), 1.0 / (D * F3), f32)))
    pos = np.arange(S, dtype=f32)
    dim = np.arange(HD3 // 2, dtype=f32)
    freq = (f32(10000.0) ** (dim / f32(HD3 // 2))).astype(f32)
    ang = (pos[None, :] / np.concatenate([freq, freq])[:, None]).astype(f32)
    sign = np.where(np.arange(HD3) < HD3 // 2, -1.0, 1.0).astype(f32)[:, None]
    by_output = lambda w: w.reshape(4, 2, 2, HD3, -1).transpose(1, 3, 0, 2, 4)
    heads = lambda n: (0, I[n].reshape(8, P).T)
    B_ = dict(
        delta=(0, I["L1_attn_delta"]), alpha=(0, I["L1_attn_alpha"]), beta=(0, I["L1_attn_beta"]),
        gamma=(0, I["L1_attn_gamma"]), omega=col("L1_attn_omega"),
        wq1=(0, I["L1_xattn_Wq"].T), wk1=(0, I["L1_xattn_Wk"].T), wv1=(0, I["L1_xattn_Wv"].T),
        bq1=col("L1_xattn_bq"), bk1=col("L1_xattn_bk"), wg1=(0, I["L1_ffn_Wg"].T),
        blk=(0, (f[:, None] // S == f[None, :] // S).astype(f32)),
        wqa2=(0, I["L2_attn_wq"]), wka2=(0, I["L2_attn_wk"]), wva2=(0, I["L2_attn_wv"]),
        lns2=col("L2_attn_ln_scale"), lnb2=col("L2_attn_ln_bias"),
        wq2=(0, I["L2_xattn_Wq"].T), wk2=(0, I["L2_xattn_Wk"].T), wv2=(0, I["L2_xattn_Wv"].T),
        bq2=col("L2_xattn_bq"), bk2=col("L2_xattn_bk"), gam2=col("L2_ffn_ln_gamma"), bet2=col("L2_ffn_ln_beta"),
        wr2=(0, I["L2_ffn_Wr"].T),
        wq3=(0, I["L3_xattn_Wq"].T), wk3=(0, I["L3_xattn_Wk"].T), wv3=(0, I["L3_xattn_Wv"].T), wo3=(0, I["L3_xattn_Wo"].T),
        bQ3=heads("L3_attn_b_Q"), bK3=heads("L3_attn_b_K"), bV3=(0, by_output(I["L3_attn_b_V"]).reshape(P, 8)),
        cos=(0, np.tile(np.cos(ang), (2, 1)).astype(f32)), sin=(0, np.tile(np.sin(ang) * sign, (2, 1)).astype(f32)),
        lgrid=(0, np.tile(np.arange(16, dtype=f32), (P, 1))))
    q, k = f[:, None] % S, np.arange(S)[None, :]
    H_ = dict(
        identb=(0, np.eye(P, dtype=bf)), causal=(0, np.where(k <= q, 0.0, -BIG).astype(bf)),
        offblk=(0, np.where(f[:, None] // S == f[None, :] // S, 0.0, -BIG).astype(bf)),
        before=(0, (f[:, None] < f[None, :]).astype(bf)), ones=(0, np.ones((P, P), bf)))
    table = I["L0_xattn_rel_table"]
    relq = np.stack([table[255 - i:255 - i + S] for i in range(S)])
    relq = relq.transpose(0, 2, 1).reshape(S, 2, HH * S).transpose(1, 0, 2).reshape(P, HH * S)
    rows = np.concatenate([I[n].reshape(1, -1) for n in (
        "L0_xattn_fc_b", "L0_ffn_b", "L1_xattn_bv", "L2_xattn_bv", "L3_attn_b_O", "L3_xattn_bo")], 1)

    def inner(w):
        return w.transpose(2, 0, 1)

    def outer(w):
        e, d, n = w.shape
        return w.transpose(2, 0, 1).reshape(n // P, P, e, d).transpose(1, 2, 0, 3)

    def per_expert(gate_up, down):
        return np.concatenate([gate_up, down.reshape(P, E, -1)], 2).reshape(P, -1)

    feeds = dict(
        x=I["x"].reshape(T, D), ctxT=I["ctx_1024"].reshape(T, D).T, pad=I["mask_BxS2_bf1"].reshape(1, T).view(np.uint8),
        packA=pack(COLS_A, A_), packB=pack(COLS_B, B_), packH=pack(COLS_H, H_, bf), rows=rows, relb=relq,
        w1=per_expert(np.concatenate([inner(I["L1_ffn_W1"]), inner(I["L1_ffn_W2"])], 2), outer(I["L1_ffn_W3"])),
        w2=per_expert(inner(I["L2_ffn_W12"]), outer(I["L2_ffn_W3"])),
        w3qkv=np.stack([I[f"L3_attn_W_{n}"].transpose(1, 0, 2).reshape(D, 1024) for n in "QKV"], 1),
        w3o=by_output(I["L3_attn_W_O"]).reshape(P, 8, D),
        wf3=np.concatenate([I["L3_ffn_w_gate"].T, I["L3_ffn_w_up"].T,
                            I["L3_ffn_w_down"].T.reshape(4, P, D).transpose(1, 0, 2).reshape(P, F3)], 1))
    nc = _bacc.Bacc("TRN2", target_bir_lowering=False, num_devices=1)
    arrays, args = {}, []
    for name, a in feeds.items():
        a = np.ascontiguousarray(a)
        arrays[f"in_{name}"] = a
        args.append(nc.dram_tensor(f"in_{name}", a.shape, mybir.dt.from_np(a.dtype), kind="ExternalInput").ap())
    out = nc.dram_tensor("out_x", (T, D), F32, kind="ExternalOutput").ap()
    bass_decoder_kernel(nc, *args, out)
    r = _run(nc, [arrays], core_ids=[0])
    return r.results[0]["out_x"].reshape(B, S, D)
```
